# Optimizing a Trainium2 kernel written in Bass

```python
import numpy as np
import jax
import jax.numpy as jnp

def _softmax(x, axis=-1):
    return jax.nn.softmax(x, axis=axis)

def _gelu(x):
    return jax.nn.gelu(x, approximate=True)

def _silu(x):
    return jax.nn.silu(x)

def _sigmoid(x):
    return jax.nn.sigmoid(x)

def _layernorm(x, axis=-1, eps=1e-05):
    m = jnp.mean(x, axis=axis, keepdims=True)
    v = jnp.var(x, axis=axis, keepdims=True)
    return (x - m) / jnp.sqrt(v + eps)

def _scatter_add(tgt, idx, src, axis=0):
    return tgt.at[idx].add(src)

def _segment_sum(src, seg, n):
    return jax.ops.segment_sum(src, seg, n)
kernel_name = 'mk_decoder_preln_d2_seqx_r4_394c35'

def setup_inputs(seed: int=0):
    np.random.seed(seed)
    _w = jnp.asarray

    def _rec_inputs():
        import jax
        import jax.numpy as jnp
        _rk = jax.random.key(seed)
        x = -0.0002928 + 1 * jax.random.normal(jax.random.fold_in(_rk, 1), (1, 2048, 256), jnp.float32)
        _lenS = 2048 - jax.random.randint(jax.random.fold_in(_rk, 7), (1,), 0, max(1, 2048 // 4) + 1, jnp.int32)
        _lenS2 = 1601 - jax.random.randint(jax.random.fold_in(_rk, 8), (1,), 0, max(1, 1601 // 4) + 1, jnp.int32)
        _ctx_1024P = jax.random.normal(jax.random.fold_in(_rk, 11), (1, 16, 256), jnp.float32)
        _ctx_1024c = jax.random.dirichlet(jax.random.fold_in(_rk, 511), 0.3 * jnp.ones((16,), jnp.float32), (1, 1601))
        _ctx_1024t = jnp.einsum('bsk,bkd->bsd', _ctx_1024c, _ctx_1024P)
        _ctx_1024t = _ctx_1024t * jax.lax.rsqrt(jnp.mean(jnp.square(_ctx_1024t)) + 1e-12) * 0.953939
        ctx_1024 = -1.39393e-06 + 0.999914 * (_ctx_1024t + 0.3 * jax.random.normal(jax.random.fold_in(_rk, 611), (1, 1601, 256), jnp.float32))
        return (x, ctx_1024)
    x, ctx_1024 = _rec_inputs()

    def _L0_attn_setup():
        import jax, jax.numpy as jnp
        import numpy as np
        BITS = 8
        NUM_HEADS = 16
        EPS = 0.01

        def _max_scale_rp(x, axis):
            m = jnp.maximum(jnp.max(jnp.abs(x), axis=axis), EPS)
            return jnp.exp2(jnp.ceil(jnp.log2(m)))

        def _dmd_dequant(x):
            half = float(1 << BITS - 1)
            s1 = _max_scale_rp(x, -2)
            x = x / s1[..., None, :]
            s2 = _max_scale_rp(x, -1)
            x = x / s2[..., None]
            q = jnp.clip(jnp.round(x * half), -half, half - 1.0)
            return s1[..., None, :] * q * (s2 / half)[..., None]

        def qmatmul(x, y):
            return jnp.matmul(_dmd_dequant(x), _dmd_dequant(y))
        key = jax.random.key(seed)
        k1, k2, k3 = jax.random.split(key, 3)
        B, S, E = (4, 256, 256)
        hidden_states = jax.random.normal(k1, (B, S, E), dtype=jnp.float32)
        w_attn = jax.random.normal(k2, (E, 3 * E), dtype=jnp.float32) * 0.02
        b_attn = jnp.zeros((3 * E,), dtype=jnp.float32)
        w_proj = jax.random.normal(k3, (E, E), dtype=jnp.float32) * 0.02
        b_proj = jnp.zeros((E,), dtype=jnp.float32)
        return {'hidden_states': hidden_states, 'w_attn': w_attn, 'b_attn': b_attn, 'w_proj': w_proj, 'b_proj': b_proj}
    _L0_attn_all = _L0_attn_setup()
    _L0_attn_in = {k: v for k, v in _L0_attn_all.items() if k in ('w_attn', 'b_attn', 'w_proj', 'b_proj')}
    del _L0_attn_all

    def _L0_xattn_setup():
        import jax, jax.numpy as jnp
        import numpy as np
        D_MODEL = 256
        H = 16
        D_H = D_MODEL // H
        key = jax.random.key(seed)
        ks = jax.random.split(key, 10)
        B, T_dec, T_enc = (2, 512, 512)
        s = 1.0 / np.sqrt(D_MODEL)
        return {'tgt': jax.random.normal(ks[0], (B, T_dec, D_MODEL), jnp.float32), 'memory': jax.random.normal(ks[1], (B, T_enc, D_MODEL), jnp.float32), 'W_q': jax.random.normal(ks[2], (D_MODEL, D_MODEL), jnp.float32) * s, 'b_q': jnp.zeros((D_MODEL,), jnp.float32), 'W_k': jax.random.normal(ks[3], (D_MODEL, D_MODEL), jnp.float32) * s, 'b_k': jnp.zeros((D_MODEL,), jnp.float32), 'W_v': jax.random.normal(ks[4], (D_MODEL, D_MODEL), jnp.float32) * s, 'b_v': jnp.zeros((D_MODEL,), jnp.float32), 'W_o': jax.random.normal(ks[5], (D_MODEL, D_MODEL), jnp.float32) * s, 'b_o': jnp.zeros((D_MODEL,), jnp.float32)}
    _L0_xattn_all = _L0_xattn_setup()
    _L0_xattn_in = {k: v for k, v in _L0_xattn_all.items() if k in ('W_q', 'b_q', 'W_k', 'b_k', 'W_v', 'b_v', 'W_o', 'b_o')}
    del _L0_xattn_all

    def _L0_ffn_setup():
        import jax, jax.numpy as jnp
        import numpy as np
        D = 256
        H = 1024
        E = 8
        TOPK = 2
        CAP_F = 1.25
        key = jax.random.key(seed)
        ks = jax.random.split(key, 6)
        sc = 0.02
        return {'x': jax.random.normal(ks[0], (4, 512, D), jnp.float32), 'Wg': jax.random.normal(ks[1], (D, E), jnp.float32) * sc, 'bg': jnp.zeros((E,), jnp.float32), 'W1': jax.random.normal(ks[2], (E, D, H), jnp.float32) * sc, 'W2': jax.random.normal(ks[3], (E, D, H), jnp.float32) * sc, 'W3': jax.random.normal(ks[4], (E, H, D), jnp.float32) * sc}
    _L0_ffn_all = _L0_ffn_setup()
    _L0_ffn_in = {k: v for k, v in _L0_ffn_all.items() if k in ('Wg', 'bg', 'W1', 'W2', 'W3')}
    del _L0_ffn_all

    def _L1_attn_setup():
        import jax, jax.numpy as jnp
        import numpy as np
        import math
        B, S, E, H = (2, 512, 256, 16)
        D = E // H
        WINDOW = 128
        EPS = 1e-05

        def _layernorm(x, gamma, beta):
            mu = jnp.mean(x, axis=-1, keepdims=True)
            var = jnp.var(x, axis=-1, keepdims=True)
            return (x - mu) * jax.lax.rsqrt(var + EPS) * gamma + beta
        key = jax.random.key(seed)
        ks = jax.random.split(key, 5)
        return {'x': jax.random.normal(ks[0], (B, S, E), jnp.float32), 'W_qkv': jax.random.normal(ks[1], (E, 3 * E), jnp.float32) * E ** (-0.5), 'b_qkv': jax.random.normal(ks[2], (3 * E,), jnp.float32) * 0.02, 'q_gamma': jnp.ones((D,), jnp.float32), 'q_beta': jnp.zeros((D,), jnp.float32), 'k_gamma': jnp.ones((D,), jnp.float32), 'k_beta': jnp.zeros((D,), jnp.float32), 'W_out': jax.random.normal(ks[3], (E, E), jnp.float32) * E ** (-0.5), 'b_out': jax.random.normal(ks[4], (E,), jnp.float32) * 0.02}
    _L1_attn_all = _L1_attn_setup()
    _L1_attn_in = {k: v for k, v in _L1_attn_all.items() if k in ('W_qkv', 'b_qkv', 'q_gamma', 'q_beta', 'k_gamma', 'k_beta', 'W_out', 'b_out')}
    del _L1_attn_all

    def _L1_xattn_setup():
        import jax, jax.numpy as jnp
        import numpy as np
        D_MODEL = 256
        NUM_HEADS = 16
        HEAD_DIM = D_MODEL // NUM_HEADS
        key = jax.random.key(seed)
        ks = jax.random.split(key, 10)
        B, SQ, SKV = (4, 512, 512)
        s = 1.0 / np.sqrt(D_MODEL)
        return {'query': jax.random.normal(ks[0], (B, SQ, D_MODEL), jnp.float32), 'key_value': jax.random.normal(ks[1], (B, SKV, D_MODEL), jnp.float32), 'Wq': jax.random.normal(ks[2], (D_MODEL, D_MODEL), jnp.float32) * s, 'bq': jnp.zeros((D_MODEL,), jnp.float32), 'Wk': jax.random.normal(ks[3], (D_MODEL, D_MODEL), jnp.float32) * s, 'bk': jnp.zeros((D_MODEL,), jnp.float32), 'Wv': jax.random.normal(ks[4], (D_MODEL, D_MODEL), jnp.float32) * s, 'bv': jnp.zeros((D_MODEL,), jnp.float32), 'Wo': jax.random.normal(ks[5], (D_MODEL, D_MODEL), jnp.float32) * s, 'bo': jnp.zeros((D_MODEL,), jnp.float32)}
    _L1_xattn_all = _L1_xattn_setup()
    _L1_xattn_in = {k: v for k, v in _L1_xattn_all.items() if k in ('Wq', 'bq', 'Wk', 'bk', 'Wv', 'bv', 'Wo', 'bo')}
    del _L1_xattn_all

    def _L1_ffn_setup():
        import jax, jax.numpy as jnp
        import numpy as np
        T, Z, D_DIM = (8, 512, 256)
        N_EXP, P_SLOT, H = (64, 32, 256)
        LN_EPS = 1e-05
        key = jax.random.key(seed)
        k = jax.random.split(key, 5)
        s = 0.02
        return {'x': jax.random.normal(k[0], (T, Z, D_DIM), dtype=jnp.float32), 'phi_w': jax.random.normal(k[1], (N_EXP * P_SLOT, D_DIM), dtype=jnp.float32) * s, 'phi_b': jax.random.normal(k[2], (N_EXP * P_SLOT,), dtype=jnp.float32) * s, 'expert_w': jax.random.normal(k[3], (N_EXP, D_DIM, H), dtype=jnp.float32) * s, 'expert_b': jax.random.normal(k[4], (N_EXP, H), dtype=jnp.float32) * s}
    _L1_ffn_all = _L1_ffn_setup()
    _L1_ffn_in = {k: v for k, v in _L1_ffn_all.items() if k in ('phi_w', 'phi_b', 'expert_w', 'expert_b')}
    del _L1_ffn_all
    return {'x': x, 'ctx_1024': ctx_1024, 'L0_attn_w_attn': _L0_attn_in['w_attn'], 'L0_attn_b_attn': _L0_attn_in['b_attn'], 'L0_attn_w_proj': _L0_attn_in['w_proj'], 'L0_attn_b_proj': _L0_attn_in['b_proj'], 'L0_xattn_W_q': _L0_xattn_in['W_q'], 'L0_xattn_b_q': _L0_xattn_in['b_q'], 'L0_xattn_W_k': _L0_xattn_in['W_k'], 'L0_xattn_b_k': _L0_xattn_in['b_k'], 'L0_xattn_W_v': _L0_xattn_in['W_v'], 'L0_xattn_b_v': _L0_xattn_in['b_v'], 'L0_xattn_W_o': _L0_xattn_in['W_o'], 'L0_xattn_b_o': _L0_xattn_in['b_o'], 'L0_ffn_Wg': _L0_ffn_in['Wg'], 'L0_ffn_bg': _L0_ffn_in['bg'], 'L0_ffn_W1': _L0_ffn_in['W1'], 'L0_ffn_W2': _L0_ffn_in['W2'], 'L0_ffn_W3': _L0_ffn_in['W3'], 'L1_attn_W_qkv': _L1_attn_in['W_qkv'], 'L1_attn_b_qkv': _L1_attn_in['b_qkv'], 'L1_attn_q_gamma': _L1_attn_in['q_gamma'], 'L1_attn_q_beta': _L1_attn_in['q_beta'], 'L1_attn_k_gamma': _L1_attn_in['k_gamma'], 'L1_attn_k_beta': _L1_attn_in['k_beta'], 'L1_attn_W_out': _L1_attn_in['W_out'], 'L1_attn_b_out': _L1_attn_in['b_out'], 'L1_xattn_Wq': _L1_xattn_in['Wq'], 'L1_xattn_bq': _L1_xattn_in['bq'], 'L1_xattn_Wk': _L1_xattn_in['Wk'], 'L1_xattn_bk': _L1_xattn_in['bk'], 'L1_xattn_Wv': _L1_xattn_in['Wv'], 'L1_xattn_bv': _L1_xattn_in['bv'], 'L1_xattn_Wo': _L1_xattn_in['Wo'], 'L1_xattn_bo': _L1_xattn_in['bo'], 'L1_ffn_phi_w': _L1_ffn_in['phi_w'], 'L1_ffn_phi_b': _L1_ffn_in['phi_b'], 'L1_ffn_expert_w': _L1_ffn_in['expert_w'], 'L1_ffn_expert_b': _L1_ffn_in['expert_b']}

def reference(x, ctx_1024, L0_attn_w_attn, L0_attn_b_attn, L0_attn_w_proj, L0_attn_b_proj, L0_xattn_W_q, L0_xattn_b_q, L0_xattn_W_k, L0_xattn_b_k, L0_xattn_W_v, L0_xattn_b_v, L0_xattn_W_o, L0_xattn_b_o, L0_ffn_Wg, L0_ffn_bg, L0_ffn_W1, L0_ffn_W2, L0_ffn_W3, L1_attn_W_qkv, L1_attn_b_qkv, L1_attn_q_gamma, L1_attn_q_beta, L1_attn_k_gamma, L1_attn_k_beta, L1_attn_W_out, L1_attn_b_out, L1_xattn_Wq, L1_xattn_bq, L1_xattn_Wk, L1_xattn_bk, L1_xattn_Wv, L1_xattn_bv, L1_xattn_Wo, L1_xattn_bo, L1_ffn_phi_w, L1_ffn_phi_b, L1_ffn_expert_w, L1_ffn_expert_b):
    import jax
    import jax.numpy as jnp

    def _L0_attn_ref(hidden_states, w_attn, b_attn, w_proj, b_proj):
        import jax, jax.numpy as jnp
        import numpy as np
        BITS = 8
        NUM_HEADS = 16
        EPS = 0.01

        def _max_scale_rp(x, axis):
            m = jnp.maximum(jnp.max(jnp.abs(x), axis=axis), EPS)
            return jnp.exp2(jnp.ceil(jnp.log2(m)))

        def _dmd_dequant(x):
            half = float(1 << BITS - 1)
            s1 = _max_scale_rp(x, -2)
            x = x / s1[..., None, :]
            s2 = _max_scale_rp(x, -1)
            x = x / s2[..., None]
            q = jnp.clip(jnp.round(x * half), -half, half - 1.0)
            return s1[..., None, :] * q * (s2 / half)[..., None]

        def qmatmul(x, y):
            return jnp.matmul(_dmd_dequant(x), _dmd_dequant(y))
        B, S, E = hidden_states.shape
        H = NUM_HEADS
        D = E // H
        qkv = qmatmul(hidden_states.reshape(-1, E), w_attn) + b_attn
        qkv = qkv.reshape(B, S, 3 * E)
        q, k, v = jnp.split(qkv, 3, axis=-1)
        split_heads = lambda t: t.reshape(B, S, H, D).transpose(0, 2, 1, 3)
        q, k, v = (split_heads(q), split_heads(k), split_heads(v))
        aw = qmatmul(q, jnp.swapaxes(k, -1, -2)) / jnp.asarray(D ** 0.5, jnp.float32)
        causal = jnp.tril(jnp.ones((S, S), dtype=bool))
        aw = jnp.where(causal, aw, jnp.finfo(aw.dtype).min)
        aw = jax.nn.softmax(aw, axis=-1)
        out = qmatmul(aw, v)
        out = out.transpose(0, 2, 1, 3).reshape(B, S, E)
        out = qmatmul(out.reshape(-1, E), w_proj) + b_proj
        return out.reshape(B, S, E)

    def _L0_xattn_ref(tgt, memory, W_q, b_q, W_k, b_k, W_v, b_v, W_o, b_o):
        import jax, jax.numpy as jnp
        import numpy as np
        D_MODEL = 256
        H = 16
        D_H = D_MODEL // H
        B, T_dec, _ = tgt.shape
        T_enc = memory.shape[1]
        Q = tgt @ W_q + b_q
        K = memory @ W_k + b_k
        V = memory @ W_v + b_v
        Q = Q.reshape(B, T_dec, H, D_H).transpose(0, 2, 1, 3)
        K = K.reshape(B, T_enc, H, D_H).transpose(0, 2, 1, 3)
        V = V.reshape(B, T_enc, H, D_H).transpose(0, 2, 1, 3)
        S = jnp.einsum('bhqd,bhkd->bhqk', Q, K) / jnp.sqrt(jnp.float32(D_H)).astype(Q.dtype)
        A = jax.nn.softmax(S, axis=-1)
        Y = jnp.einsum('bhqk,bhkd->bhqd', A, V)
        Y = Y.transpose(0, 2, 1, 3).reshape(B, T_dec, D_MODEL)
        return Y @ W_o + b_o

    def _L0_ffn_ref(x, Wg, bg, W1, W2, W3):
        import jax, jax.numpy as jnp
        import numpy as np
        D = 256
        H = 1024
        E = 8
        TOPK = 2
        CAP_F = 1.25
        b, s, d = x.shape
        xt = x.reshape(-1, d)
        T = xt.shape[0]
        capacity = int(T / E * CAP_F)
        gate_logits = xt @ Wg + bg
        top_v, top_i = jax.lax.top_k(gate_logits, TOPK)
        expert_label = jax.nn.one_hot(top_i, E, dtype=xt.dtype).sum(axis=1)
        seq = jnp.cumsum(expert_label, axis=0) * expert_label
        valid = (seq > 0) & (seq <= capacity)
        slot = (seq - 1.0).astype(jnp.int32)
        flat_idx = jnp.where(valid, jnp.arange(E, dtype=jnp.int32)[None, :] * capacity + slot, E * capacity)
        src = jnp.broadcast_to(xt[:, None, :], (T, E, d)).reshape(-1, d)
        buf = jnp.zeros((E * capacity + 1, d), xt.dtype).at[flat_idx.reshape(-1)].set(src)
        disp = buf[:-1].reshape(E, capacity, d)
        h = jax.nn.silu(jnp.einsum('ecd,edh->ech', disp, W1)) * jnp.einsum('ecd,edh->ech', disp, W2)
        out = jnp.einsum('ech,ehd->ecd', h, W3)
        out_flat = jnp.concatenate([out.reshape(E * capacity, d), jnp.zeros((1, d), xt.dtype)], axis=0)
        all_expert_output = out_flat[flat_idx]
        sel = jnp.take_along_axis(all_expert_output, top_i[:, :, None], axis=1)
        routing_w = jax.nn.softmax(top_v, axis=-1)
        y = (routing_w[:, :, None] * sel).sum(axis=1)
        return y.reshape(b, s, d)

    def _L1_attn_ref(x, W_qkv, b_qkv, q_gamma, q_beta, k_gamma, k_beta, W_out, b_out):
        import jax, jax.numpy as jnp
        import numpy as np
        import math
        B, S, E, H = (2, 512, 256, 16)
        D = E // H
        WINDOW = 128
        EPS = 1e-05

        def _layernorm(x, gamma, beta):
            mu = jnp.mean(x, axis=-1, keepdims=True)
            var = jnp.var(x, axis=-1, keepdims=True)
            return (x - mu) * jax.lax.rsqrt(var + EPS) * gamma + beta
        b, s, e = x.shape
        qkv = (x @ W_qkv + b_qkv).reshape(b, s, 3, H, D).transpose(2, 0, 3, 1, 4)
        q, k, v = (qkv[0], qkv[1], qkv[2])
        q = _layernorm(q, q_gamma, q_beta)
        k = _layernorm(k, k_gamma, k_beta)
        scores = jnp.einsum('bhqd,bhkd->bhqk', q, k) / math.sqrt(D)
        row = jnp.arange(s)[:, None]
        col = jnp.arange(s)[None, :]
        masked = (col > row) | (row - col >= WINDOW)
        scores = jnp.where(masked[None, None], -jnp.inf, scores)
        attn = jax.nn.softmax(scores, axis=-1)
        out = jnp.einsum('bhqk,bhkd->bhqd', attn, v)
        out = out.transpose(0, 2, 1, 3).reshape(b, s, e)
        return out @ W_out + b_out

    def _L1_xattn_ref(query, key_value, Wq, bq, Wk, bk, Wv, bv, Wo, bo):
        import jax, jax.numpy as jnp
        import numpy as np
        D_MODEL = 256
        NUM_HEADS = 16
        HEAD_DIM = D_MODEL // NUM_HEADS
        B, SQ, _ = query.shape
        SKV = key_value.shape[1]
        H, Dh = (NUM_HEADS, HEAD_DIM)
        Q = (query @ Wq.T + bq).reshape(B, SQ, H, Dh).transpose(0, 2, 1, 3)
        K = (key_value @ Wk.T + bk).reshape(B, SKV, H, Dh).transpose(0, 2, 1, 3)
        V = (key_value @ Wv.T + bv).reshape(B, SKV, H, Dh).transpose(0, 2, 1, 3)
        scale = jnp.asarray(np.sqrt(Dh), query.dtype)
        scores = jnp.einsum('bhqd,bhkd->bhqk', Q, K) / scale
        weights = jax.nn.softmax(scores, axis=-1)
        attn = jnp.einsum('bhqk,bhkd->bhqd', weights, V)
        attn = attn.transpose(0, 2, 1, 3).reshape(B, SQ, H * Dh)
        return attn @ Wo.T + bo

    def _L1_ffn_ref(x, phi_w, phi_b, expert_w, expert_b):
        import jax, jax.numpy as jnp
        import numpy as np
        T, Z, D_DIM = (8, 512, 256)
        N_EXP, P_SLOT, H = (64, 32, 256)
        LN_EPS = 1e-05
        t, z, d = x.shape
        n = expert_w.shape[0]
        p = phi_w.shape[0] // n
        logits = (jnp.einsum('tzd,ed->tze', x, phi_w) + phi_b).reshape(t, z, n, p)
        D = jax.nn.softmax(logits, axis=3)
        C = jax.nn.softmax(logits, axis=2)
        X_tilde = jnp.einsum('tznp,tzd->npd', D, x)
        X_tilde = jnp.clip(X_tilde, -33000.0, 65000.0)
        mu = jnp.mean(X_tilde, axis=-1, keepdims=True)
        var = jnp.mean(jnp.square(X_tilde - mu), axis=-1, keepdims=True)
        X_tilde = (X_tilde - mu) * jax.lax.rsqrt(var + LN_EPS)
        X_tilde = jnp.tanh(X_tilde)
        Y_tilde = jnp.einsum('npd,ndH->npH', X_tilde, expert_w) + expert_b[:, None, :]
        Y = jnp.einsum('tznp,npH->tzH', C, Y_tilde)
        return Y
    x = x + _L0_attn_ref(_layernorm(x, axis=-1), L0_attn_w_attn, L0_attn_b_attn, L0_attn_w_proj, L0_attn_b_proj)
    x = x + _L0_xattn_ref(_layernorm(x, axis=-1), ctx_1024, L0_xattn_W_q, L0_xattn_b_q, L0_xattn_W_k, L0_xattn_b_k, L0_xattn_W_v, L0_xattn_b_v, L0_xattn_W_o, L0_xattn_b_o)
    x = x + _L0_ffn_ref(_layernorm(x, axis=-1), L0_ffn_Wg, L0_ffn_bg, L0_ffn_W1, L0_ffn_W2, L0_ffn_W3)
    x = x + _L1_attn_ref(_layernorm(x, axis=-1), L1_attn_W_qkv, L1_attn_b_qkv, L1_attn_q_gamma, L1_attn_q_beta, L1_attn_k_gamma, L1_attn_k_beta, L1_attn_W_out, L1_attn_b_out)
    x = x + _L1_xattn_ref(_layernorm(x, axis=-1), ctx_1024, L1_xattn_Wq, L1_xattn_bq, L1_xattn_Wk, L1_xattn_bk, L1_xattn_Wv, L1_xattn_bv, L1_xattn_Wo, L1_xattn_bo)
    x = x + _L1_ffn_ref(_layernorm(x, axis=-1), L1_ffn_phi_w, L1_ffn_phi_b, L1_ffn_expert_w, L1_ffn_expert_b)
    return x

_drawn_inputs = setup_inputs


def setup_inputs(seed=0):
    import zlib

    import numpy as np

    out = dict(_drawn_inputs(seed))
    spreads = {'L0_attn_b_attn': (0.0, 0.1),
     'L0_attn_b_proj': (0.0, 0.1),
     'L0_xattn_b_q': (0.0, 0.394),
     'L0_xattn_b_k': (0.0, 2.0),
     'L0_xattn_b_v': (0.0, 0.1),
     'L0_xattn_b_o': (0.0, 0.1),
     'L0_ffn_bg': (0.0, 0.8),
     'L1_attn_q_gamma': (1.0, 0.6),
     'L1_attn_q_beta': (0.0, 2.0),
     'L1_attn_k_gamma': (1.0, 0.6),
     'L1_attn_k_beta': (0.0, 2.0),
     'L1_xattn_bq': (0.0, 0.405),
     'L1_xattn_bk': (0.0, 2.0),
     'L1_xattn_bv': (0.0, 0.1),
     'L1_xattn_bo': (0.0, 0.1)}
    factors = {'L0_attn_w_attn': 8.0,
     'L0_ffn_Wg': 5.609,
     'L0_ffn_W1': 5.215,
     'L0_ffn_W2': 5.132,
     'L0_ffn_W3': 5.167,
     'L1_attn_b_out': 3.057,
     'L1_ffn_phi_b': 64.0,
     'L1_attn_b_qkv': 5.281,
     'L1_ffn_phi_w': 3.716}
    for name, (base, spread) in spreads.items():
        noise = np.random.default_rng([zlib.crc32(name.encode()), seed]).standard_normal(out[name].shape)
        drawn = base * np.exp(spread * noise) if base else spread * noise
        out[name] = jnp.asarray(drawn.astype(out[name].dtype))
    for name, factor in factors.items():
        out[name] = (out[name] * factor).astype(out[name].dtype)
    return out
```

```python
from contextlib import ExitStack

import concourse.bass as bass
from concourse import mybir

F32, BF16, I32, U32, U8 = (mybir.dt.float32, mybir.dt.bfloat16, mybir.dt.int32, mybir.dt.uint32,
                           mybir.dt.uint8)
ALU = mybir.AluOpType
ACT = mybir.ActivationFunctionType
X = mybir.AxisListType.X

P = 128
N = 2048
T = N // P
D = 256
DT = D // P
H = 16
HD = D // H
HALF_HEADS = P // HD
BANK = 512
CH = N // BANK
WIDE = 2 * BANK
NWIDE = N // WIDE
M = 1601
MT = (M + P - 1) // P
MPAD = MT * P
PARTS = 3
PAIRS = 6
SR = PAIRS * HD
SRM = SR + PARTS
BIG = -1.0e30
MAGIC = 12582912.0
TINY_SCALE = 0.01
HALF = 128.0


class Line:

    def __init__(self, eng, sem):
        self.eng, self.sem, self.n = eng, sem, 0

    def __call__(self, ins):
        self.n += 1
        ins.then_inc(self.sem, 1)
        self.eng.wait_ge(self.sem, self.n)


def wait(eng, sem, value):
    if not isinstance(value, int) or value > 0:
        eng.wait_ge(sem, value)


class Core:

    def __init__(self, nc, ctx):
        self.nc, self.ctx, self.n, self.sems = nc, ctx, 0, []

    def sb(self, ctx, name, shape, dt=F32):
        return ctx.enter_context(self.nc.sbuf_tensor(self.unique(name), shape, dt))

    def ps(self, ctx, name, shape, dt=F32):
        return ctx.enter_context(self.nc.psum_tensor(self.unique(name), shape, dt))

    def sem(self, name):
        self.sems.append(self.nc.alloc_semaphore(self.unique(name)))
        return self.sems[-1]

    def recycle(self):
        self.nc.clear_and_free_semaphores(self.sems)
        self.nc.all_engine_barrier()
        self.sems = []

    def dram(self, name, shape, dt=F32):
        return self.nc.dram_tensor(name, shape, dt, kind="Internal").ap()

    def unique(self, name):
        self.n += 1
        return f"{name}_{self.n}"


def setup(c, x_in):
    nc = c.nc
    c.x = c.sb(c.ctx, "x", [P, T, D])
    c.identf = c.sb(c.ctx, "identf", [P, P])
    c.identb = c.sb(c.ctx, "identb", [P, P], BF16)
    c.onesf = c.sb(c.ctx, "onesf", [P, P])
    c.onesb = c.sb(c.ctx, "onesb", [P, P], BF16)
    c.triu = c.sb(c.ctx, "triu", [P, P], BF16)
    c.mask_qk = c.sb(c.ctx, "mask_qk", [P, 2 * P], BF16)
    c.mask_kq = c.sb(c.ctx, "mask_kq", [P, 2 * P], BF16)
    c.mask_first = c.sb(c.ctx, "mask_first", [P, 2 * P], BF16)
    c.eps = c.sb(c.ctx, "eps", [P, 1])
    c.ones_wide = c.sb(c.ctx, "ones_wide", [8 * PARTS, 2 * N], BF16)
    x_loaded, made, filled = c.sem("x_loaded"), c.sem("made"), c.sem("filled")
    with nc.Block() as block:
        @block.sync
        def _(sp):
            sp.dma_start(c.x[:], x_in.rearrange("b (t p) d -> p (b t) d", p=P)).then_inc(x_loaded, 16)
            sp.wait_ge(x_loaded, 16)

        @block.gpsimd
        def _(pool):
            for buf, v in ((c.identf, 0.0), (c.identb, 0.0), (c.onesf, 1.0), (c.onesb, 1.0),
                           (c.triu, 1.0), (c.mask_qk, 0.0), (c.mask_kq, 0.0), (c.eps, 1e-5), (c.ones_wide, 1.0),
                           (c.mask_first[:, 0:P], BIG), (c.mask_first[:, P:2 * P], 0.0)):
                pool.memset(buf if isinstance(buf, bass.AP) else buf[:], v).then_inc(filled, 1)
            pool.wait_ge(filled, 11)

            def keep(ap, op, fill, row, col):
                pool.affine_select(out=ap, in_=ap, compare_op=op, fill=fill, base=0,
                                   pattern=[[col, P]], channel_multiplier=row).then_inc(made, 1)

            keep(c.identf[:], ALU.not_equal, 1.0, 1, -1)
            keep(c.identb[:], ALU.not_equal, 1.0, 1, -1)
            keep(c.triu[:], ALU.is_ge, 0.0, -1, 1)
            keep(c.mask_qk[:, 0:P], ALU.is_gt, BIG, -1, 1)
            keep(c.mask_qk[:, P:2 * P], ALU.is_ge, BIG, 1, -1)
            keep(c.mask_first[:, P:2 * P], ALU.is_ge, BIG, 1, -1)
            keep(c.mask_kq[:, 0:P], ALU.is_ge, BIG, -1, 1)
            keep(c.mask_kq[:, P:2 * P], ALU.is_gt, BIG, 1, -1)
            pool.wait_ge(made, 8)


def layernorm(c, src, dst):
    nc = c.nc
    with ExitStack() as s:
        stats = c.sb(s, "stats", [P, T, 6])
        mv = c.sb(s, "mv", [P, T, 2])
        rstd = c.sb(s, "rstd", [P, T])
        root = c.sb(s, "root", [P, T])
        chain, var_ready, root_ready = c.sem("chain"), c.sem("var_ready"), c.sem("root_ready")
        stats_done = c.sem("stats_done")
        with nc.Block() as block:
            @block.vector
            def _(dve):
                line = Line(dve, chain)
                for t in range(T):
                    dve.bn_stats(stats[:, t, :], src[:, t, :]).then_inc(stats_done, 1)
                for t in range(T):
                    dve.wait_ge(stats_done, t + 1)
                    ins = dve.bn_aggr(mv[:, t, :], stats[:, t, :])
                    ins.then_inc(var_ready, 1)
                dve.wait_ge(root_ready, 1)
                line(dve.reciprocal(rstd[:], root[:]))
                for t in range(T):
                    last = dve.tensor_scalar(dst[:, t, :], src[:, t, :], mv[:, t, 0:1],
                                             rstd[:, t:t + 1], ALU.subtract, ALU.mult)
                line(last)

            @block.scalar
            def _(act):
                act.wait_ge(var_ready, T)
                nc.scalar.activation(root[:], mv[:, :, 1], ACT.Sqrt, bias=c.eps[:, 0:1]).then_inc(root_ready, 1)


def transpose_tiles(c, src, dst, tiles=T, rows=N, dt=F32, scale=None):
    nc = c.nc
    ident = c.identf if dt == F32 else c.identb
    groups = [(h, g) for h in range(DT) for g in range((tiles + 3) // 4)]
    with ExitStack() as s:
        slots = [c.ps(s, "tp", [P, BANK], dt) for _ in range(4)]
        turned, copied = c.sem("turned"), [c.sem("copied_dve"), c.sem("copied_act")]
        width = lambda g: min(4 * P, rows - 4 * P * g)
        with nc.Block() as block:
            @block.tensor
            def _(pe):
                for i, (h, g) in enumerate(groups):
                    if i >= 4:
                        pe.wait_ge(copied[i % 2], (i - 4) // 2 + 1)
                    for t in range(4 * g, min(4 * g + 4, tiles)):
                        n = min(P, rows - t * P)
                        o = (t - 4 * g) * P
                        last = pe.transpose(slots[i % 4][:, o:o + n], src[0:n, t, h * P:(h + 1) * P],
                                            ident[0:n, 0:n])
                    last.then_inc(turned, 1)

            def copy(i, eng):
                h, g = groups[i]
                n = width(g)
                eng.wait_ge(turned, i + 1)
                out, in_ = dst[:, h, 4 * P * g:4 * P * g + n], slots[i % 4][:, 0:n]
                if scale is not None:
                    if i % 2:
                        ins = nc.scalar.activation(out, in_, ACT.Copy, scale=scale[:, h:h + 1])
                    else:
                        ins = eng.tensor_scalar(out, in_, scale[:, h:h + 1], None, ALU.mult)
                else:
                    ins = nc.scalar.activation(out, in_, ACT.Copy) if i % 2 else eng.tensor_copy(out, in_)
                ins.then_inc(copied[i % 2], 1)

            @block.vector
            def _(dve):
                for i in range(0, len(groups), 2):
                    copy(i, dve)

            @block.scalar
            def _(act):
                for i in range(1, len(groups), 2):
                    copy(i, act)


def ceil_pow2(line, dve, m, low, step):
    line(dve.tensor_scalar(m, m, TINY_SCALE, None, ALU.max))
    line(dve.tensor_scalar(low.bitcast(I32), m.bitcast(I32), 0x7F800000, None, ALU.bitwise_and))
    line(dve.tensor_tensor(step, m, low, ALU.is_gt))
    line(dve.scalar_tensor_tensor(m, step, 1.0, low, ALU.add, ALU.mult))


def quantize(c, src, dst, tiles, cols, group, rows_first=False, fold=1.0):
    nc = c.nc
    G, B = cols // group, cols // P
    with ExitStack() as s:
        cmax = c.sb(s, "cmax", [P, cols])
        col = c.sb(s, "col", [P, B])
        cl, cs = c.sb(s, "cl", [P, B]), c.sb(s, "cs", [P, B])
        diag = c.sb(s, "diag", [P, B, P])
        cscale = c.sb(s, "cscale", [P, cols])
        cinv = c.sb(s, "cinv", [P, cols])
        row = c.sb(s, "row", [P, tiles * G])
        rl, rs = c.sb(s, "rl", [P, tiles * G]), c.sb(s, "rs", [P, tiles * G])
        nb = (cols + BANK - 1) // BANK
        turned_ps = c.ps(s, "turned_ps", [P, nb * BANK])
        spread_ps = c.ps(s, "spread_ps", [P, nb * BANK])
        chain, cmax_ready, turned = c.sem("chain"), c.sem("cmax_ready"), c.sem("turned")
        diag_ready, spread = c.sem("diag_ready"), c.sem("spread")
        grouped = src[:, :, :].rearrange("p t (g e) -> p (t g) e", e=group)
        over_cols = lambda a: a[:, None, :].to_broadcast([P, tiles, cols])
        over_group = lambda a: a[:, :, None].to_broadcast([P, tiles * G, group])
        with nc.Block() as block:
            @block.vector
            def _(dve):
                line = Line(dve, chain)

                def column_scales():
                    dve.tensor_reduce(cmax[:], src[:, :, :].rearrange("p t c -> p c t"), X, ALU.max,
                                      apply_absolute_value=True).then_inc(cmax_ready, 1)
                    dve.wait_ge(turned, 1)
                    line(dve.tensor_reduce(col[:], turned_ps[:, 0:cols].rearrange("p (b q) -> p b q", q=P),
                                           X, ALU.max))
                    ceil_pow2(line, dve, col[:], cl[:], cs[:])
                    for b in range(B):
                        last = dve.tensor_scalar(diag[:, b, :], c.identf[:], col[:, b:b + 1], None, ALU.mult)
                        last.then_inc(diag_ready, 1)
                    dve.wait_ge(spread, 1)
                    line(dve.tensor_copy(cscale[:], spread_ps[:, 0:cols]))
                    line(dve.reciprocal(cinv[:], cscale[:]))

                def row_scales():
                    line(dve.tensor_reduce(row[:], grouped, X, ALU.max, apply_absolute_value=True))
                    ceil_pow2(line, dve, row[:], rl[:], rs[:])
                    line(dve.reciprocal(rl[:], row[:]))

                def to_integers():
                    line(dve.tensor_scalar(src[:, :, :], src[:, :, :], MAGIC, MAGIC + HALF - 1, ALU.add, ALU.min))

                if not rows_first:
                    column_scales()
                    line(dve.tensor_tensor(src[:, :, :], src[:, :, :], over_cols(cinv), ALU.mult))
                    row_scales()
                    line(dve.tensor_scalar(rl[:], rl[:], HALF, None, ALU.mult))
                    line(dve.tensor_tensor(grouped, grouped, over_group(rl), ALU.mult))
                    to_integers()
                    line(dve.tensor_scalar(row[:], row[:], fold / HALF, None, ALU.mult))
                    line(dve.scalar_tensor_tensor(grouped, grouped, -MAGIC, over_group(row), ALU.add, ALU.mult))
                    line(dve.tensor_tensor(dst[:, :, :], src[:, :, :], over_cols(cscale), ALU.mult))
                else:
                    row_scales()
                    line(dve.tensor_tensor(grouped, grouped, over_group(rl), ALU.mult))
                    column_scales()
                    line(dve.tensor_scalar(cinv[:], cinv[:], HALF, None, ALU.mult))
                    line(dve.tensor_tensor(src[:, :, :], src[:, :, :], over_cols(cinv), ALU.mult))
                    to_integers()
                    line(dve.tensor_scalar(row[:], row[:], fold / HALF, None, ALU.mult))
                    line(dve.scalar_tensor_tensor(grouped, grouped, -MAGIC, over_group(row), ALU.add, ALU.mult))
                    line(dve.tensor_tensor(dst[:, :, :], src[:, :, :], over_cols(cscale), ALU.mult))

            @block.tensor
            def _(pe):
                pe.wait_ge(cmax_ready, 1)
                for b in range(B):
                    last = pe.transpose(turned_ps[:, b * P:(b + 1) * P], cmax[:, b * P:(b + 1) * P], c.identf[:])
                last.then_inc(turned, 1)
                pe.wait_ge(diag_ready, B)
                for b in range(B):
                    last = pe.matmul(spread_ps[:, b * P:(b + 1) * P], c.onesf[:], diag[:, b, :],
                                     start=True, stop=True)
                last.then_inc(spread, 1)


def load(c, pairs):
    nc = c.nc
    loaded = [c.sem("loaded_sp"), c.sem("loaded_act")]
    with nc.Block() as block:
        def send(eng, half):
            mine = pairs[half::2]
            for dst, src in mine:
                eng.dma_start(dst, src).then_inc(loaded[half], 16)
            if mine:
                eng.wait_ge(loaded[half], 16 * len(mine))

        @block.sync
        def _(sp):
            send(sp, 0)

        @block.scalar
        def _(act):
            send(act, 1)


def row_of(vec, n):
    return vec.rearrange("(o n) -> o n", o=1).to_broadcast([P, n])


def project_tokens(c, lhs, rhs, bias, width, tiles, rows, dst, scale=None, residual=None):
    nc = c.nc
    spans = [(o, min(BANK, width - o)) for o in range(0, width, BANK)]
    with ExitStack() as s:
        slots = [c.ps(s, "prod", [P, len(spans) * BANK]) for _ in range(8 // len(spans) // 2)]
        K = len(slots)
        temp = c.sb(s, "temp", [P, 2, width])
        multiplied, added, chain = c.sem("multiplied"), c.sem("added"), c.sem("chain")
        with nc.Block() as block:
            @block.tensor
            def _(pe):
                for t in range(tiles):
                    n = min(P, rows - t * P)
                    if t >= K:
                        pe.wait_ge(added, t - K + 1)
                    for o, w in spans:
                        for k in range(DT):
                            last = pe.matmul(slots[t % K][0:n, o:o + w], lhs[:, k, t * P:t * P + n],
                                             rhs[:, k, o:o + w], start=(k == 0), stop=(k == DT - 1))
                    last.then_inc(multiplied, 1)

            @block.vector
            def _(dve):
                line = Line(dve, chain)
                for t in range(tiles):
                    n = min(P, rows - t * P)
                    dve.wait_ge(multiplied, t + 1)
                    src = slots[t % K][0:n, 0:width]
                    if scale is not None:
                        line(dve.scalar_tensor_tensor(temp[0:n, t % 2, :], src, scale[0:n, t:t + 1],
                                                      bias[0:n, 0:width], ALU.mult, ALU.add))
                    elif residual is not None:
                        line(dve.tensor_tensor(temp[0:n, t % 2, :], src, bias[0:n, 0:width], ALU.add))
                    if residual is not None:
                        ins = dve.tensor_tensor(dst[0:n, t, :], temp[0:n, t % 2, :], residual[0:n, t, :], ALU.add)
                    else:
                        ins = dve.tensor_tensor(dst[0:n, t, 0:width], src, bias[0:n, 0:width], ALU.add)
                    ins.then_inc(added, 1)
                dve.wait_ge(added, tiles)


def transposed_to_dram(c, srcs):
    nc = c.nc
    jobs = [(n, h, g) for n in range(len(srcs)) for h in range(DT) for g in range(T // 4)]
    per_half = T // 4
    with ExitStack() as s:
        slots = [c.ps(s, "tp", [P, 4 * P], BF16) for _ in range(4)]
        stage = c.sb(s, "stage", [P, len(srcs), DT, N], BF16)
        turned, copied, stored = c.sem("turned"), c.sem("copied"), c.sem("stored")
        with nc.Block() as block:
            @block.tensor
            def _(pe):
                for i, (n, h, g) in enumerate(jobs):
                    if i >= 4:
                        pe.wait_ge(copied, i - 3)
                    for t in range(4):
                        last = pe.transpose(slots[i % 4][:, t * P:(t + 1) * P],
                                            srcs[n][0][:, 4 * g + t, h * P:(h + 1) * P], c.identb[:])
                    last.then_inc(turned, 1)

            @block.vector
            def _(dve):
                for i, (n, h, g) in enumerate(jobs):
                    dve.wait_ge(turned, i + 1)
                    dve.tensor_copy(stage[:, n, h, g * BANK:(g + 1) * BANK], slots[i % 4][:]).then_inc(copied, 1)

            @block.sync
            def _(sp):
                for n, (_, op) in enumerate(srcs):
                    for h in range(DT):
                        sp.wait_ge(copied, (n * DT + h + 1) * per_half)
                        for e in range(HALF_HEADS):
                            sp.dma_start(op[0:HD, h * HALF_HEADS + e, :],
                                         stage[e * HD:(e + 1) * HD, n, h, :]).then_inc(stored, 16)
                sp.wait_ge(stored, 16 * len(srcs) * H)


def split_rows(c, values, rows):
    nc = c.nc
    W = H * T
    rows = [r.rearrange("h (t q) -> (h t) q", q=P) for r in rows]
    with ExitStack() as s:
        part = c.sb(s, "part", [P, PARTS, W], BF16)
        rest = c.sb(s, "rest", [P, 2, W])
        turned_sb = c.sb(s, "turned_sb", [P, PARTS, W // P, P], BF16)
        turned_ps = c.ps(s, "turned_ps", [P, PARTS, W // P, P], BF16)
        chain, parted, turned, copied, stored = (c.sem("chain"), c.sem("parted"), c.sem("turned"),
                                                 c.sem("copied"), c.sem("stored"))
        with nc.Block() as block:
            @block.vector
            def _(dve):
                line = Line(dve, chain)
                line(dve.tensor_copy(part[:, 0, :], values))
                line(dve.tensor_tensor(rest[:, 0, :], values, part[:, 0, :], ALU.subtract))
                line(dve.tensor_copy(part[:, 1, :], rest[:, 0, :]))
                line(dve.tensor_tensor(rest[:, 1, :], rest[:, 0, :], part[:, 1, :], ALU.subtract))
                dve.tensor_copy(part[:, 2, :], rest[:, 1, :]).then_inc(parted, 1)
                dve.wait_ge(turned, 1)
                dve.tensor_copy(turned_sb[:], turned_ps[:]).then_inc(copied, 1)

            @block.tensor
            def _(pe):
                pe.wait_ge(parted, 1)
                for i in range(PARTS):
                    for b in range(W // P):
                        last = pe.transpose(turned_ps[:, i, b, :], part[:, i, b * P:(b + 1) * P], c.identb[:])
                last.then_inc(turned, 1)

            @block.sync
            def _(sp):
                sp.wait_ge(copied, 1)
                for i in range(PARTS):
                    sp.dma_start(rows[i].rearrange("(b r) q -> r b q", r=P), turned_sb[:, i, :, :]).then_inc(stored, 16)
                sp.wait_ge(stored, 16 * PARTS)


R1, R2, R3 = HD, HD + PARTS, HD + 2 * PARTS


def causal_stats(c, operands, low, sums):
    nc = c.nc
    units = [(t, o, min(o + WIDE, (t + 1) * P)) for t in range(T) for o in range(0, (t + 1) * P, WIDE)]
    U, S = len(units), 4
    assert (2 * U) % S == 0
    with ExitStack() as s:
        q_sb = [c.sb(s, "q_sb", [R3, N], BF16) for _ in range(2)]
        k_sb = [c.sb(s, "k_sb", [R3, N], BF16) for _ in range(2)]
        slots = [c.ps(s, "score", [P, WIDE]) for _ in range(S)]
        loaded = [c.sem("loaded0"), c.sem("loaded1")]
        scored, maxed, summed = c.sem("scored"), c.sem("maxed"), c.sem("summed")
        q_op, k_op = operands

        def column(g, par, unit):
            t, o, _ = unit
            return bass.ds(g * (2 * T * NWIDE) + ((par * T + t) * NWIDE + o // WIDE), 1)

        with nc.Block() as block:
            @block.sync
            def _(sp):
                def loads(head, par, wait_for):
                    wait(sp, scored, wait_for)
                    sp.dma_start(q_sb[par][0:R1, None, :], q_op[0:R1, bass.ds(head, 1), :]).then_inc(loaded[par], 16)
                    sp.dma_start(k_sb[par][0:R1, None, :], k_op[0:R1, bass.ds(head, 1), :]).then_inc(loaded[par], 16)

                loads(0, 0, 0)
                loads(1, 1, 0)
                with sp.Fori(0, H // 2 - 1) as g:
                    for par in range(2):
                        loads(g * 2 + (2 + par), par, g * (2 * U) + U * (par + 1))

            @block.tensor
            def _(pe):
                with pe.Fori(0, H // 2) as g:
                    for par in range(2):
                        pe.wait_ge(loaded[par], (g + 1) * (16 * 2))
                        for u, (t, lo, hi) in enumerate(units):
                            i = par * U + u
                            pe.wait_ge(summed, g * (2 * U) + (i + 1))
                            diag = t * P - lo
                            for a in range(0, hi - lo, BANK):
                                b = min(a + BANK, hi - lo)
                                has_diag = a <= diag < b
                                last = pe.matmul(slots[i % S][:, a:b], q_sb[par][0:R1, t * P:(t + 1) * P],
                                                 k_sb[par][0:R1, lo + a:lo + b], start=True, stop=not has_diag)
                                if has_diag:
                                    last = pe.matmul(slots[i % S][:, diag:diag + P], c.identb[:],
                                                     c.mask_qk[:, P:2 * P], start=False, stop=True)
                            last.then_inc(scored, 1)

            @block.vector
            def _(dve):
                with dve.Fori(0, H // 2) as g:
                    for par in range(2):
                        for u, unit in enumerate(units):
                            i = par * U + u
                            dve.wait_ge(scored, g * (2 * U) + (i + 1))
                            dve.tensor_reduce(low[:, column(g, par, unit)], slots[i % S][:, 0:unit[2] - unit[1]],
                                              X, ALU.max, negate=True).then_inc(maxed, 1)

            @block.scalar
            def _(act):
                act.sem_inc(summed, S)
                with act.Fori(0, H // 2) as g:
                    for par in range(2):
                        for u, unit in enumerate(units):
                            i = par * U + u
                            act.wait_ge(maxed, g * (2 * U) + (i + 1))
                            score = slots[i % S][:, 0:unit[2] - unit[1]]
                            nc.scalar.activation(score, score, ACT.Exp, bias=low[:, column(g, par, unit)],
                                                 accum_out=sums[:, column(g, par, unit)]).then_inc(summed, 1)


def causal_maxima(c, operands, rows, by_key, out):
    nc = c.nc
    with ExitStack() as s:
        q_sb = [c.sb(s, "q_sb", [R3, N], BF16) for _ in range(2)]
        k_sb = [c.sb(s, "k_sb", [R3, N], BF16) for _ in range(2)]
        slots = [c.ps(s, "score", [P, N]) for _ in range(2)]
        loaded = [c.sem("loaded0"), c.sem("loaded1")]
        scored, maxed = c.sem("scored"), c.sem("maxed")
        q_op, k_op = operands
        n_loads = 2

        def span(t):
            return (t * P, N) if by_key else (0, (t + 1) * P)

        with nc.Block() as block:
            @block.sync
            def _(sp):
                def loads(head, par, wait_for):
                    wait(sp, scored, wait_for)
                    sp.dma_start(q_sb[par][0:rows, None, :], q_op[0:rows, bass.ds(head, 1), :]).then_inc(loaded[par], 16)
                    sp.dma_start(k_sb[par][0:rows, None, :], k_op[0:rows, bass.ds(head, 1), :]).then_inc(loaded[par], 16)

                loads(0, 0, 0)
                loads(1, 1, 0)
                with sp.Fori(0, H // 2 - 1) as g:
                    for par in range(2):
                        loads(g * 2 + (2 + par), par, g * (2 * T) + T * (par + 1))

            @block.tensor
            def _(pe):
                with pe.Fori(0, H // 2) as g:
                    for par in range(2):
                        pe.wait_ge(loaded[par], (g + 1) * (16 * n_loads))
                        for t in range(T):
                            i = par * T + t
                            pe.wait_ge(maxed, g * (2 * T) + (i + 1))
                            lo, hi = span(t)
                            moving, still = (q_sb, k_sb) if by_key else (k_sb, q_sb)
                            diag = t * P
                            for o in range(lo // BANK * BANK, hi, BANK):
                                a, b = max(o, lo), min(o + BANK, hi)
                                has_diag = a <= diag < b
                                last = pe.matmul(slots[i % 2][:, a:b], still[par][0:rows, t * P:(t + 1) * P],
                                                 moving[par][0:rows, a:b], start=True, stop=not has_diag)
                                if has_diag:
                                    mask = c.mask_kq[:, 0:P] if by_key else c.mask_qk[:, P:2 * P]
                                    last = pe.matmul(slots[i % 2][:, diag:diag + P], c.identb[:], mask,
                                                     start=False, stop=True)
                            last.then_inc(scored, 1)

            @block.vector
            def _(dve):
                dve.sem_inc(maxed, 2)
                with dve.Fori(0, H // 2) as g:
                    for par in range(2):
                        for t in range(T):
                            i = par * T + t
                            dve.wait_ge(scored, g * (2 * T) + (i + 1))
                            lo, hi = span(t)
                            dve.tensor_reduce(out[:, bass.ds(g * (2 * T) + i, 1)], slots[i % 2][:, lo:hi], X,
                                              ALU.max).then_inc(maxed, 1)


def causal_weights(c, operands, values32, out_rows):
    nc = c.nc
    units = [(k, max(k * P, a), a + N // 2) for k in range(T) for a in (0, N // 2) if k * P < a + N // 2]
    U, LAG, S = len(units), 2, 3
    assert (2 * U) % S == 0
    with ExitStack() as s:
        q_sb = [c.sb(s, "q_sb", [R3, N], BF16) for _ in range(2)]
        k_sb = [c.sb(s, "k_sb", [R3, N], BF16) for _ in range(2)]
        v_sb = [c.sb(s, "v_sb", [P, T, 32], BF16) for _ in range(2)]
        slots = [c.ps(s, "score", [P, N // 2]) for _ in range(S)]
        sums = [c.ps(s, "sums", [P, BANK]) for _ in range(2)]
        rounded = [c.sb(s, "rounded", [P, N // 2], U8) for _ in range(S)]
        weights = [c.sb(s, "weights", [P, N // 2], BF16) for _ in range(S)]
        stage = [c.sb(s, "stage", [P, BANK]) for _ in range(2)]
        loaded = [c.sem("loaded0"), c.sem("loaded1")]
        scored, exped, clipped, used = c.sem("scored"), c.sem("exped"), c.sem("clipped"), c.sem("used")
        staged, stored = c.sem("staged"), [c.sem("stored0"), c.sem("stored1")]
        q_op, k_op = operands
        HEAD_PAIRS = H // 2
        with nc.Block() as block:
            @block.sync
            def _(sp):
                def loads(head, par, products, sums_):
                    wait(sp, used, sums_)
                    sp.dma_start(q_sb[par][0:R3, None, :], q_op[0:R3, bass.ds(head, 1), :]).then_inc(loaded[par], 16)
                    sp.dma_start(k_sb[par][0:R3, None, :], k_op[0:R3, bass.ds(head, 1), :]).then_inc(loaded[par], 16)
                    sp.dma_start(v_sb[par][:, None, :, :], values32[:, bass.ds(head, 1), :, :]).then_inc(loaded[par], 16)

                def store(head, par, n):
                    sp.wait_ge(staged, n)
                    sp.dma_start(out_rows[bass.ds(head, 1), :, :].rearrange("o p q -> (o p) q"), stage[par][:]).then_inc(stored[par], 16)

                loads(0, 0, 0, 0)
                loads(1, 1, 0, 0)
                with sp.Fori(0, HEAD_PAIRS - 1) as g:
                    for par in range(2):
                        loads(g * 2 + (2 + par), par, 0, g * (2 * U) + U * (par + 1))
                        store(g * 2 + par, par, g * 2 + (par + 1))
                for par in range(2):
                    store(H - 2 + par, par, H - 1 + par)
                for par in range(2):
                    sp.wait_ge(stored[par], 16 * HEAD_PAIRS)

            @block.tensor
            def _(pe):
                def score(g, i):
                    par, (k, lo, hi), slot = i // U % 2, units[i % U], i % S
                    if i % U == 0:
                        pe.wait_ge(loaded[par], (g + (i // U // 2 + 1)) * (16 * 3))
                    if not (isinstance(g, int) and g * 2 * U + i < S):
                        pe.wait_ge(exped, g * (2 * U) + (i - S + 1))
                    a0 = hi - N // 2
                    diag = k * P
                    for o in range(lo // BANK * BANK, hi, BANK):
                        a, b = max(o, lo), min(o + BANK, hi)
                        has_diag = a <= diag < b
                        last = pe.matmul(slots[slot][:, a - a0:b - a0], k_sb[par][0:R3, k * P:(k + 1) * P],
                                         q_sb[par][0:R3, a:b], start=True, stop=not has_diag)
                        if has_diag:
                            last = pe.matmul(slots[slot][:, diag - a0:diag - a0 + P], c.identb[:],
                                             c.mask_kq[:, 0:P], start=False, stop=True)
                    last.then_inc(scored, 1)

                def add_up(g, i):
                    par, (k, lo, hi), slot = i // U, units[i % U], i % S
                    pe.wait_ge(clipped, g * (2 * U) + (i + 1))
                    if i % U == 0:
                        wait(pe, staged, g * 2 + (par - 1))
                    a0 = hi - N // 2
                    for o in range(lo // BANK * BANK, hi, BANK):
                        a, b, j = max(o, lo), min(o + BANK, hi), o // BANK
                        last = pe.matmul(sums[par][32 * j:32 * j + 32, a - o:b - o], v_sb[par][:, k, :],
                                         weights[slot][:, a - a0:b - a0], start=(k == 0),
                                         stop=(k == 4 * j + 3), skip_group_check=True)
                    last.then_inc(used, 1)

                def pair(g, more):
                    for i in range(2 * U):
                        if more or i + LAG < 2 * U:
                            score(g, i + LAG)
                        add_up(g, i)

                for i in range(LAG):
                    score(0, i)
                pair(0, True)
                with pe.Fori(1, HEAD_PAIRS - 1) as g:
                    pair(g, True)
                pair(HEAD_PAIRS - 1, False)

            @block.scalar
            def _(act):
                def exp(g, i):
                    k, lo, hi = units[i % U]
                    a0 = hi - N // 2
                    act.wait_ge(scored, g * (2 * U) + (i + 1))
                    if not (isinstance(g, int) and i < S):
                        act.wait_ge(clipped, g * (2 * U) + (i - S + 1))
                    nc.scalar.activation(rounded[i % S][:, lo - a0:hi - a0], slots[i % S][:, lo - a0:hi - a0],
                                         ACT.Exp).then_inc(exped, 1)

                for i in range(2 * U):
                    exp(0, i)
                with act.Fori(1, HEAD_PAIRS) as g:
                    for i in range(2 * U):
                        exp(g, i)

            @block.vector
            def _(dve):
                def clip(g, i):
                    k, lo, hi = units[i % U]
                    a0 = hi - N // 2
                    dve.wait_ge(exped, g * (2 * U) + (i + 1))
                    if not (isinstance(g, int) and i < S):
                        dve.wait_ge(used, g * (2 * U) + (i - S + 1))
                    dve.tensor_scalar(weights[i % S][:, lo - a0:hi - a0], rounded[i % S][:, lo - a0:hi - a0],
                                      HALF - 1, None, ALU.min).then_inc(clipped, 1)

                def evacuate(g, par):
                    dve.wait_ge(used, g * (2 * U) + U * (par + 1))
                    wait(dve, stored[par], g * 16)
                    dve.tensor_copy(stage[par][:], sums[par][:]).then_inc(staged, 1)

                def pair(g, first, last):
                    for i in range(2 * U):
                        clip(g, i)
                        if i == LAG + 1 and not first:
                            evacuate(g - 1, 1)
                        if i == U + LAG + 1:
                            evacuate(g, 0)
                    if last:
                        evacuate(g, 1)

                pair(0, True, False)
                pair(1, False, False)
                with dve.Fori(2, HEAD_PAIRS - 1) as g:
                    pair(g, False, False)
                pair(HEAD_PAIRS - 1, False, True)


def layer0_attention(c, w_attn, b_attn, w_proj, b_proj, upto=None):
    nc = c.nc
    q_op = c.dram("q_op", [R3, H, N], BF16)
    k_op = c.dram("k_op", [R3, H, N], BF16)
    sums = c.dram("sums", [H, P, BANK])
    scales = c.dram("scales", [H, N])
    with ExitStack() as s:
        wp = c.sb(s, "wp", [P, DT, D], BF16)
        b_proj_sb = c.sb(s, "b_proj_sb", [P, D])
        values = c.sb(s, "values", [P, T, D], BF16)
        with ExitStack() as s1:
            wq = c.sb(s1, "wq", [P, DT, 3 * D], BF16)
            hT = c.sb(s1, "hT", [P, DT, N], BF16)
            b_attn_sb = c.sb(s1, "b_attn_sb", [P, 3 * D])
            with ExitStack() as s2:
                h = c.sb(s2, "h", [P, T, D])
                hq = c.sb(s2, "hq", [P, T, D], BF16)
                wa = c.sb(s2, "wa", [P, DT, 3 * D])
                wo = c.sb(s2, "wo", [P, DT, D])
                load(c, [(wa[:], w_attn.rearrange("(k p) n -> p k n", p=P)),
                         (wo[:], w_proj.rearrange("(k p) n -> p k n", p=P)),
                         (b_attn_sb[:], row_of(b_attn, 3 * D)), (b_proj_sb[:], row_of(b_proj, D)),
                         ] + [(op[a:a + PARTS].rearrange("r (g h) n -> (r g) (h n)", g=8), c.ones_wide[0:8 * PARTS, :])
                              for op, a in ((q_op, R2), (k_op, R1))])
                layernorm(c, c.x, h)
                quantize(c, h, hq, T, D, D)
                quantize(c, wa, wq, DT, 3 * D, 3 * D)
                quantize(c, wo, wp, DT, D, D)
                transpose_tiles(c, hq, hT, dt=BF16)
            qkv = [c.sb(s1, n, [P, T, D]) for n in ("q", "k", "v")]
            for i, dst in enumerate(qkv):
                project_tokens(c, hT, wq[:, :, i * D:(i + 1) * D], b_attn_sb[:, i * D:(i + 1) * D], D, T, N, dst)
            qd = c.sb(s1, "qd", [P, T, D], BF16)
            kd = c.sb(s1, "kd", [P, T, D], BF16)
            quantize(c, qkv[0], qd, T, D, HD, fold=HD ** -0.5)
            quantize(c, qkv[1], kd, T, D, HD, rows_first=True)
            quantize(c, qkv[2], values, T, D, HD)
            transposed_to_dram(c, [(qd, q_op), (kd, k_op)])
        c.recycle()
        HT = H * T
        values32 = c.sb(s, "values32", [P, H, T, 32], BF16)
        shift, total, logs = c.sb(s, "shift", [P, HT]), c.sb(s, "total", [P, HT]), c.sb(s, "logs", [P, HT])
        scale, low, step = c.sb(s, "scale", [P, HT]), c.sb(s, "low", [P, HT]), c.sb(s, "step", [P, HT])
        top = c.sb(s, "top", [P, HT])

        def small(*steps):
            chain = c.sem("chain")
            order = list(enumerate(steps))
            with nc.Block() as block:
                def run(eng, mine):
                    for i, (who, f) in order:
                        if who == mine:
                            wait(eng, chain, i)
                            f(eng).then_inc(chain, 1)

                @block.vector
                def _(dve):
                    run(dve, "dve")

                @block.scalar
                def _(act):
                    run(act, "act")

                @block.gpsimd
                def _(pool):
                    run(pool, "pool")

        act = lambda out, in_, f, **k: ("act", lambda e: nc.scalar.activation(out, in_, f, **k))
        two = lambda out, a, b, op: ("dve", lambda e: e.tensor_tensor(out, a, b, op))
        one = lambda out, a, v, op: ("dve", lambda e: e.tensor_scalar(out, a, v, None, op))

        def scale_of(m):
            return [act(scale[:], m, ACT.Exp), one(scale[:], scale[:], TINY_SCALE, ALU.max),
                    ("dve", lambda e: e.tensor_scalar(low[:].bitcast(I32), scale[:].bitcast(I32), 0x7F800000, None,
                                                      ALU.bitwise_and)),
                    two(step[:], scale[:], low[:], ALU.is_gt),
                    ("dve", lambda e: e.scalar_tensor_tensor(scale[:], step[:], 1.0, low[:], ALU.add, ALU.mult))]

        with ExitStack() as s1:
            lows, sums1 = c.sb(s1, "lows", [P, HT * NWIDE]), c.sb(s1, "sums", [P, HT * NWIDE])
            by_chunk = lambda a: a[:].rearrange("p (i c) -> p i c", c=NWIDE)
            small(("dve", lambda e: e.memset(lows[:], -BIG)), ("dve", lambda e: e.memset(sums1[:], 0.0)))
            causal_stats(c, (q_op, k_op), lows, sums1)
            small(("dve", lambda e: e.tensor_reduce(shift[:], by_chunk(lows), X, ALU.min)),
                  two(by_chunk(lows), shift[:, :, None].to_broadcast([P, HT, NWIDE]), by_chunk(lows), ALU.subtract),
                  act(lows[:], lows[:], ACT.Exp), two(sums1[:], sums1[:], lows[:], ALU.mult),
                  ("dve", lambda e: e.tensor_reduce(total[:], by_chunk(sums1), X, ALU.add)),
                  act(logs[:], total[:], ACT.Ln), two(shift[:], shift[:], logs[:], ALU.subtract))
        split_rows(c, shift[:], [q_op[R1 + i] for i in range(PARTS)])
        causal_maxima(c, (q_op, k_op), R2, True, top)
        by_tile = scale[:].rearrange("p (h t) -> p h t", h=H)
        small(*scale_of(top[:]), act(logs[:], scale[:], ACT.Ln), one(logs[:], logs[:], -1.0, ALU.mult),
              ("dve", lambda e: e.memset(values32[:], 0.0)),
              ("dve", lambda e: e.tensor_tensor(values32[:, :, :, 0:HD],
                                                values[:, :, :].rearrange("p t (h e) -> p h t e", e=HD),
                                                by_tile[:, :, :, None].to_broadcast([P, H, T, HD]), ALU.mult)))
        split_rows(c, logs[:], [k_op[R2 + i] for i in range(PARTS)])
        causal_maxima(c, (q_op, k_op), R3, False, top)
        small(*scale_of(top[:]), one(scale[:], scale[:], 1.0 / HALF, ALU.mult), act(logs[:], scale[:], ACT.Ln),
              two(shift[:], shift[:], logs[:], ALU.subtract))
        split_rows(c, shift[:], [q_op[R1 + i] for i in range(PARTS)])
        rows_to_dram(c, scale[:], scales)
        causal_weights(c, (q_op, k_op), values32, sums)
        quantized_output(c, sums, scales, wp, b_proj_sb)


def rows_to_dram(c, values, out):
    nc = c.nc
    W = H * T
    with ExitStack() as s:
        ps = c.ps(s, "turned", [P, W // P, P])
        sb = c.sb(s, "turned", [P, W // P, P])
        turned, copied, stored = c.sem("turned"), c.sem("copied"), c.sem("stored")
        with nc.Block() as block:
            @block.tensor
            def _(pe):
                for b in range(W // P):
                    last = pe.transpose(ps[:, b, :], values[:, b * P:(b + 1) * P], c.identf[:])
                last.then_inc(turned, 1)

            @block.vector
            def _(dve):
                dve.wait_ge(turned, 1)
                dve.tensor_copy(sb[:], ps[:]).then_inc(copied, 1)

            @block.sync
            def _(sp):
                sp.wait_ge(copied, 1)
                sp.dma_start(out.rearrange("h (t q) -> (h t) q", q=P).rearrange("(b r) q -> r b q", r=P),
                             sb[:]).then_inc(stored, 16)
                sp.wait_ge(stored, 16)


def quantized_output(c, sums, scales, wp, bias):
    nc = c.nc
    with ExitStack() as s:
        oT = c.sb(s, "oT", [P, DT, N])
        by_query = c.sb(s, "by_query", [P, DT, N])
        o = c.sb(s, "o", [P, T, D])
        oq = c.sb(s, "oq", [P, T, D], BF16)
        oqT = c.sb(s, "oqT", [P, DT, N], BF16)
        col, cl, cs, ci = (c.sb(s, n, [P, DT]) for n in ("col", "cl", "cs", "ci"))
        row, rl, rs = (c.sb(s, n, [P, T]) for n in ("row", "rl", "rs"))
        load_heads(c, sums, oT, scales=(scales, by_query))
        chain = c.sem("chain")
        with nc.Block() as block:
            @block.vector
            def _(dve):
                line = Line(dve, chain)
                line(dve.tensor_tensor(oT[:], oT[:], by_query[:], ALU.mult))
                line(dve.tensor_reduce(col[:], oT[:], X, ALU.max, apply_absolute_value=True))
                ceil_pow2(line, dve, col[:], cl[:], cs[:])
                line(dve.reciprocal(ci[:], col[:]))
        transpose_tiles_back(c, oT, o, ci)
        rows_scaled = c.sem("rows_scaled")
        with nc.Block() as block:
            @block.vector
            def _(dve):
                line = Line(dve, rows_scaled)
                line(dve.tensor_reduce(row[:], o[:], X, ALU.max, apply_absolute_value=True))
                ceil_pow2(line, dve, row[:], rl[:], rs[:])
                line(dve.reciprocal(rl[:], row[:]))
                line(dve.tensor_scalar(rl[:], rl[:], HALF, None, ALU.mult))
                line(dve.tensor_tensor(o[:], o[:], rl[:, :, None].to_broadcast([P, T, D]), ALU.mult))
                line(dve.tensor_scalar(o[:], o[:], MAGIC, MAGIC + HALF - 1, ALU.add, ALU.min))
                line(dve.tensor_scalar(oq[:], o[:], MAGIC, None, ALU.subtract))
                line(dve.tensor_scalar(row[:], row[:], 1.0 / HALF, None, ALU.mult))
        transpose_tiles(c, oq, oqT, dt=BF16, scale=col)
        project_tokens(c, oqT, wp, bias, D, T, N, c.x, scale=row, residual=c.x)


def load_heads(c, sums, oT, scales=None, totals=None):
    jobs = []
    for h in range(H):
        half, p = h // HALF_HEADS, h % HALF_HEADS * HD
        by_row = sums[h].rearrange("(j r) q -> r j q", r=32)
        jobs.append((oT[p:p + HD, half, :].rearrange("p (j q) -> p j q", q=BANK), by_row[0:HD]))
        if totals is not None:
            jobs.append((totals[p:p + HD, half, :].rearrange("p (j q) -> p j q", q=BANK), by_row[HD:2 * HD]))
        if scales is not None:
            jobs.append((scales[1][p:p + HD, half, :], scales[0][h:h + 1, :].to_broadcast([HD, N])))
    load(c, jobs)


def transpose_tiles_back(c, src, dst, scale):
    nc = c.nc
    with ExitStack() as s:
        slots = [c.ps(s, "tp", [P, 2 * D]) for _ in range(4)]
        scaled, turned, copied = c.sem("scaled"), c.sem("turned"), c.sem("copied")
        with nc.Block() as block:
            @block.scalar
            def _(act):
                for h in range(DT):
                    nc.scalar.activation(src[:, h, :], src[:, h, :], ACT.Copy, scale=scale[:, h:h + 1]).then_inc(scaled, 1)

            @block.tensor
            def _(pe):
                pe.wait_ge(scaled, DT)
                for i in range(T // 2):
                    if i >= 4:
                        pe.wait_ge(copied, i - 3)
                    for t in range(2):
                        for h in range(DT):
                            last = pe.transpose(slots[i % 4][:, t * D + h * P:t * D + (h + 1) * P],
                                                src[:, h, (2 * i + t) * P:(2 * i + t + 1) * P], c.identf[:])
                    last.then_inc(turned, 1)

            @block.vector
            def _(dve):
                for i in range(T // 2):
                    dve.wait_ge(turned, i + 1)
                    dve.tensor_copy(dst[:, 2 * i:2 * i + 2, :],
                                    slots[i % 4][:].rearrange("p (t d) -> p t d", t=2)).then_inc(copied, 1)


def project_features(c, lhs, rhs, bias, cols, dst, scale=1.0):
    nc = c.nc
    jobs = [(h, o, min(BANK, cols - o)) for h in range(DT) for o in range(0, cols, BANK)]
    with ExitStack() as s:
        slots = [c.ps(s, "prod", [P, BANK]) for _ in range(4)]
        scaled = c.sb(s, "scaled", [P, DT])
        multiplied, bias_ready = c.sem("multiplied"), c.sem("bias_ready")
        added = [c.sem("added_dve"), c.sem("added_act")]
        with nc.Block() as block:
            @block.tensor
            def _(pe):
                for i, (h, o, w) in enumerate(jobs):
                    if i >= 4:
                        pe.wait_ge(added[i % 2], (i - 4) // 2 + 1)
                    for k in range(DT):
                        last = pe.matmul(slots[i % 4][:, 0:w], lhs[:, k, h * P:(h + 1) * P],
                                         rhs[:, k, o:o + w], start=(k == 0), stop=(k == DT - 1))
                    last.then_inc(multiplied, 1)

            @block.vector
            def _(dve):
                dve.tensor_scalar(scaled[:], bias[:], scale, None, ALU.mult).then_inc(bias_ready, 1)
                dve.wait_ge(bias_ready, 1)
                for i in range(0, len(jobs), 2):
                    h, o, w = jobs[i]
                    dve.wait_ge(multiplied, i + 1)
                    dve.tensor_scalar(dst[:, h, o:o + w], slots[i % 4][:, 0:w], scale, scaled[:, h:h + 1],
                                      ALU.mult, ALU.add).then_inc(added[0], 1)

            @block.scalar
            def _(act):
                act.wait_ge(bias_ready, 1)
                for i in range(1, len(jobs), 2):
                    h, o, w = jobs[i]
                    act.wait_ge(multiplied, i + 1)
                    nc.scalar.activation(dst[:, h, o:o + w], slots[i % 4][:, 0:w], ACT.Identity,
                                         bias=scaled[:, h:h + 1], scale=scale).then_inc(added[1], 1)


def split_to_dram(c, src, cols, parts):
    nc = c.nc
    step = 2 * BANK
    jobs = [(h, o, min(step, cols - o)) for h in range(DT) for o in range(0, cols, step)]
    J = len(jobs)
    with ExitStack() as s:
        part = c.sb(s, "part", [P, J, PARTS, step], BF16)
        rest = c.sb(s, "rest", [P, 2, step])
        high, middle, rested, low, stored = (c.sem("high"), c.sem("middle"), c.sem("rested"), c.sem("low"),
                                             c.sem("stored"))
        with nc.Block() as block:
            @block.scalar
            def _(act):
                for i, (h, o, w) in enumerate(jobs):
                    nc.scalar.activation(part[:, i, 0, 0:w], src[:, h, o:o + w], ACT.Copy).then_inc(high, 1)

            @block.vector
            def _(dve):
                for i, (h, o, w) in enumerate(jobs):
                    dve.wait_ge(high, i + 1)
                    if i >= 2:
                        dve.wait_ge(low, i - 1)
                    dve.tensor_tensor(rest[:, i % 2, 0:w], src[:, h, o:o + w], part[:, i, 0, 0:w],
                                      ALU.subtract).then_inc(rested, 1)
                    dve.wait_ge(rested, i + 1)
                    dve.tensor_copy(part[:, i, 1, 0:w], rest[:, i % 2, 0:w]).then_inc(middle, 1)

            @block.gpsimd
            def _(pool):
                for i, (h, o, w) in enumerate(jobs):
                    pool.wait_ge(middle, i + 1)
                    pool.tensor_tensor(part[:, i, 2, 0:w], rest[:, i % 2, 0:w], part[:, i, 1, 0:w],
                                       ALU.subtract).then_inc(low, 1)

            @block.sync
            def _(sp):
                for i, (h, o, w) in enumerate(jobs):
                    sp.wait_ge(low, i + 1)
                    sp.dma_start(parts[:, h * P:(h + 1) * P, o:o + w].rearrange("a p n -> p a n"),
                                 part[:, i, :, 0:w]).then_inc(stored, 16)
                sp.wait_ge(stored, 16 * J)


Q_RUNS = [(0, 0, 3), (3, 0, 2), (5, 0, 1)]
K_RUNS = [(0, 0, 3), (3, 1, 2), (5, 2, 1)]


class Step:

    def __init__(self, g, o):
        self.head, self.slot, self.prior = g * 3 + o, o % 3, g + o // 3


def cross_attention(c, q_parts, k_parts, values, out_rows):
    nc = c.nc
    CHUNKS = 4
    edges = [M * i // CHUNKS for i in range(CHUNKS + 1)]
    NA = T * CHUNKS
    NB = MT * CH
    SA, SB, SP = 3, 4, 3
    LEAD = 4 * CHUNKS
    BEHIND = 2
    mrows = c.dram(c.unique("mrows"), [3, PARTS, N], BF16)
    with ExitStack() as s:
        q_sb = [c.sb(s, "q_sb", [SRM, N], BF16) for _ in range(3)]
        k_sb = [c.sb(s, "k_sb", [SRM, M], BF16) for _ in range(3)]
        v_sb = [c.sb(s, "v_sb", [P, MT, 32]) for _ in range(3)]
        a_slots = [c.ps(s, "a_score", [P, BANK]) for _ in range(SA)]
        b_slots = [c.ps(s, "b_score", [P, BANK]) for _ in range(SB)]
        sums = c.ps(s, "sums", [P, BANK])
        probs = [[c.sb(s, "probs", [P, BANK]) for _ in range(CH)] for _ in range(SP)]
        maxima = c.sb(s, "maxima", [P, T, CHUNKS])
        shift, rest = c.sb(s, "shift", [P, T]), c.sb(s, "rest", [P, T])
        part = c.sb(s, "part", [P, PARTS, 32], BF16)
        turned = [c.sb(s, "turned", [P, PARTS, 32], BF16) for _ in range(3)]
        stage = [c.sb(s, "stage", [P, BANK]) for _ in range(3)]
        loaded, shift_stored, shift_loaded, stored = ([c.sem(f"{n}{i}") for i in range(3)] for n in
                                                      ("loaded", "shift_stored", "shift_loaded", "stored"))
        a_scored, a_maxed, scored, exped, used = (c.sem(n) for n in ("a_scored", "a_maxed", "scored", "exped", "used"))
        chain, shift_ready, staged, ones_set, pad_set = (c.sem(n) for n in ("chain", "shift_ready", "staged", "ones_set", "pad_set"))
        LOADS = 2 * PAIRS + 1
        LINKS = 5
        quarter = P // 32

        def over_steps(eng, step, first, last):
            first()
            for o in range(1, 4):
                step(Step(0, o), Step(0, o - 1), Step(0, o + 1))
            with eng.Fori(1, (H - 1) // 3 - 1) as g:
                for o in range(1, 4):
                    step(Step(g, o), Step(g, o - 1), Step(g, o + 1))
            g = (H - 1) // 3 - 1
            for o in range(1, 4):
                step(Step(g, o), Step(g, o - 1), Step(g, o + 1) if o < 3 else None)
            last()

        def maxima_chunks(a, ahead):
            return [(a, n) for n in range(LEAD, NA)] + ([(ahead, n) for n in range(LEAD)] if ahead else [])

        with nc.Block() as block:
            @block.sync
            def _(sp):
                def loads(a):
                    wait(sp, used, (a.head - 2) * MT)
                    row = a.head * HD
                    for at, first, n in Q_RUNS:
                        for m in range(n):
                            sp.dma_start(q_sb[a.slot][(at + m) * HD:(at + m + 1) * HD, None, :],
                                         part_rows(q_parts, first + m, row)).then_inc(loaded[a.slot], 16)
                    for at, first, n in K_RUNS:
                        for m in range(n):
                            sp.dma_start(k_sb[a.slot][(at + m) * HD:(at + m + 1) * HD, None, :],
                                         part_rows(k_parts, first, row)).then_inc(loaded[a.slot], 16)
                    sp.dma_start(v_sb[a.slot][:, None, :, :],
                                 values[:, bass.ds(a.head, 1), :, :]).then_inc(loaded[a.slot], 16)

                def part_rows(parts, part, row):
                    return parts[part:part + 1, bass.ds(row, HD), :].rearrange("o r n -> r o n")

                def shifts(a):
                    wait(sp, shift_loaded[a.slot], a.prior * 16)
                    sp.wait_ge(shift_ready, a.head + 1)
                    rows = mrows[a.slot].rearrange("a (t b q) -> t b a q", b=quarter, q=32)
                    for b in range(quarter):
                        sp.dma_start(rows[:, b, :, :], turned[a.slot][32 * b:32 * b + T, :, :])\
                            .then_inc(shift_stored[a.slot], 16)
                    sp.wait_ge(shift_stored[a.slot], (a.prior + 1) * (16 * quarter))
                    sp.dma_start(q_sb[a.slot][SR:SRM, :], mrows[a.slot]).then_inc(shift_loaded[a.slot], 16)

                loads(Step(0, 0))
                loads(Step(0, 1))
                shifts(Step(0, 0))
                for o in range(1, 4):
                    loads(Step(0, o + 1))
                    shifts(Step(0, o))
                with sp.Fori(1, (H - 1) // 3 - 1) as g:
                    for o in range(1, 4):
                        loads(Step(g, o + 1))
                        shifts(Step(g, o))
                g = (H - 1) // 3 - 1
                for o in range(1, 4):
                    if o < 3:
                        loads(Step(g, o + 1))
                    shifts(Step(g, o))

            @block.gpsimd
            def _(pool):
                for k in range(3):
                    pool.memset(k_sb[k][SR:SRM, :], 1.0).then_inc(ones_set, 1)
                pool.wait_ge(ones_set, 3)
                pool.memset(part[:], 0.0).then_inc(pad_set, 1)

                def store(b):
                    pool.wait_ge(staged, b.head + 1)
                    pool.dma_start(out_rows[bass.ds(b.head, 1), :, :].rearrange("o p q -> (o p) q"),
                                   stage[b.slot][:]).then_inc(stored[b.slot], 16)

                over_steps(pool, lambda a, b, ahead: store(b), lambda: None, lambda: store(Step(0, H - 1)))
                for k in range(3):
                    pool.wait_ge(stored[k], 16 * len(range(k, H, 3)))

            @block.tensor
            def _(pe):
                def maxima_scores(a, n):
                    t, ch = n // CHUNKS, n % CHUNKS
                    if n == 0:
                        pe.wait_ge(loaded[a.slot], (a.prior + 1) * (16 * LOADS))
                    wait(pe, a_maxed, a.head * NA + (n - SA + 1))
                    lo, hi = edges[ch], edges[ch + 1]
                    pe.matmul(a_slots[(a.slot * NA + n) % SA][:, 0:hi - lo], q_sb[a.slot][0:SR, t * P:(t + 1) * P],
                              k_sb[a.slot][0:SR, lo:hi], start=True, stop=True).then_inc(a_scored, 1)

                def scores(b, k, j):
                    u = k * CH + j
                    n = min(P, M - k * P)
                    if u == 0:
                        pe.wait_ge(shift_loaded[b.slot], (b.prior + 1) * 16)
                    wait(pe, exped, b.head * NB + (u - SB + 1))
                    pe.matmul(b_slots[(b.slot * NB + u) % SB][0:n, :], k_sb[b.slot][0:SRM, k * P:k * P + n],
                              q_sb[b.slot][0:SRM, j * BANK:(j + 1) * BANK], start=True, stop=True).then_inc(scored, 1)

                def add_up(b, k):
                    n = min(P, M - k * P)
                    if k == 0:
                        wait(pe, staged, b.head)
                    for j in range(CH):
                        pe.wait_ge(exped, b.head * NB + (k * CH + j + 1))
                        last = pe.matmul(sums[32 * j:32 * j + 32, :], v_sb[b.slot][0:n, k, :],
                                         probs[(b.slot * MT + k) % SP][j][0:n, :], start=(k == 0), stop=(k == MT - 1),
                                         skip_group_check=True)
                    last.then_inc(used, 1)

                events = []
                for k in range(MT):
                    for j in range(CH):
                        events.append(("s", k, j))
                    if k >= BEHIND:
                        events.append(("p", k - BEHIND, 0))
                events += [("p", k, 0) for k in range(MT - BEHIND, MT)]

                def step(a, b, ahead):
                    chunks = maxima_chunks(a, ahead) if a else []
                    done = 0
                    for e, (what, k, j) in enumerate(events):
                        due = len(chunks) * (e + 1) // len(events)
                        for head, n in chunks[done:due]:
                            maxima_scores(head, n)
                        done = due
                        if what == "s":
                            scores(b, k, j)
                        else:
                            add_up(b, k)

                def first():
                    pe.wait_ge(ones_set, 3)
                    for n in range(LEAD):
                        maxima_scores(Step(0, 0), n)
                    for head, n in maxima_chunks(Step(0, 0), Step(0, 1)):
                        maxima_scores(head, n)

                over_steps(pe, step, first, lambda: step(None, Step(0, H - 1), None))

            @block.scalar
            def _(act):
                def exps(b):
                    for u in range(NB):
                        k, j = u // CH, u % CH
                        n = min(P, M - k * P)
                        act.wait_ge(scored, b.head * NB + (u + 1))
                        wait(act, used, b.head * MT + (k - SP + 1))
                        nc.scalar.activation(probs[(b.slot * MT + k) % SP][j][0:n, :], b_slots[(b.slot * NB + u) % SB][0:n, :],
                                             ACT.Exp).then_inc(exped, 1)

                over_steps(act, lambda a, b, ahead: exps(b), lambda: None, lambda: exps(Step(0, H - 1)))

            @block.vector
            def _(dve):
                def maximum(a, n):
                    t, ch = n // CHUNKS, n % CHUNKS
                    dve.wait_ge(a_scored, a.head * NA + (n + 1))
                    w = edges[ch + 1] - edges[ch]
                    dve.tensor_reduce(maxima[:, t, ch:ch + 1], a_slots[(a.slot * NA + n) % SA][:, 0:w], X, ALU.max).then_inc(a_maxed, 1)

                def negate_and_split(a):
                    at = [0]

                    def link(ins):
                        at[0] += 1
                        ins.then_inc(chain, 1)
                        dve.wait_ge(chain, a.head * LINKS + at[0])

                    dve.wait_ge(a_maxed, a.head * NA + NA)
                    link(dve.tensor_reduce(shift[:], maxima[:], X, ALU.max, negate=True))
                    link(dve.tensor_copy(part[:, 0, 0:T], shift[:]))
                    link(dve.tensor_tensor(rest[:], shift[:], part[:, 0, 0:T], ALU.subtract))
                    link(dve.tensor_copy(part[:, 1, 0:T], rest[:]))
                    link(dve.tensor_tensor(part[:, 2, 0:T], rest[:], part[:, 1, 0:T], ALU.subtract))
                    wait(dve, shift_stored[a.slot], a.prior * (16 * quarter))
                    dve.transpose(turned[a.slot][:].rearrange("p a q -> p (a q)"),
                                  part[:].rearrange("p a q -> p (a q)")).then_inc(shift_ready, 1)

                def evacuate(b):
                    dve.wait_ge(used, b.head * MT + MT)
                    wait(dve, stored[b.slot], b.prior * 16)
                    dve.tensor_copy(stage[b.slot][:], sums[:]).then_inc(staged, 1)

                def step(a, b, ahead):
                    for head, n in maxima_chunks(a, ahead):
                        maximum(head, n)
                        if head is a and n == NA - 1:
                            negate_and_split(a)
                    if b:
                        evacuate(b)

                def first():
                    dve.wait_ge(pad_set, 1)
                    for n in range(LEAD):
                        maximum(Step(0, 0), n)
                    step(Step(0, 0), None, Step(0, 1))

                over_steps(dve, step, first, lambda: evacuate(Step(0, H - 1)))


def attention_output(c, sums, w, bias):
    nc = c.nc
    with ExitStack() as s:
        oT = c.sb(s, "oT", [P, DT, N])
        totals = c.sb(s, "totals", [P, DT, N])
        load_heads(c, sums, oT, totals=totals)
        inverse, weighted = c.sem("inverse"), c.sem("weighted")
        with nc.Block() as block:
            @block.vector
            def _(dve):
                dve.reciprocal(totals[:], totals[:]).then_inc(inverse, 1)
                dve.wait_ge(inverse, 1)
                dve.tensor_tensor(oT[:], oT[:], totals[:], ALU.mult).then_inc(weighted, 1)
                dve.wait_ge(weighted, 1)
        project_tokens(c, oT, w, bias, D, T, N, c.x, residual=c.x)


def values_with_ones(c, v, out, tiles):
    nc = c.nc
    filled, placed = c.sem("filled"), c.sem("placed")
    with nc.Block() as block:
        @block.vector
        def _(dve):
            dve.memset(out[:, :, :, HD:2 * HD], 1.0).then_inc(filled, 1)
            dve.tensor_copy(out[:, :, :, 0:HD], v[:].rearrange("p t (h e) -> p h t e", e=HD)).then_inc(placed, 1)
            dve.wait_ge(filled, 1)
            dve.wait_ge(placed, 1)


def zero(c, buf):
    nc = c.nc
    zeroed = c.sem("zeroed")
    with nc.Block() as block:
        @block.gpsimd
        def _(pool):
            pool.memset(buf, 0.0).then_inc(zeroed, 1)
            pool.wait_ge(zeroed, 1)


def by_feature(dst, v):
    return [(dst[:, h:h + 1], v.rearrange("(h p o) -> h p o", p=P, o=1)[h]) for h in range(DT)]


def cross_layer(c, name, ctx_in, ws, bs, transposed):
    nc = c.nc
    q_parts = c.dram(f"{name}_q_parts", [PARTS, D, N], BF16)
    k_parts = c.dram(f"{name}_k_parts", [PARTS, D, M], BF16)
    sums = c.dram(f"{name}_sums", [H, P, BANK])
    with ExitStack() as s:
        w_sb = [c.sb(s, n, [P, DT, D]) for n in ("wq", "wk", "wv", "wo")]
        bq, bk = c.sb(s, "bq", [P, DT]), c.sb(s, "bk", [P, DT])
        bv, bo = c.sb(s, "bv", [P, D]), c.sb(s, "bo", [P, D])
        jobs = by_feature(bq, bs[0]) + by_feature(bk, bs[1]) + [(bv[:], row_of(bs[2], D)), (bo[:], row_of(bs[3], D))]
        if transposed:
            with ExitStack() as s1:
                raw = [c.sb(s1, "raw", [P, DT, D]) for _ in range(4)]
                load(c, [(r[:], w.rearrange("(k p) n -> p k n", p=P)) for r, w in zip(raw, ws)] + jobs)
                for r, w in zip(raw, w_sb):
                    transpose_tiles(c, r, w, tiles=DT, rows=D)
        else:
            load(c, [(r[:], w.rearrange("(k p) n -> p k n", p=P)) for r, w in zip(w_sb, ws)] + jobs)
        values = c.sb(s, "values", [P, H, MT, 32])
        with ExitStack() as s1:
            ctxT = c.sb(s1, "ctxT", [P, DT, M])
            with ExitStack() as s2:
                ctx = c.sb(s2, "ctx", [P, MT, D])
                full = (MT - 1) * P
                load(c, [(ctx[:, 0:MT - 1, :], ctx_in[0, 0:full, :].rearrange("(t p) d -> p t d", p=P)),
                         (ctx[0:M - full, MT - 1, :], ctx_in[0, full:M, :])])
                transpose_tiles(c, ctx, ctxT, tiles=MT, rows=M)
            with ExitStack() as s2:
                v = c.sb(s2, "v", [P, MT, D])
                zero(c, v[:])
                project_tokens(c, ctxT, w_sb[2], bv, D, MT, M, v)
                values_with_ones(c, v, values, MT)
            with ExitStack() as s2:
                kT = c.sb(s2, "kT", [P, DT, M])
                project_features(c, w_sb[1], ctxT, bk, M, kT)
                split_to_dram(c, kT, M, k_parts)
        with ExitStack() as s1:
            hT = c.sb(s1, "hT", [P, DT, N])
            with ExitStack() as s2:
                h = c.sb(s2, "h", [P, T, D])
                layernorm(c, c.x, h)
                transpose_tiles(c, h, hT)
            qT = c.sb(s1, "qT", [P, DT, N])
            project_features(c, w_sb[0], hT, bq, N, qT, scale=HD ** -0.5)
            split_to_dram(c, qT, N, q_parts)
        cross_attention(c, q_parts, k_parts, values, sums)
        attention_output(c, sums, w_sb[3], bo)


E = 8
HID = 1024
MH = HID // P
CAP = int(N / E * 1.25)
ST = (CAP + P - 1) // P


def route(c, gates, scatter_at, gather_at, weight):
    nc = c.nc
    with ExitStack() as s:
        best = c.sb(s, "best", [P, T, 8])
        index = c.sb(s, "index", [P, T, 8], U32)
        number_i, number = c.sb(s, "number_i", [P, E], I32), c.sb(s, "number", [P, E])
        token_i, token = c.sb(s, "token_i", [P, T], I32), c.sb(s, "token", [P, T])
        which = [c.sb(s, "which", [P, T]) for _ in range(2)]
        chosen = [c.sb(s, "chosen", [P, T, E]) for _ in range(2)]
        label = c.sb(s, "label", [P, T, E], BF16)
        before = c.sb(s, "before", [P, T, E])
        place = c.sb(s, "place", [P, T, E])
        masked = c.sb(s, "masked", [P, T, E])
        seat, fits, row, back = (c.sb(s, n, [P, T]) for n in ("seat", "fits", "row", "back"))
        gap, ratio, one = (c.sb(s, n, [P, T]) for n in ("gap", "ratio", "one"))
        counts = c.ps(s, "counts", [P, T, E])
        totals = c.ps(s, "totals", [P, T, E])
        chain, numbered, labelled, counted = (c.sem(n) for n in ("chain", "numbered", "labelled", "counted"))
        gap_ready, ratio_ready, topped = c.sem("gap_ready"), c.sem("ratio_ready"), c.sem("topped")
        spread = lambda a: a[:, :, None].to_broadcast([P, T, E])
        with nc.Block() as block:
            @block.gpsimd
            def _(pool):
                pool.iota(number_i[:], pattern=[[1, E]], base=0, channel_multiplier=0).then_inc(numbered, 1)
                pool.iota(token_i[:], pattern=[[P, T]], base=0, channel_multiplier=1).then_inc(numbered, 1)

            @block.tensor
            def _(pe):
                pe.wait_ge(labelled, 1)
                pe.matmul(counts[:], c.triu[:], label[:], start=True, stop=True)
                pe.matmul(totals[:], c.onesb[:], label[:], start=True, stop=True).then_inc(counted, 1)

            @block.scalar
            def _(act):
                act.wait_ge(gap_ready, 1)
                nc.scalar.activation(ratio[:], gap[:], ACT.Exp).then_inc(ratio_ready, 1)

            @block.vector
            def _(dve):
                line = Line(dve, chain)
                for t in range(T):
                    dve.max(best[:, t, :], gates[:, t, :]).then_inc(topped, 1)
                for t in range(T):
                    dve.wait_ge(topped, t + 1)
                    last = dve.max_index(index[:, t, :], best[:, t, :], gates[:, t, :])
                line(last)
                dve.tensor_tensor(gap[:], best[:, :, 1], best[:, :, 0], ALU.subtract).then_inc(gap_ready, 1)
                dve.wait_ge(numbered, 2)
                line(dve.tensor_copy(number[:], number_i[:]))
                line(dve.tensor_copy(token[:], token_i[:]))
                for k in range(2):
                    line(dve.tensor_copy(which[k][:], index[:, :, k]))
                    line(dve.tensor_tensor(chosen[k][:], number[:, None, :].to_broadcast([P, T, E]), spread(which[k]),
                                           ALU.is_equal))
                dve.tensor_tensor(label[:], chosen[0][:], chosen[1][:], ALU.add).then_inc(labelled, 1)
                line(dve.memset(before[:, 0, :], 0.0))
                dve.wait_ge(counted, 1)
                for t in range(1, T):
                    line(dve.tensor_tensor(before[:, t, :], before[:, t - 1, :], totals[:, t - 1, :], ALU.add))
                line(dve.tensor_tensor(place[:], counts[:], before[:], ALU.add))
                for k in range(2):
                    line(dve.tensor_tensor(masked[:], place[:], chosen[k][:], ALU.mult))
                    line(dve.tensor_reduce(seat[:], masked[:], X, ALU.add))
                    line(dve.tensor_scalar(fits[:], seat[:], float(CAP), None, ALU.is_le))
                    line(dve.scalar_tensor_tensor(row[:], which[k][:], float(CAP), seat[:], ALU.mult, ALU.add))
                    line(dve.tensor_scalar(back[:], token[:], float(E * CAP + k * N), None, ALU.add))
                    line(dve.scalar_tensor_tensor(row[:], row[:], -1.0, back[:], ALU.add, ALU.subtract))
                    line(dve.tensor_tensor(row[:], row[:], fits[:], ALU.mult))
                    line(dve.tensor_tensor(scatter_at[k][:], row[:], back[:], ALU.add))
                    line(dve.tensor_tensor(row[:], row[:], back[:], ALU.add))
                    line(dve.tensor_scalar(row[:], row[:], float(E * CAP), None, ALU.min))
                    line(dve.tensor_copy(gather_at[k][:], row[:]))
                dve.wait_ge(ratio_ready, 1)
                line(dve.tensor_scalar(one[:], ratio[:], 1.0, None, ALU.add))
                line(dve.reciprocal(weight[0][:], one[:]))
                line(dve.tensor_tensor(weight[1][:], ratio[:], weight[0][:], ALU.mult))


def indirect(c, jobs):
    nc = c.nc
    moved = c.sem("moved")
    with nc.Block() as block:
        @block.gpsimd
        def _(pool):
            for scatter, a, rows, b in jobs:
                at = bass.IndirectOffsetOnAxis(ap=rows, axis=0)
                pool.indirect_dma_start(out=a, out_offset=at if scatter else None, in_=b,
                                        in_offset=None if scatter else at).then_inc(moved, 16)
            pool.wait_ge(moved, 16 * len(jobs))


def experts(c, slots_in, w1, w2, w3, slots_out):
    nc = c.nc
    full = CAP // P
    part = CAP - full * P
    sizes = [min(P, CAP - i * P) for i in range(ST)]
    with ExitStack() as s:
        w1_sb = [c.sb(s, "w1", [P, DT, HID]) for _ in range(2)]
        w2_sb = [c.sb(s, "w2", [P, DT, HID]) for _ in range(2)]
        w3_sb = [c.sb(s, "w3", [P, MH, D]) for _ in range(2)]
        rows = [c.sb(s, "rows", [P, ST, D]) for _ in range(2)]
        rowsT = [c.sb(s, "rowsT", [P, DT, CAP]) for _ in range(2)]
        tanh = [c.sb(s, "tanh", [P, CAP]) for _ in range(2)]
        gate = [c.sb(s, "gate", [P, CAP]) for _ in range(2)]
        hidden = [c.sb(s, "hidden", [P, MH, CAP]) for _ in range(2)]
        out_sb = [c.sb(s, "out", [P, ST, D]) for _ in range(2)]
        turn_ps = [c.ps(s, "turn", [P, BANK]) for _ in range(2)]
        a_ps = [c.ps(s, "a", [P, BANK]) for _ in range(2)]
        b_ps = [c.ps(s, "b", [P, BANK]) for _ in range(2)]
        out_ps = [c.ps(s, "outp", [P, BANK]) for _ in range(2)]
        loaded = [c.sem("loaded0"), c.sem("loaded1")]
        stored = [c.sem("stored0"), c.sem("stored1")]
        turned, placed, multiplied, tanhed, gated, joined, summed, copied = (
            c.sem(n) for n in ("turned", "placed", "multiplied", "tanhed", "gated", "joined", "summed", "copied"))
        LOADS = 3 + 1 + (part > 0)

        def pairs(eng, step):
            for par in range(2):
                step(0, par)
            with eng.Fori(1, E // 2 - 1) as g:
                for par in range(2):
                    step(g, par)
            for par in range(2):
                step(E // 2 - 1, par)

        with nc.Block() as block:
            @block.sync
            def _(sp):
                def loads(g, par):
                    e = g * 2 + par
                    wait(sp, summed, (e - 1) * ST)
                    sp.dma_start(rows[par][:, 0:full, :],
                                 slots_in[bass.ds(e * CAP, full * P), :].rearrange("(t p) d -> p t d", p=P))\
                        .then_inc(loaded[par], 16)
                    if part:
                        sp.dma_start(rows[par][0:part, full, :],
                                     slots_in[bass.ds(e * CAP + full * P, part), :]).then_inc(loaded[par], 16)
                    for dst, w, n in ((w1_sb, w1, DT), (w2_sb, w2, DT), (w3_sb, w3, MH)):
                        sp.dma_start(dst[par][:, :, :],
                                     w[bass.ds(e, 1), :, :].rearrange("o (k p) n -> p (o k) n", p=P))\
                            .then_inc(loaded[par], 16)

                pairs(sp, loads)

            @block.gpsimd
            def _(pool):
                def store(g, par):
                    e = g * 2 + par
                    pool.wait_ge(copied, (e + 1) * ST)
                    pool.dma_start(slots_out[bass.ds(e * CAP, full * P), :].rearrange("(t p) d -> p t d", p=P),
                                   out_sb[par][:, 0:full, :]).then_inc(stored[par], 16)
                    if part:
                        pool.dma_start(slots_out[bass.ds(e * CAP + full * P, part), :],
                                       out_sb[par][0:part, full, :]).then_inc(stored[par], 16)

                pairs(pool, store)
                for par in range(2):
                    pool.wait_ge(stored[par], 16 * (E // 2) * (1 + (part > 0)))

            @block.tensor
            def _(pe):
                def turn(g, par):
                    e = g * 2 + par
                    pe.wait_ge(loaded[par], (g + 1) * (16 * LOADS))
                    for h in range(DT):
                        wait(pe, placed, e * DT + (h - 1))
                        for i, n in enumerate(sizes):
                            last = pe.transpose(turn_ps[h % 2][:, i * P:i * P + n], rows[par][0:n, i, h * P:(h + 1) * P],
                                                c.identf[0:n, 0:n])
                        last.then_inc(turned, 1)

                def widen(g, par):
                    e = g * 2 + par
                    pe.wait_ge(placed, (e + 1) * DT)
                    for m in range(MH):
                        wait(pe, joined, e * MH + (m - 1))
                        for ps, w in ((a_ps, w1_sb), (b_ps, w2_sb)):
                            for k in range(DT):
                                last = pe.matmul(ps[m % 2][:, 0:CAP], w[par][:, k, m * P:(m + 1) * P],
                                                 rowsT[par][:, k, :], start=(k == 0), stop=(k == DT - 1))
                        last.then_inc(multiplied, 1)

                def narrow(g, par):
                    e = g * 2 + par
                    pe.wait_ge(joined, (e + 1) * MH)
                    for i, n in enumerate(sizes):
                        wait(pe, copied, e * ST + (i - 1))
                        for m in range(MH):
                            last = pe.matmul(out_ps[(par * ST + i) % 2][0:n, 0:D], hidden[par][:, m, i * P:i * P + n],
                                             w3_sb[par][:, m, :], start=(m == 0), stop=(m == MH - 1))
                        last.then_inc(summed, 1)

                def step(g, par):
                    widen(g, par)
                    if not (isinstance(g, int) and g * 2 + par == E - 1):
                        turn(g + par, 1 - par)
                    narrow(g, par)

                turn(0, 0)
                pairs(pe, step)

            @block.scalar
            def _(act):
                def step(g, par):
                    e = g * 2 + par
                    for m in range(MH):
                        act.wait_ge(multiplied, e * MH + (m + 1))
                        wait(act, gated, e * MH + (m - 1))
                        nc.scalar.activation(tanh[m % 2][:], a_ps[m % 2][:, 0:CAP], ACT.Tanh, scale=0.5)\
                            .then_inc(tanhed, 1)
                    for i, n in enumerate(sizes):
                        act.wait_ge(summed, e * ST + (i + 1))
                        if i == 0:
                            wait(act, stored[par], g * (16 * (1 + (part > 0))))
                        nc.scalar.activation(out_sb[par][0:n, i, :], out_ps[(par * ST + i) % 2][0:n, 0:D], ACT.Copy)\
                            .then_inc(copied, 1)

                pairs(act, step)

            @block.vector
            def _(dve):
                def place(g, par):
                    e = g * 2 + par
                    for h in range(DT):
                        dve.wait_ge(turned, e * DT + (h + 1))
                        dve.tensor_copy(rowsT[par][:, h, :], turn_ps[h % 2][:, 0:CAP]).then_inc(placed, 1)

                def step(g, par):
                    e = g * 2 + par
                    for m in range(MH):
                        dve.wait_ge(tanhed, e * MH + (m + 1))
                        wait(dve, joined, e * MH + (m - 1))
                        dve.scalar_tensor_tensor(gate[m % 2][:], tanh[m % 2][:], 1.0, a_ps[m % 2][:, 0:CAP],
                                                 ALU.add, ALU.mult).then_inc(gated, 1)
                        dve.wait_ge(gated, e * MH + (m + 1))
                        if m == 0:
                            wait(dve, summed, (e - 1) * ST)
                        dve.scalar_tensor_tensor(hidden[par][:, m, :], gate[m % 2][:], 0.5, b_ps[m % 2][:, 0:CAP],
                                                 ALU.mult, ALU.mult).then_inc(joined, 1)
                    if not (isinstance(g, int) and e == E - 1):
                        place(g + par, 1 - par)

                place(0, 0)
                pairs(dve, step)


def expert_layer(c, wg, bg, w1, w2, w3):
    nc = c.nc
    slots_in = c.dram("slots_in", [E * CAP + 2 * N, D])
    slots_out = c.dram("slots_out", [E * CAP + 1, D])
    with ExitStack() as s:
        scatter_at = [c.sb(s, "scatter_at", [P, T], U32) for _ in range(2)]
        gather_at = [c.sb(s, "gather_at", [P, T], U32) for _ in range(2)]
        weight = [c.sb(s, "weight", [P, T]) for _ in range(2)]
        with ExitStack() as s1:
            h = c.sb(s1, "h", [P, T, D])
            hT = c.sb(s1, "hT", [P, DT, N])
            wg_sb, bg_sb = c.sb(s1, "wg", [P, DT, E]), c.sb(s1, "bg", [P, E])
            gates = c.sb(s1, "gates", [P, T, E])
            zeros = c.sb(s1, "zeros", [P, E * CAP // P, D])
            zero(c, zeros[:])
            load(c, [(wg_sb[:], wg.rearrange("(k p) n -> p k n", p=P)), (bg_sb[:], row_of(bg, E)),
                     (slots_in[0:E * CAP, :].rearrange("(t p) d -> p t d", p=P), zeros[:]),
                     (slots_out[E * CAP:E * CAP + 1, :], zeros[0:1, 0, :])])
            layernorm(c, c.x, h)
            transpose_tiles(c, h, hT)
            project_tokens(c, hT, wg_sb, bg_sb, E, T, N, gates)
            route(c, gates, scatter_at, gather_at, weight)
            indirect(c, [(True, slots_in, scatter_at[k][:, t:t + 1], h[:, t, :]) for t in range(T) for k in range(2)])
        experts(c, slots_in, w1, w2, w3, slots_out)
        with ExitStack() as s1:
            y = [c.sb(s1, "y", [P, T, D]) for _ in range(2)]
            indirect(c, [(False, y[k][:, t, :], gather_at[k][:, t:t + 1], slots_out) for t in range(T) for k in range(2)])
            added = c.sem("added")
            with nc.Block() as block:
                @block.vector
                def _(dve):
                    for k in range(2):
                        for t in range(T):
                            if k:
                                dve.wait_ge(added, t + 1)
                            dve.scalar_tensor_tensor(c.x[:, t, :], y[k][:, t, :], weight[k][:, t:t + 1], c.x[:, t, :],
                                                     ALU.mult, ALU.add).then_inc(added, 1)


def load_pairs(eng, q_dst, k_dst, q_parts, k_parts, row, cols, sem):
    for dst, parts, runs, step, n_cols in ((q_dst, q_parts, Q_RUNS, 1, N), (k_dst, k_parts, K_RUNS, 0, cols)):
        for at, first, n in runs:
            for m in range(n):
                part = first + m * step
                eng.dma_start(dst[(at + m) * HD:(at + m + 1) * HD, None, :],
                              parts[part:part + 1, bass.ds(row, HD), :].rearrange("o r n -> r o n")).then_inc(sem, 16)


WIN = 2 * P


def window_maxima(c, q_parts, k_parts, shift):
    nc = c.nc
    GT = N // WIN
    G = T // GT
    with ExitStack() as s:
        q_sb = [c.sb(s, "q_sb", [SR, N], BF16) for _ in range(2)]
        k_sb = [c.sb(s, "k_sb", [SR, N], BF16) for _ in range(2)]
        slots = [c.ps(s, "score", [P, GT, WIN]) for _ in range(2)]
        loaded = [c.sem("loaded0"), c.sem("loaded1")]
        scored, maxed = c.sem("scored"), c.sem("maxed")
        with nc.Block() as block:
            @block.sync
            def _(sp):
                def loads(head, par, products):
                    wait(sp, scored, products)
                    load_pairs(sp, q_sb[par], k_sb[par], q_parts, k_parts, head * HD, N, loaded[par])

                loads(0, 0, 0)
                loads(1, 1, 0)
                with sp.Fori(0, H // 2 - 1) as g:
                    for par in range(2):
                        loads(g * 2 + (2 + par), par, g * (2 * G) + G * (par + 1))

            @block.tensor
            def _(pe):
                with pe.Fori(0, H // 2) as g:
                    for par in range(2):
                        pe.wait_ge(loaded[par], (g + 1) * (16 * 2 * PAIRS))
                        for i in range(G):
                            n = par * G + i
                            pe.wait_ge(maxed, g * (2 * G) + (n + 1))
                            for t in range(GT * i, GT * (i + 1)):
                                o = slots[n % 2][:, t - GT * i, :]
                                still = q_sb[par][:, t * P:(t + 1) * P]
                                if t:
                                    pe.matmul(o, still, k_sb[par][:, (t - 1) * P:(t + 1) * P], start=True, stop=False)
                                    last = pe.matmul(o, c.identb[:], c.mask_qk[:], start=False, stop=True)
                                else:
                                    pe.matmul(o, c.identb[:], c.mask_first[:], start=True, stop=False)
                                    last = pe.matmul(o[:, P:2 * P], still, k_sb[par][:, 0:P], start=False, stop=True)
                            last.then_inc(scored, 1)

            @block.vector
            def _(dve):
                dve.sem_inc(maxed, 2)
                with dve.Fori(0, H // 2) as g:
                    for par in range(2):
                        for i in range(G):
                            n = par * G + i
                            dve.wait_ge(scored, g * (2 * G) + (n + 1))
                            dve.tensor_reduce(shift[:, bass.ds(g * (2 * T) + n * GT, GT)], slots[n % 2][:], X, ALU.max,
                                              negate=True).then_inc(maxed, 1)


def window_weights(c, q_parts, k_parts, shift_rows, values, out_rows):
    nc = c.nc
    KT = 4
    U, LAG, S = T // KT, 2, 2
    HEAD_PAIRS = H // 2
    LOADS = 2 * PAIRS + 2
    with ExitStack() as s:
        q_sb = [c.sb(s, "q_sb", [SRM, N], BF16) for _ in range(2)]
        k_sb = [c.sb(s, "k_sb", [SRM, N], BF16) for _ in range(2)]
        v_sb = [c.sb(s, "v_sb", [P, T, 32]) for _ in range(2)]
        slots = [c.ps(s, "score", [P, KT, WIN]) for _ in range(S)]
        sums = [c.ps(s, "sums", [P, BANK]) for _ in range(2)]
        probs = [c.sb(s, "probs", [P, KT, WIN]) for _ in range(S)]
        stage = [c.sb(s, "stage", [P, BANK]) for _ in range(2)]
        loaded = [c.sem("loaded0"), c.sem("loaded1")]
        stored = [c.sem("stored0"), c.sem("stored1")]
        scored, exped, used, staged, ones_set = (c.sem(n) for n in ("scored", "exped", "used", "staged", "ones_set"))

        def pairs(eng, pair):
            pair(0, False)
            with eng.Fori(1, HEAD_PAIRS - 1) as g:
                pair(g, False)
            pair(HEAD_PAIRS - 1, True)

        with nc.Block() as block:
            @block.sync
            def _(sp):
                def loads(head, par, products):
                    wait(sp, used, products)
                    load_pairs(sp, q_sb[par], k_sb[par], q_parts, k_parts, head * HD, N, loaded[par])
                    sp.dma_start(q_sb[par][SR:SRM, None, :], shift_rows[:, bass.ds(head, 1), :]).then_inc(loaded[par], 16)
                    sp.dma_start(v_sb[par][:, None, :, :], values[:, bass.ds(head, 1), :, :]).then_inc(loaded[par], 16)

                loads(0, 0, 0)
                loads(1, 1, 0)
                with sp.Fori(0, HEAD_PAIRS - 1) as g:
                    for par in range(2):
                        loads(g * 2 + (2 + par), par, g * (2 * U) + U * (par + 1))

            @block.gpsimd
            def _(pool):
                for par in range(2):
                    pool.memset(k_sb[par][SR:SRM, :], 1.0).then_inc(ones_set, 1)

                def pair(g, last):
                    for par in range(2):
                        pool.wait_ge(staged, g * 2 + (par + 1))
                        pool.dma_start(out_rows[bass.ds(g * 2 + par, 1), :, :].rearrange("o p q -> (o p) q"),
                                       stage[par][:]).then_inc(stored[par], 16)

                pairs(pool, pair)
                for par in range(2):
                    pool.wait_ge(stored[par], 16 * HEAD_PAIRS)

            @block.tensor
            def _(pe):
                def score(g, i):
                    par, u, slot = i // U % 2, i % U, i % S
                    if u == 0:
                        pe.wait_ge(loaded[par], (g + (i // U // 2 + 1)) * (16 * LOADS))
                    wait(pe, exped, g * (2 * U) + (i - S + 1))
                    for k in range(KT * u, KT * (u + 1)):
                        w = min(WIN, N - k * P)
                        o = slots[slot][:, k - KT * u, 0:w]
                        pe.matmul(o, k_sb[par][:, k * P:(k + 1) * P], q_sb[par][:, k * P:k * P + w],
                                  start=True, stop=False)
                        last = pe.matmul(o, c.identb[:], c.mask_kq[:, 0:w], start=False, stop=True)
                    last.then_inc(scored, 1)

                def add_up(g, i):
                    par, u, slot = i // U, i % U, i % S
                    pe.wait_ge(exped, g * (2 * U) + (i + 1))
                    if u == 0:
                        wait(pe, staged, g * 2 + (par - 1))
                    for k in range(KT * u, KT * (u + 1)):
                        for t in (k, k + 1):
                            if t == T:
                                continue
                            j, o = t // CH, t % CH * P
                            last = pe.matmul(sums[par][32 * j:32 * j + 32, o:o + P], v_sb[par][:, k, :],
                                             probs[slot][:, k - KT * u, (t - k) * P:(t - k + 1) * P],
                                             start=(k == 0 and t == 0) or (k + 1 == t and t % CH == 0),
                                             stop=(t == k), skip_group_check=True)
                    last.then_inc(used, 1)

                def pair(g, last):
                    for i in range(2 * U):
                        if not last or i + LAG < 2 * U:
                            score(g, i + LAG)
                        add_up(g, i)

                pe.wait_ge(ones_set, 2)
                for i in range(LAG):
                    score(0, i)
                pairs(pe, pair)

            @block.scalar
            def _(act):
                def pair(g, last):
                    for i in range(2 * U):
                        u, slot = i % U, i % S
                        act.wait_ge(scored, g * (2 * U) + (i + 1))
                        wait(act, used, g * (2 * U) + (i - S + 1))
                        end = KT * WIN - (P if u == U - 1 else 0)
                        flat = lambda a: a[:].rearrange("p k w -> p (k w)")[:, 0:end]
                        nc.scalar.activation(flat(probs[slot]), flat(slots[slot]), ACT.Exp).then_inc(exped, 1)

                pairs(act, pair)

            @block.vector
            def _(dve):
                def pair(g, last):
                    for par in range(2):
                        dve.wait_ge(used, g * (2 * U) + U * (par + 1))
                        wait(dve, stored[par], g * 16)
                        dve.tensor_copy(stage[par][:], sums[par][:]).then_inc(staged, 1)

                pairs(dve, pair)


def head_norm(c, a, gamma, beta, fold):
    nc = c.nc
    HT = H * T
    with ExitStack() as s:
        mean, var, root = (c.sb(s, n, [P, HT]) for n in ("mean", "var", "root"))
        square = c.sb(s, "square", [P, T, D])
        chain, centred, squared, var_ready, root_ready = (c.sem(n) for n in ("chain", "centred", "squared", "var_ready", "root_ready"))
        by_head = lambda x: x[:, :, :].rearrange("p t (h e) -> p (t h) e", e=HD)
        over = lambda x: x[:, :, None].to_broadcast([P, HT, HD])
        rows = lambda x: x[:, None, :].to_broadcast([P, T, D])
        with nc.Block() as block:
            @block.vector
            def _(dve):
                line = Line(dve, chain)
                line(dve.tensor_reduce(mean[:], by_head(a), X, ALU.add))
                line(dve.tensor_scalar(mean[:], mean[:], -1.0 / HD, None, ALU.mult))
                dve.tensor_tensor(by_head(a), by_head(a), over(mean), ALU.add).then_inc(centred, 1)
                dve.wait_ge(squared, 1)
                line(dve.tensor_reduce(var[:], by_head(square), X, ALU.add))
                dve.tensor_scalar(var[:], var[:], 1.0 / HD, None, ALU.mult).then_inc(var_ready, 1)
                dve.wait_ge(root_ready, 1)
                line(dve.reciprocal(root[:], root[:]))
                line(dve.tensor_scalar(gamma[:], gamma[:], fold, None, ALU.mult))
                line(dve.tensor_scalar(beta[:], beta[:], fold, None, ALU.mult))
                line(dve.tensor_tensor(by_head(a), by_head(a), over(root), ALU.mult))
                line(dve.tensor_tensor(a[:, :, :], a[:, :, :], rows(gamma), ALU.mult))
                line(dve.tensor_tensor(a[:, :, :], a[:, :, :], rows(beta), ALU.add))

            @block.scalar
            def _(act):
                act.wait_ge(centred, 1)
                nc.scalar.activation(square[:], a[:, :, :], ACT.Square).then_inc(squared, 1)
                act.wait_ge(var_ready, 1)
                nc.scalar.activation(root[:], var[:], ACT.Sqrt, bias=c.eps[:, 0:1]).then_inc(root_ready, 1)


def per_head_row(v):
    return v.rearrange("(o h e) -> o h e", o=1, h=1).to_broadcast([P, H, HD])


def window_layer(c, w_qkv, b_qkv, q_gamma, q_beta, k_gamma, k_beta, w_out, b_out):
    nc = c.nc
    q_parts = c.dram("w_q_parts", [PARTS, D, N], BF16)
    k_parts = c.dram("w_k_parts", [PARTS, D, N], BF16)
    shift_rows = c.dram("w_shift_rows", [PARTS, H, N], BF16)
    sums = c.dram("w_sums", [H, P, BANK])
    with ExitStack() as s:
        wo, bo = c.sb(s, "wo", [P, DT, D]), c.sb(s, "bo", [P, D])
        values = c.sb(s, "values", [P, H, T, 32])
        with ExitStack() as s1:
            w, b = c.sb(s1, "w", [P, DT, 3 * D]), c.sb(s1, "b", [P, 3 * D])
            affine = [c.sb(s1, "affine", [P, D]) for _ in range(4)]
            load(c, [(w[:], w_qkv.rearrange("(k p) n -> p k n", p=P)), (b[:], row_of(b_qkv, 3 * D)),
                     (wo[:], w_out.rearrange("(k p) n -> p k n", p=P)), (bo[:], row_of(b_out, D))] +
                 [(a[:].rearrange("p (h e) -> p h e", e=HD), per_head_row(v))
                  for a, v in zip(affine, (q_gamma, q_beta, k_gamma, k_beta))])
            qk = [c.sb(s1, n, [P, T, D]) for n in ("q", "k")]
            with ExitStack() as s2:
                hT = c.sb(s2, "hT", [P, DT, N])
                v = c.sb(s2, "v", [P, T, D])
                layernorm(c, c.x, v)
                transpose_tiles(c, v, hT)
                for i, dst in enumerate((*qk, v)):
                    project_tokens(c, hT, w[:, :, i * D:(i + 1) * D], b[:, i * D:(i + 1) * D], D, T, N, dst)
                values_with_ones(c, v, values, T)
            for i, parts in enumerate((q_parts, k_parts)):
                with ExitStack() as s2:
                    head_norm(c, qk[i], affine[2 * i], affine[2 * i + 1], (HD ** -0.5, 1.0)[i])
                    turned = c.sb(s2, "turned", [P, DT, N])
                    transpose_tiles(c, qk[i], turned)
                    split_to_dram(c, turned, N, parts)
        shift = c.sb(s, "shift", [P, H * T])
        window_maxima(c, q_parts, k_parts, shift)
        split_rows(c, shift[:], [shift_rows[i] for i in range(PARTS)])
        window_weights(c, q_parts, k_parts, shift_rows, values, sums)
        attention_output(c, sums, wo, bo)


NE = 64
NP = 32
SL = NE * NP
SLT = SL // P
SPT = P // NP
LOW_CLIP, HIGH_CLIP = -33000.0, 65000.0


def bias_rows(c, v, rows):
    nc = c.nc
    parts = c.dram("bias_parts", [PARTS, SL], BF16)
    with ExitStack() as s:
        a = c.sb(s, "a", [SLT, P])
        part = c.sb(s, "part", [SLT, PARTS, P], BF16)
        rest = c.sb(s, "rest", [SLT, 2, P])
        loaded, chain, stored = c.sem("loaded"), c.sem("chain"), c.sem("stored")
        with nc.Block() as block:
            @block.sync
            def _(sp):
                sp.dma_start(a[:], v.rearrange("(t q) -> t q", q=P)).then_inc(loaded, 16)
                sp.wait_ge(chain, 5)
                sp.dma_start(parts.rearrange("a (t q) -> t a q", q=P), part[:]).then_inc(stored, 16)
                sp.wait_ge(stored, 16)
                sp.dma_start(rows[:], parts).then_inc(loaded, 16)
                sp.wait_ge(loaded, 32)

            @block.vector
            def _(dve):
                line = Line(dve, chain)
                dve.wait_ge(loaded, 16)
                line(dve.tensor_copy(part[:, 0, :], a[:]))
                line(dve.tensor_tensor(rest[:, 0, :], a[:], part[:, 0, :], ALU.subtract))
                line(dve.tensor_copy(part[:, 1, :], rest[:, 0, :]))
                line(dve.tensor_tensor(rest[:, 1, :], rest[:, 0, :], part[:, 1, :], ALU.subtract))
                line(dve.tensor_copy(part[:, 2, :], rest[:, 1, :]))


def logits(c, pe, out, hT, phiT, bias, t, first_col, cols):
    for o in range(0, cols, BANK):
        pe.matmul(out[:, o:o + BANK], c.onesb[0:PARTS, :], bias[:, first_col + o:first_col + o + BANK],
                  start=True, stop=False)
        for k in range(DT):
            last = pe.matmul(out[:, o:o + BANK], hT[:, k, t * P:(t + 1) * P],
                             phiT[:, k, first_col + o:first_col + o + BANK], start=False, stop=(k == DT - 1))
    return last


def dispatch(c, h, hT, phiT, bias, mixed):
    nc = c.nc
    W = SL // 2
    G = W // NP
    jobs = [(half, t) for half in range(2) for t in range(T)]
    ht = SLT // 2
    S, LAG = 4, 2
    with ExitStack() as s:
        lg = [c.ps(s, "logit", [P, W]) for _ in range(2)]
        acc = c.ps(s, "acc", [P, ht, D])
        e = [c.sb(s, "e", [P, W]) for _ in range(S)]
        top, total, inverse = ([c.sb(s, n, [P, G]) for _ in range(S)] for n in ("top", "total", "inverse"))
        scored, topped, shifted, exped, summed, inverted, weighed, used, out = (
            c.sem(n) for n in ("scored", "topped", "shifted", "exped", "summed", "inverted", "weighed", "used", "out"))
        by = lambda a: a[:].rearrange("p (g e) -> p g e", e=NP)
        over = lambda a: a[:, :, None].to_broadcast([P, G, NP])
        with nc.Block() as block:
            @block.tensor
            def _(pe):
                def mix(i):
                    half, t = jobs[i]
                    pe.wait_ge(weighed, i + 1)
                    if t == 0 and half:
                        pe.wait_ge(out, 1)
                    for b in range(ht):
                        last = pe.matmul(acc[:, b, :], e[i % S][:, b * P:(b + 1) * P], h[:, t, :],
                                         start=(t == 0 and b % 2 == 0), stop=(t == T - 1), skip_group_check=True)
                    last.then_inc(used, 1)

                for i, (half, t) in enumerate(jobs):
                    wait(pe, shifted, i - 1)
                    logits(c, pe, lg[i % 2], hT, phiT, bias, t, half * W, W).then_inc(scored, 1)
                    if i >= LAG:
                        mix(i - LAG)
                for i in range(len(jobs) - LAG, len(jobs)):
                    mix(i)

            @block.vector
            def _(dve):
                def shift(i):
                    b = i % S
                    dve.wait_ge(scored, i + 1)
                    dve.tensor_reduce(top[b][:], by(lg[i % 2]), X, ALU.max).then_inc(topped, 1)
                    dve.wait_ge(topped, i + 1)
                    wait(dve, used, i - S + 1)
                    dve.tensor_tensor(by(e[b]), by(lg[i % 2]), over(top[b]), ALU.subtract).then_inc(shifted, 1)

                def total_of(i):
                    b = i % S
                    dve.wait_ge(exped, i + 1)
                    dve.tensor_reduce(total[b][:], by(e[b]), X, ALU.add).then_inc(summed, 1)
                    dve.wait_ge(summed, i + 1)
                    dve.reciprocal(inverse[b][:], total[b][:]).then_inc(inverted, 1)

                def clip(half):
                    dve.wait_ge(used, (half + 1) * T)
                    dve.tensor_scalar(mixed[:, half * ht:(half + 1) * ht, :], acc[:], LOW_CLIP, HIGH_CLIP,
                                      ALU.max, ALU.min).then_inc(out, 1)

                for i in range(len(jobs)):
                    if i == T + LAG:
                        clip(0)
                    shift(i)
                    if i:
                        total_of(i - 1)
                total_of(len(jobs) - 1)
                clip(1)

            @block.scalar
            def _(act):
                for i in range(len(jobs)):
                    act.wait_ge(shifted, i + 1)
                    nc.scalar.activation(e[i % S][:], e[i % S][:], ACT.Exp).then_inc(exped, 1)

            @block.gpsimd
            def _(pool):
                for i in range(len(jobs)):
                    pool.wait_ge(inverted, i + 1)
                    pool.tensor_tensor(by(e[i % S]), by(e[i % S]), over(inverse[i % S]), ALU.mult).then_inc(weighed, 1)


def soft_experts(c, slotsT, w, bias, results):
    nc = c.nc
    B = 6
    with ExitStack() as s:
        w_sb = [c.sb(s, "w", [P, SPT * DT, D]) for _ in range(B)]
        pick = c.sb(s, "pick", [SPT, P])
        slots = [c.ps(s, "out", [P, D]) for _ in range(4)]
        loaded = [c.sem("loaded") for _ in range(B)]
        ones_set, picked, multiplied, copied = (c.sem(n) for n in ("ones_set", "picked", "multiplied", "copied"))
        with nc.Block() as block:
            @block.sync
            def _(sp):
                for i in range(SLT):
                    wait(sp, multiplied, i - B + 1)
                    sp.dma_start(w_sb[i % B][:], w[i * SPT:(i + 1) * SPT].rearrange("e (k p) n -> p (e k) n", p=P))\
                        .then_inc(loaded[i % B], 16)

            @block.gpsimd
            def _(pool):
                pool.memset(pick[:], 1.0).then_inc(ones_set, 1)
                pool.wait_ge(ones_set, 1)
                pool.affine_select(out=pick[:], in_=pick[:], compare_op=ALU.is_ge, fill=0.0, base=0,
                                   pattern=[[1, P]], channel_multiplier=-NP).then_inc(picked, 1)
                pool.wait_ge(picked, 1)
                pool.affine_select(out=pick[:], in_=pick[:], compare_op=ALU.is_gt, fill=0.0, base=NP,
                                   pattern=[[-1, P]], channel_multiplier=NP).then_inc(picked, 1)

            @block.tensor
            def _(pe):
                pe.wait_ge(picked, 2)
                for i in range(SLT):
                    wait(pe, copied, i - 3)
                    pe.wait_ge(loaded[i % B], (i // B + 1) * 16)
                    pe.matmul(slots[i % 4][:], pick[:], bias[:, i, :], start=True, stop=False, skip_group_check=True)
                    for k in range(DT):
                        for j in range(SPT):
                            a = i * P + j * NP
                            last = pe.matmul(slots[i % 4][j * NP:(j + 1) * NP, :], slotsT[:, k, a:a + NP],
                                             w_sb[i % B][:, j * DT + k, :], start=False, stop=(k == DT - 1),
                                             skip_group_check=True)
                    last.then_inc(multiplied, 1)

            @block.vector
            def _(dve):
                for i in range(SLT):
                    dve.wait_ge(multiplied, i + 1)
                    dve.tensor_copy(results[:, i, :], slots[i % 4][:]).then_inc(copied, 1)


def combine(c, hT, phiT, bias, results):
    nc = c.nc
    with ExitStack() as s:
        lg = c.ps(s, "logit", [P, SL])
        turn = [c.ps(s, "turn", [P, BANK]) for _ in range(2)]
        y = [c.ps(s, "y", [P, BANK]) for _ in range(2)]
        e = [c.sb(s, "e", [P, SL]) for _ in range(2)]
        eT = [c.sb(s, "eT", [P, SLT, P]) for _ in range(2)]
        top, total, inverse = ([c.sb(s, n, [P, NP]) for _ in range(2)] for n in ("top", "total", "inverse"))
        scored, topped, shifted, exped, summed, inverted, weighed, turned, copied, used, added = (
            c.sem(n) for n in ("scored", "topped", "shifted", "exped", "summed", "inverted", "weighed", "turned", "copied", "used",
                               "added"))
        by_number = lambda a: a[:].rearrange("p (n q) -> p q n", q=NP)
        by = lambda a: a[:].rearrange("p (n q) -> p n q", q=NP)
        over = lambda a: a[:, None, :].to_broadcast([P, NE, NP])
        TG = SLT // 4
        with nc.Block() as block:
            @block.tensor
            def _(pe):
                def turn_over(t):
                    pe.wait_ge(weighed, t + 1)
                    for g in range(TG):
                        n = t * TG + g
                        wait(pe, copied, n - 1)
                        for b in range(4):
                            st = 4 * g + b
                            last = pe.transpose(turn[n % 2][:, b * P:(b + 1) * P], e[t % 2][:, st * P:(st + 1) * P],
                                                c.identf[:])
                        last.then_inc(turned, 1)

                def sum_up(t):
                    pe.wait_ge(copied, (t + 1) * TG)
                    wait(pe, added, t - 1)
                    for st in range(SLT):
                        last = pe.matmul(y[t % 2][:, 0:D], eT[t % 2][:, st, :], results[:, st, :],
                                         start=(st == 0), stop=(st == SLT - 1))
                    last.then_inc(used, 1)

                for t in range(T):
                    wait(pe, shifted, t)
                    logits(c, pe, lg, hT, phiT, bias, t, 0, SL).then_inc(scored, 1)
                    if t:
                        turn_over(t - 1)
                        sum_up(t - 1)
                turn_over(T - 1)
                sum_up(T - 1)

            @block.vector
            def _(dve):
                def shift(t):
                    dve.wait_ge(scored, t + 1)
                    dve.tensor_reduce(top[t % 2][:], by_number(lg), X, ALU.max).then_inc(topped, 1)
                    dve.wait_ge(topped, t + 1)
                    wait(dve, turned, (t - 1) * TG)
                    dve.tensor_tensor(by(e[t % 2]), by(lg), over(top[t % 2]), ALU.subtract).then_inc(shifted, 1)

                def total_of(t):
                    dve.wait_ge(exped, t + 1)
                    dve.tensor_reduce(total[t % 2][:], by_number(e[t % 2]), X, ALU.add).then_inc(summed, 1)
                    dve.wait_ge(summed, t + 1)
                    dve.reciprocal(inverse[t % 2][:], total[t % 2][:]).then_inc(inverted, 1)

                def add(t):
                    dve.wait_ge(used, t + 1)
                    dve.tensor_tensor(c.x[:, t, :], y[t % 2][:, 0:D], c.x[:, t, :], ALU.add).then_inc(added, 1)

                for t in range(T):
                    shift(t)
                    total_of(t)
                    if t:
                        add(t - 1)
                add(T - 1)

            @block.scalar
            def _(act):
                def copy(t):
                    wait(act, used, t - 1)
                    for g in range(TG):
                        act.wait_ge(turned, t * TG + g + 1)
                        out = eT[t % 2][:, 4 * g:4 * g + 4, :].rearrange("p a b -> p (a b)")
                        nc.scalar.activation(out, turn[g % 2][:], ACT.Copy).then_inc(copied, 1)

                for t in range(T):
                    if t:
                        copy(t - 1)
                    act.wait_ge(shifted, t + 1)
                    nc.scalar.activation(e[t % 2][:], e[t % 2][:], ACT.Exp).then_inc(exped, 1)
                copy(T - 1)

            @block.gpsimd
            def _(pool):
                for t in range(T):
                    pool.wait_ge(inverted, t + 1)
                    pool.tensor_tensor(by(e[t % 2]), by(e[t % 2]), over(inverse[t % 2]), ALU.mult).then_inc(weighed, 1)


def soft_layer(c, phi_w, phi_b, expert_w, expert_b):
    nc = c.nc
    with ExitStack() as s:
        hT = c.sb(s, "hT", [P, DT, N])
        phiT = c.sb(s, "phiT", [P, DT, SL])
        bias = c.sb(s, "bias", [PARTS, SL], BF16)
        expert_bias = c.sb(s, "expert_bias", [SPT, SLT, D])
        results = c.sb(s, "results", [P, SLT, D])
        with ExitStack() as s1:
            mixed = c.sb(s1, "mixed", [P, SLT, D])
            with ExitStack() as s2:
                h, phi = c.sb(s2, "h", [P, T, D]), c.sb(s2, "phi", [P, SLT, D])
                load(c, [(phi[:], phi_w.rearrange("(t p) d -> p t d", p=P)),
                         (expert_bias[:], expert_b.rearrange("(t j) d -> j t d", j=SPT))])
                bias_rows(c, phi_b, bias)
                transpose_tiles(c, phi, phiT)
                layernorm(c, c.x, h)
                transpose_tiles(c, h, hT)
                dispatch(c, h, hT, phiT, bias, mixed)
            slotsT = c.sb(s1, "slotsT", [P, DT, SL])
            layernorm(c, mixed, mixed)
            squashed = c.sem("squashed")
            with nc.Block() as block:
                @block.scalar
                def _(act):
                    nc.scalar.activation(mixed[:], mixed[:], ACT.Tanh).then_inc(squashed, 1)
                    act.wait_ge(squashed, 1)
            transpose_tiles(c, mixed, slotsT)
            soft_experts(c, slotsT, expert_w, expert_bias, results)
        combine(c, hT, phiT, bias, results)


def store_x(c, out):
    nc = c.nc
    stored = c.sem("stored")
    with nc.Block() as block:
        @block.sync
        def _(sp):
            sp.dma_start(out.rearrange("b (t p) d -> p (b t) d", p=P), c.x[:]).then_inc(stored, 16)
            sp.wait_ge(stored, 16)


def decoder(nc, a, out):
    with ExitStack() as ctx:
        c = Core(nc, ctx)
        setup(c, a["x"])
        layer0_attention(c, *(a[f"L0_attn_{n}"] for n in ("w_attn", "b_attn", "w_proj", "b_proj")))
        c.recycle()
        cross_layer(c, "c0", a["ctx_1024"], [a[f"L0_xattn_W_{n}"] for n in "qkvo"],
                    [a[f"L0_xattn_b_{n}"] for n in "qkvo"], False)
        c.recycle()
        expert_layer(c, *(a[f"L0_ffn_{n}"] for n in ("Wg", "bg", "W1", "W2", "W3")))
        c.recycle()
        window_layer(c, *(a[f"L1_attn_{n}"] for n in ("W_qkv", "b_qkv", "q_gamma", "q_beta", "k_gamma", "k_beta",
                                                      "W_out", "b_out")))
        c.recycle()
        cross_layer(c, "c1", a["ctx_1024"], [a[f"L1_xattn_W{n}"] for n in "qkvo"],
                    [a[f"L1_xattn_b{n}"] for n in "qkvo"], True)
        c.recycle()
        soft_layer(c, *(a[f"L1_ffn_{n}"] for n in ("phi_w", "phi_b", "expert_w", "expert_b")))
        store_x(c, out)


def kernel(**inputs):
    import numpy as np
    import concourse.bacc as bacc
    from concourse.bass_utils import run_bass_kernel_spmd

    nc = bacc.Bacc("TRN2", target_bir_lowering=False, num_devices=1)
    arrays, args = {}, {}
    for name, value in inputs.items():
        value = np.ascontiguousarray(value)
        arrays[f"in_{name}"] = value
        args[name] = nc.dram_tensor(f"in_{name}", value.shape, mybir.dt.from_np(value.dtype), kind="ExternalInput").ap()
    out = nc.dram_tensor("out_x", (1, N, D), F32, kind="ExternalOutput").ap()
    decoder(nc, args, out)
    return run_bass_kernel_spmd(nc, [arrays], core_ids=[0]).results[0]["out_x"]
```

```python
from contextlib import ExitStack

import concourse.bass as bass
from concourse import mybir

F32, BF16, I32, U32, U8 = (mybir.dt.float32, mybir.dt.bfloat16, mybir.dt.int32, mybir.dt.uint32,
                           mybir.dt.uint8)
ALU = mybir.AluOpType
ACT = mybir.ActivationFunctionType
X = mybir.AxisListType.X

P = 128
N = 2048
T = N // P
D = 256
DT = D // P
H = 16
HD = D // H
HALF_HEADS = P // HD
BANK = 512
CH = N // BANK
WIDE = 2 * BANK
NWIDE = N // WIDE
BANKS = 8
M = 1601
MT = (M + P - 1) // P
MPAD = MT * P
PARTS = 3
PAIRS = 6
SR = PAIRS * HD
SRM = SR + PARTS
BIG = -1.0e30
MAGIC = 12582912.0
TINY_SCALE = 0.01
HALF = 128.0


class Line:

    def __init__(self, eng, sem):
        self.eng, self.sem, self.n = eng, sem, 0

    def __call__(self, ins):
        self.n += 1
        ins.then_inc(self.sem, 1)
        self.eng.wait_ge(self.sem, self.n)


def wait(eng, sem, value):
    if not isinstance(value, int) or value > 0:
        eng.wait_ge(sem, value)


class Core:

    def __init__(self, nc, ctx):
        self.nc, self.ctx, self.n, self.sems = nc, ctx, 0, []

    def sb(self, ctx, name, shape, dt=F32):
        return ctx.enter_context(self.nc.sbuf_tensor(self.unique(name), shape, dt))

    def ps(self, ctx, name, shape, dt=F32):
        return ctx.enter_context(self.nc.psum_tensor(self.unique(name), shape, dt))

    def sem(self, name):
        self.sems.append(self.nc.alloc_semaphore(self.unique(name)))
        return self.sems[-1]

    def recycle(self):
        self.nc.clear_and_free_semaphores(self.sems)
        self.nc.all_engine_barrier()
        self.sems = []

    def dram(self, name, shape, dt=F32):
        return self.nc.dram_tensor(name, shape, dt, kind="Internal").ap()

    def unique(self, name):
        self.n += 1
        return f"{name}_{self.n}"


def setup(c, x_in):
    nc = c.nc
    c.x = c.sb(c.ctx, "x", [P, T, D])
    c.identf = c.sb(c.ctx, "identf", [P, P])
    c.identb = c.sb(c.ctx, "identb", [P, P], BF16)
    c.onesf = c.sb(c.ctx, "onesf", [P, P])
    c.onesb = c.sb(c.ctx, "onesb", [P, P], BF16)
    c.triu = c.sb(c.ctx, "triu", [P, P], BF16)
    c.mask_qk = c.sb(c.ctx, "mask_qk", [P, 2 * P], BF16)
    c.mask_kq = c.sb(c.ctx, "mask_kq", [P, 2 * P], BF16)
    c.mask_first = c.sb(c.ctx, "mask_first", [P, 2 * P], BF16)
    c.eps = c.sb(c.ctx, "eps", [P, 1])
    c.ones_wide = c.sb(c.ctx, "ones_wide", [8 * PARTS, 2 * N], BF16)
    x_loaded, made, filled = c.sem("x_loaded"), c.sem("made"), c.sem("filled")
    with nc.Block() as block:
        @block.sync
        def _(sp):
            sp.dma_start(c.x[:], x_in.rearrange("b (t p) d -> p (b t) d", p=P)).then_inc(x_loaded, 16)
            sp.wait_ge(x_loaded, 16)

        @block.gpsimd
        def _(pool):
            for buf, v in ((c.identf, 0.0), (c.identb, 0.0), (c.onesf, 1.0), (c.onesb, 1.0),
                           (c.triu, 1.0), (c.mask_qk, 0.0), (c.mask_kq, 0.0), (c.eps, 1e-5), (c.ones_wide, 1.0),
                           (c.mask_first[:, 0:P], BIG), (c.mask_first[:, P:2 * P], 0.0)):
                pool.memset(buf if isinstance(buf, bass.AP) else buf[:], v).then_inc(filled, 1)
            pool.wait_ge(filled, 11)

            def keep(ap, op, fill, row, col):
                pool.affine_select(out=ap, in_=ap, compare_op=op, fill=fill, base=0,
                                   pattern=[[col, P]], channel_multiplier=row).then_inc(made, 1)

            keep(c.identf[:], ALU.not_equal, 1.0, 1, -1)
            keep(c.identb[:], ALU.not_equal, 1.0, 1, -1)
            keep(c.triu[:], ALU.is_ge, 0.0, -1, 1)
            keep(c.mask_qk[:, 0:P], ALU.is_gt, BIG, -1, 1)
            keep(c.mask_qk[:, P:2 * P], ALU.is_ge, BIG, 1, -1)
            keep(c.mask_first[:, P:2 * P], ALU.is_ge, BIG, 1, -1)
            keep(c.mask_kq[:, 0:P], ALU.is_ge, BIG, -1, 1)
            keep(c.mask_kq[:, P:2 * P], ALU.is_gt, BIG, 1, -1)
            pool.wait_ge(made, 8)


def layernorm(c, src, dst):
    nc = c.nc
    with ExitStack() as s:
        stats = c.sb(s, "stats", [P, T, 6])
        mv = c.sb(s, "mv", [P, T, 2])
        rstd = c.sb(s, "rstd", [P, T])
        root = c.sb(s, "root", [P, T])
        chain, var_ready, root_ready = c.sem("chain"), c.sem("var_ready"), c.sem("root_ready")
        stats_done = c.sem("stats_done")
        with nc.Block() as block:
            @block.vector
            def _(dve):
                line = Line(dve, chain)
                for t in range(T):
                    dve.bn_stats(stats[:, t, :], src[:, t, :]).then_inc(stats_done, 1)
                for t in range(T):
                    dve.wait_ge(stats_done, t + 1)
                    ins = dve.bn_aggr(mv[:, t, :], stats[:, t, :])
                    ins.then_inc(var_ready, 1)
                dve.wait_ge(root_ready, 1)
                line(dve.reciprocal(rstd[:], root[:]))
                for t in range(T):
                    last = dve.tensor_scalar(dst[:, t, :], src[:, t, :], mv[:, t, 0:1],
                                             rstd[:, t:t + 1], ALU.subtract, ALU.mult)
                line(last)

            @block.scalar
            def _(act):
                act.wait_ge(var_ready, T)
                nc.scalar.activation(root[:], mv[:, :, 1], ACT.Sqrt, bias=c.eps[:, 0:1]).then_inc(root_ready, 1)


def transpose_tiles(c, src, dst, tiles=T, rows=N, dt=F32, scale=None, bias=None):
    nc = c.nc
    ident = c.identf if dt == F32 else c.identb
    groups = [(h, g) for h in range(DT) for g in range((tiles + 3) // 4)]
    with ExitStack() as s:
        slots = [c.ps(s, "tp", [P, BANK], dt) for _ in range(4)]
        turned, copied = c.sem("turned"), [c.sem("copied_dve"), c.sem("copied_act")]
        width = lambda g: min(4 * P, rows - 4 * P * g)
        with nc.Block() as block:
            @block.tensor
            def _(pe):
                for i, (h, g) in enumerate(groups):
                    if i >= 4:
                        pe.wait_ge(copied[i % 2], (i - 4) // 2 + 1)
                    for t in range(4 * g, min(4 * g + 4, tiles)):
                        n = min(P, rows - t * P)
                        o = (t - 4 * g) * P
                        last = pe.transpose(slots[i % 4][:, o:o + n], src[0:n, t, h * P:(h + 1) * P],
                                            ident[0:n, 0:n])
                    last.then_inc(turned, 1)

            def copy(i, eng):
                h, g = groups[i]
                n = width(g)
                eng.wait_ge(turned, i + 1)
                out, in_ = dst[:, h, 4 * P * g:4 * P * g + n], slots[i % 4][:, 0:n]
                if bias is not None:
                    if i % 2:
                        ins = nc.scalar.activation(out, in_, ACT.Identity, scale=scale[:, h:h + 1],
                                                   bias=bias[:, h:h + 1])
                    else:
                        ins = eng.tensor_scalar(out, in_, scale[:, h:h + 1], bias[:, h:h + 1], ALU.mult, ALU.add)
                elif scale is not None:
                    if i % 2:
                        ins = nc.scalar.activation(out, in_, ACT.Copy, scale=scale[:, h:h + 1])
                    else:
                        ins = eng.tensor_scalar(out, in_, scale[:, h:h + 1], None, ALU.mult)
                else:
                    ins = nc.scalar.activation(out, in_, ACT.Copy) if i % 2 else eng.tensor_copy(out, in_)
                ins.then_inc(copied[i % 2], 1)

            @block.vector
            def _(dve):
                for i in range(0, len(groups), 2):
                    copy(i, dve)

            @block.scalar
            def _(act):
                for i in range(1, len(groups), 2):
                    copy(i, act)


def norm_and_turn(c, src, dst, h, function=ACT.Copy):
    nc = c.nc
    groups = [(g, k) for g in range(T // 4) for k in range(DT)]
    with ExitStack() as s:
        stats, mv = c.sb(s, "stats", [P, T, 6]), c.sb(s, "mv", [P, T, 2])
        rstd, root = c.sb(s, "rstd", [P, T]), c.sb(s, "root", [P, T])
        slots = [c.ps(s, "tp", [P, BANK]) for _ in range(4)]
        stats_done, var_ready, root_ready, rstd_ready, normed, turned, copied = (
            c.sem(n) for n in ("stats_done", "var_ready", "root_ready", "rstd_ready", "normed", "turned", "copied"))
        with nc.Block() as block:
            @block.vector
            def _(dve):
                for t in range(T):
                    dve.bn_stats(stats[:, t, :], src[:, t, :]).then_inc(stats_done, 1)
                for t in range(T):
                    dve.wait_ge(stats_done, t + 1)
                    dve.bn_aggr(mv[:, t, :], stats[:, t, :]).then_inc(var_ready, 1)
                dve.wait_ge(root_ready, 1)
                dve.reciprocal(rstd[:], root[:]).then_inc(rstd_ready, 1)
                dve.wait_ge(rstd_ready, 1)
                for t in range(T):
                    dve.tensor_scalar(h[:, t, :], src[:, t, :], mv[:, t, 0:1], rstd[:, t:t + 1],
                                      ALU.subtract, ALU.mult).then_inc(normed, 1)

            @block.scalar
            def _(act):
                act.wait_ge(var_ready, T)
                nc.scalar.activation(root[:], mv[:, :, 1], ACT.Sqrt, bias=c.eps[:, 0:1]).then_inc(root_ready, 1)
                for i, (g, k) in enumerate(groups):
                    act.wait_ge(turned, i + 1)
                    nc.scalar.activation(dst[:, k, g * BANK:(g + 1) * BANK], slots[i % 4][:], function).then_inc(copied, 1)
                act.wait_ge(copied, len(groups))

            @block.tensor
            def _(pe):
                for i, (g, k) in enumerate(groups):
                    if i >= 4:
                        pe.wait_ge(copied, i - 3)
                    pe.wait_ge(normed, 4 * g + 4)
                    for t in range(4):
                        last = pe.transpose(slots[i % 4][:, t * P:(t + 1) * P], h[:, 4 * g + t, k * P:(k + 1) * P],
                                            c.identf[:])
                    last.then_inc(turned, 1)


def ceil_pow2(line, dve, m, low, step):
    line(dve.tensor_scalar(m, m, TINY_SCALE, None, ALU.max))
    line(dve.tensor_scalar(low.bitcast(I32), m.bitcast(I32), 0x7F800000, None, ALU.bitwise_and))
    line(dve.tensor_tensor(step, m, low, ALU.is_gt))
    line(dve.scalar_tensor_tensor(m, step, 1.0, low, ALU.add, ALU.mult))


def quantize(c, src, dst, tiles, cols, group, rows_first=False, fold=1.0, by_element=False):
    nc = c.nc
    G, B = cols // group, cols // P
    with ExitStack() as s:
        cmax = c.sb(s, "cmax", [P, cols])
        col = c.sb(s, "col", [P, B])
        cl, cs = c.sb(s, "cl", [P, B]), c.sb(s, "cs", [P, B])
        diag = c.sb(s, "diag", [P, B, P])
        cscale = c.sb(s, "cscale", [P, cols])
        cinv = c.sb(s, "cinv", [P, cols])
        row = c.sb(s, "row", [P, tiles * G])
        rl, rs = c.sb(s, "rl", [P, tiles * G]), c.sb(s, "rs", [P, tiles * G])
        nb = (cols + BANK - 1) // BANK
        turned_ps = c.ps(s, "turned_ps", [P, nb * BANK])
        spread_ps = c.ps(s, "spread_ps", [P, nb * BANK])
        chain, cmax_ready, turned = c.sem("chain"), c.sem("cmax_ready"), c.sem("turned")
        diag_ready, spread = c.sem("diag_ready"), c.sem("spread")
        grouped = src[:, :, :].rearrange("p t (g e) -> p (t g) e", e=group)
        over_cols = lambda a: a[:, None, :].to_broadcast([P, tiles, cols])
        over_group = lambda a: a[:, :, None].to_broadcast([P, tiles * G, group])

        def scaled_back(dve):
            if not by_element:
                return dve.tensor_tensor(dst[:, :, :], src[:, :, :], over_cols(cscale), ALU.mult)
            return dve.tensor_tensor(dst[:, :, :].rearrange("p t (e h) -> p t h e", e=HD),
                                     src[:, :, :].rearrange("p t (h e) -> p t h e", e=HD),
                                     cscale[:].rearrange("p (h e) -> p h e", e=HD)[:, None, :, :]
                                     .to_broadcast([P, tiles, H, HD]), ALU.mult)

        with nc.Block() as block:
            @block.vector
            def _(dve):
                line = Line(dve, chain)

                def column_scales():
                    dve.tensor_reduce(cmax[:], src[:, :, :].rearrange("p t c -> p c t"), X, ALU.max,
                                      apply_absolute_value=True).then_inc(cmax_ready, 1)
                    dve.wait_ge(turned, 1)
                    line(dve.tensor_reduce(col[:], turned_ps[:, 0:cols].rearrange("p (b q) -> p b q", q=P),
                                           X, ALU.max))
                    ceil_pow2(line, dve, col[:], cl[:], cs[:])
                    for b in range(B):
                        last = dve.tensor_scalar(diag[:, b, :], c.identf[:], col[:, b:b + 1], None, ALU.mult)
                        last.then_inc(diag_ready, 1)
                    dve.wait_ge(spread, 1)
                    line(dve.tensor_copy(cscale[:], spread_ps[:, 0:cols]))
                    line(dve.reciprocal(cinv[:], cscale[:]))

                def row_scales():
                    line(dve.tensor_reduce(row[:], grouped, X, ALU.max, apply_absolute_value=True))
                    ceil_pow2(line, dve, row[:], rl[:], rs[:])
                    line(dve.reciprocal(rl[:], row[:]))

                def to_integers():
                    line(dve.tensor_scalar(src[:, :, :], src[:, :, :], MAGIC, MAGIC + HALF - 1, ALU.add, ALU.min))

                if not rows_first:
                    column_scales()
                    line(dve.tensor_tensor(src[:, :, :], src[:, :, :], over_cols(cinv), ALU.mult))
                    row_scales()
                    line(dve.tensor_scalar(rl[:], rl[:], HALF, None, ALU.mult))
                    line(dve.tensor_tensor(grouped, grouped, over_group(rl), ALU.mult))
                    to_integers()
                    line(dve.tensor_scalar(row[:], row[:], fold / HALF, None, ALU.mult))
                    line(dve.scalar_tensor_tensor(grouped, grouped, -MAGIC, over_group(row), ALU.add, ALU.mult))
                    line(scaled_back(dve))
                else:
                    row_scales()
                    line(dve.tensor_tensor(grouped, grouped, over_group(rl), ALU.mult))
                    column_scales()
                    line(dve.tensor_scalar(cinv[:], cinv[:], HALF, None, ALU.mult))
                    line(dve.tensor_tensor(src[:, :, :], src[:, :, :], over_cols(cinv), ALU.mult))
                    to_integers()
                    line(dve.tensor_scalar(row[:], row[:], fold / HALF, None, ALU.mult))
                    line(dve.scalar_tensor_tensor(grouped, grouped, -MAGIC, over_group(row), ALU.add, ALU.mult))
                    line(scaled_back(dve))

            @block.tensor
            def _(pe):
                pe.wait_ge(cmax_ready, 1)
                for b in range(B):
                    last = pe.transpose(turned_ps[:, b * P:(b + 1) * P], cmax[:, b * P:(b + 1) * P], c.identf[:])
                last.then_inc(turned, 1)
                pe.wait_ge(diag_ready, B)
                for b in range(B):
                    last = pe.matmul(spread_ps[:, b * P:(b + 1) * P], c.onesf[:], diag[:, b, :],
                                     start=True, stop=True)
                last.then_inc(spread, 1)


def start_loads(c, pairs):
    loaded = [c.sem("loaded_sp"), c.sem("loaded_act")]
    with c.nc.Block() as block:
        def send(eng, half):
            for dst, src in pairs[half::2]:
                eng.dma_start(dst, src).then_inc(loaded[half], 16)

        @block.sync
        def _(sp):
            send(sp, 0)

        @block.scalar
        def _(act):
            send(act, 1)
    return [(sem, 16 * len(pairs[half::2])) for half, sem in enumerate(loaded)]


def finish_loads(c, started):
    with c.nc.Block() as block:
        @block.sync
        def _(sp):
            for sem, count in started:
                wait(sp, sem, count)


def load(c, pairs):
    finish_loads(c, start_loads(c, pairs))


def row_of(vec, n):
    return vec.rearrange("(o n) -> o n", o=1).to_broadcast([P, n])


def project_tokens(c, lhs, rhs, bias, width, tiles, rows, dst, scale=None, residual=None):
    nc = c.nc
    spans = [(o, min(BANK, width - o)) for o in range(0, width, BANK)]
    with ExitStack() as s:
        slots = [c.ps(s, "prod", [P, len(spans) * BANK]) for _ in range(8 // len(spans) // 2)]
        K = len(slots)
        temp = c.sb(s, "temp", [P, 2, width])
        multiplied, added, chain = c.sem("multiplied"), c.sem("added"), c.sem("chain")
        with nc.Block() as block:
            @block.tensor
            def _(pe):
                for t in range(tiles):
                    n = min(P, rows - t * P)
                    if t >= K:
                        pe.wait_ge(added, t - K + 1)
                    for o, w in spans:
                        for k in range(DT):
                            last = pe.matmul(slots[t % K][0:n, o:o + w], lhs[:, k, t * P:t * P + n],
                                             rhs[:, k, o:o + w], start=(k == 0), stop=(k == DT - 1))
                    last.then_inc(multiplied, 1)

            @block.vector
            def _(dve):
                line = Line(dve, chain)
                for t in range(tiles):
                    n = min(P, rows - t * P)
                    dve.wait_ge(multiplied, t + 1)
                    src = slots[t % K][0:n, 0:width]
                    if scale is not None:
                        line(dve.scalar_tensor_tensor(temp[0:n, t % 2, :], src, scale[0:n, t:t + 1],
                                                      bias[0:n, 0:width], ALU.mult, ALU.add))
                    elif residual is not None:
                        line(dve.tensor_tensor(temp[0:n, t % 2, :], src, bias[0:n, 0:width], ALU.add))
                    if residual is not None:
                        ins = dve.tensor_tensor(dst[0:n, t, :], temp[0:n, t % 2, :], residual[0:n, t, :], ALU.add)
                    else:
                        ins = dve.tensor_tensor(dst[0:n, t, 0:width], src, bias[0:n, 0:width], ALU.add)
                    ins.then_inc(added, 1)
                dve.wait_ge(added, tiles)


def transposed_to_dram(c, srcs):
    nc = c.nc
    jobs = [(n, h, g) for n in range(len(srcs)) for h in range(DT) for g in range(T // 4)]
    per_half = T // 4
    with ExitStack() as s:
        slots = [c.ps(s, "tp", [P, 4 * P], BF16) for _ in range(4)]
        stage = c.sb(s, "stage", [P, len(srcs), DT, N], BF16)
        turned, copied, stored = c.sem("turned"), c.sem("copied"), c.sem("stored")
        with nc.Block() as block:
            @block.tensor
            def _(pe):
                for i, (n, h, g) in enumerate(jobs):
                    if i >= 4:
                        pe.wait_ge(copied, i - 3)
                    for t in range(4):
                        last = pe.transpose(slots[i % 4][:, t * P:(t + 1) * P],
                                            srcs[n][0][:, 4 * g + t, h * P:(h + 1) * P], c.identb[:])
                    last.then_inc(turned, 1)

            @block.vector
            def _(dve):
                for i, (n, h, g) in enumerate(jobs):
                    dve.wait_ge(turned, i + 1)
                    dve.tensor_copy(stage[:, n, h, g * BANK:(g + 1) * BANK], slots[i % 4][:]).then_inc(copied, 1)

            @block.sync
            def _(sp):
                for n, (_, op) in enumerate(srcs):
                    for h in range(DT):
                        sp.wait_ge(copied, (n * DT + h + 1) * per_half)
                        sp.dma_start(op[0:HD].rearrange("(f e) h n -> f (e h) n", f=DT)[h],
                                     stage[:, n, h, :]).then_inc(stored, 16)
                sp.wait_ge(stored, 16 * len(srcs) * DT)


def split_rows(c, values, rows):
    nc = c.nc
    W = H * T
    rows = [r.rearrange("h (t q) -> (h t) q", q=P) for r in rows]
    with ExitStack() as s:
        part = c.sb(s, "part", [P, PARTS, W], BF16)
        rest = c.sb(s, "rest", [P, 2, W])
        turned_sb = c.sb(s, "turned_sb", [P, PARTS, W // P, P], BF16)
        turned_ps = c.ps(s, "turned_ps", [P, PARTS, W // P, P], BF16)
        chain, parted, turned, copied, stored = (c.sem("chain"), c.sem("parted"), c.sem("turned"),
                                                 c.sem("copied"), c.sem("stored"))
        with nc.Block() as block:
            @block.vector
            def _(dve):
                line = Line(dve, chain)
                line(dve.tensor_copy(part[:, 0, :], values))
                line(dve.tensor_tensor(rest[:, 0, :], values, part[:, 0, :], ALU.subtract))
                line(dve.tensor_copy(part[:, 1, :], rest[:, 0, :]))
                line(dve.tensor_tensor(rest[:, 1, :], rest[:, 0, :], part[:, 1, :], ALU.subtract))
                dve.tensor_copy(part[:, 2, :], rest[:, 1, :]).then_inc(parted, 1)
                dve.wait_ge(turned, 1)
                dve.tensor_copy(turned_sb[:], turned_ps[:]).then_inc(copied, 1)

            @block.tensor
            def _(pe):
                pe.wait_ge(parted, 1)
                for i in range(PARTS):
                    for b in range(W // P):
                        last = pe.transpose(turned_ps[:, i, b, :], part[:, i, b * P:(b + 1) * P], c.identb[:])
                last.then_inc(turned, 1)

            @block.sync
            def _(sp):
                sp.wait_ge(copied, 1)
                for i in range(PARTS):
                    sp.dma_start(rows[i].rearrange("(b r) q -> r b q", r=P), turned_sb[:, i, :, :]).then_inc(stored, 16)
                sp.wait_ge(stored, 16 * PARTS)


R1, R2, R3 = HD, HD + PARTS, HD + 2 * PARTS


def ring_of_banks(jobs):
    first, sizes, at = [], [(hi - 1) // BANK - lo // BANK + 1 for _, lo, hi in jobs], 0
    for n in sizes:
        assert at % BANKS + n <= BANKS
        first.append(at % BANKS)
        at += n
    assert at % BANKS == 0
    holders = []
    for i, n in enumerate(sizes):
        j = i - 1
        while not (first[j % len(jobs)] < first[i] + n and first[i] < first[j % len(jobs)] + sizes[j % len(jobs)]):
            j -= 1
        holders.append(j)
    return [f * BANK - lo // BANK * BANK for f, (_, lo, _) in zip(first, jobs)], holders


def causal_scores(c, pe, ring, still, moving, shift, job, mask):
    t, lo, hi = job
    diag = t * P
    for o in range(lo // BANK * BANK, hi, BANK):
        a, b = max(o, lo), min(o + BANK, hi)
        has_diag = a <= diag < b
        last = pe.matmul(ring[:, shift + a:shift + b], still[:, t * P:(t + 1) * P], moving[:, a:b],
                         start=True, stop=not has_diag)
        if has_diag:
            last = pe.matmul(ring[:, shift + diag:shift + diag + P], c.identb[:], mask, start=False, stop=True)
    return last


def load_head_pairs(sp, buffers, operands, rows, loaded, scored, jobs):
    def loads(head, par, wait_for):
        wait(sp, scored, wait_for)
        for buf, op in zip(buffers, operands):
            sp.dma_start(buf[par][0:rows, None, :], op[0:rows, bass.ds(head, 1), :]).then_inc(loaded[par], 16)

    loads(0, 0, 0)
    loads(1, 1, 0)
    with sp.Fori(0, H // 2 - 1) as g:
        for par in range(2):
            loads(g * 2 + (2 + par), par, g * (2 * jobs) + jobs * (par + 1))


def causal_stats(c, operands, low, sums):
    nc = c.nc
    every = [(t, o, min(o + WIDE, (t + 1) * P)) for t in range(T) for o in range(0, (t + 1) * P, WIDE)]
    one = [job for job in every if job[2] - job[1] <= BANK]
    two = [job for job in every if job[2] - job[1] > BANK]
    jobs = []
    while one:
        jobs += [two.pop(), one.pop(), two.pop(), one.pop(), two.pop()]
    jobs += two
    U = len(jobs)
    places, holders = ring_of_banks(jobs)
    START = -min(holders)
    with ExitStack() as s:
        q_sb = [c.sb(s, "q_sb", [R3, N], BF16) for _ in range(2)]
        k_sb = [c.sb(s, "k_sb", [R3, N], BF16) for _ in range(2)]
        ring = c.ps(s, "ring", [P, BANKS * BANK])
        loaded = [c.sem("loaded0"), c.sem("loaded1")]
        scored, maxed, summed = c.sem("scored"), c.sem("maxed"), c.sem("summed")

        def column(g, par, job):
            t, o, _ = job
            return bass.ds(g * (2 * T * NWIDE) + ((par * T + t) * NWIDE + o // WIDE), 1)

        with nc.Block() as block:
            @block.sync
            def _(sp):
                load_head_pairs(sp, (q_sb, k_sb), operands, R1, loaded, scored, U)

            @block.tensor
            def _(pe):
                with pe.Fori(0, H // 2) as g:
                    for par in range(2):
                        pe.wait_ge(loaded[par], (g + 1) * (16 * 2))
                        for u, job in enumerate(jobs):
                            pe.wait_ge(summed, g * (2 * U) + (par * U + holders[u] + 1 + START))
                            causal_scores(c, pe, ring, q_sb[par][0:R1], k_sb[par][0:R1], places[u], job,
                                          c.mask_qk[:, P:2 * P]).then_inc(scored, 1)

            @block.vector
            def _(dve):
                with dve.Fori(0, H // 2) as g:
                    for par in range(2):
                        for u, job in enumerate(jobs):
                            dve.wait_ge(scored, g * (2 * U) + (par * U + u + 1))
                            dve.tensor_reduce(low[:, column(g, par, job)], ring[:, places[u] + job[1]:places[u] + job[2]],
                                              X, ALU.max, negate=True).then_inc(maxed, 1)

            @block.scalar
            def _(act):
                act.sem_inc(summed, START)
                with act.Fori(0, H // 2) as g:
                    for par in range(2):
                        for u, job in enumerate(jobs):
                            act.wait_ge(maxed, g * (2 * U) + (par * U + u + 1))
                            score = ring[:, places[u] + job[1]:places[u] + job[2]]
                            nc.scalar.activation(score, score, ACT.Exp, bias=low[:, column(g, par, job)],
                                                 accum_out=sums[:, column(g, par, job)]).then_inc(summed, 1)


def causal_maxima(c, operands, rows, by_key, out):
    nc = c.nc
    span = (lambda t: (T - 1 - t, (T - 1 - t) * P, N)) if by_key else (lambda t: (t, 0, (t + 1) * P))
    by_size = [[span(t) for t in range(4 * n, 4 * n + 4)] for n in range(4)]
    jobs = by_size[3] + [job for pair in zip(by_size[2], by_size[0]) for job in pair] + by_size[1]
    places, holders = ring_of_banks(jobs)
    START = -min(holders)
    with ExitStack() as s:
        q_sb = [c.sb(s, "q_sb", [R3, N], BF16) for _ in range(2)]
        k_sb = [c.sb(s, "k_sb", [R3, N], BF16) for _ in range(2)]
        ring = c.ps(s, "ring", [P, BANKS * BANK])
        loaded = [c.sem("loaded0"), c.sem("loaded1")]
        scored, maxed = c.sem("scored"), c.sem("maxed")
        with nc.Block() as block:
            @block.sync
            def _(sp):
                load_head_pairs(sp, (q_sb, k_sb), operands, rows, loaded, scored, T)

            @block.tensor
            def _(pe):
                moving, still = (q_sb, k_sb) if by_key else (k_sb, q_sb)
                mask = c.mask_kq[:, 0:P] if by_key else c.mask_qk[:, P:2 * P]
                with pe.Fori(0, H // 2) as g:
                    for par in range(2):
                        pe.wait_ge(loaded[par], (g + 1) * (16 * 2))
                        for u, job in enumerate(jobs):
                            pe.wait_ge(maxed, g * (2 * T) + (par * T + holders[u] + 1 + START))
                            causal_scores(c, pe, ring, still[par][0:rows], moving[par][0:rows], places[u], job,
                                          mask).then_inc(scored, 1)

            @block.vector
            def _(dve):
                dve.sem_inc(maxed, START)
                with dve.Fori(0, H // 2) as g:
                    for par in range(2):
                        for u, (t, lo, hi) in enumerate(jobs):
                            dve.wait_ge(scored, g * (2 * T) + (par * T + u + 1))
                            dve.tensor_reduce(out[:, bass.ds(g * (2 * T) + (par * T + t), 1)],
                                              ring[:, places[u] + lo:places[u] + hi], X, ALU.max).then_inc(maxed, 1)


def causal_weights(c, operands, values32, out_rows):
    nc = c.nc
    left = [(k, k * P, N // 2) for k in range(T // 2)]
    right = [(k, max(k * P, N // 2), N) for k in range(T)]
    merged = 5
    units = []
    for k in range(T // 2):
        units += [[left[k]] if k < merged else [left[k], right[k + T // 2]], [right[k]]]
    units += [[right[k]] for k in range(T // 2, T // 2 + merged)]
    assert sorted(sum(units, [])) == sorted(left + right)
    U, LAG, S, W = len(units), 2, 3, 6

    def places(unit):
        if len(unit) == 1:
            return [(*unit[0], unit[0][1] % (N // 2))], N // 2
        (_, lo, hi), (_, lo2, hi2) = unit
        return [(*unit[0], BANK - (hi - lo)), (*unit[1], BANK)], BANK + hi2 - lo2

    def columns(unit):
        segments, end = places(unit)
        return slice(segments[0][3], end)

    def pieces(segment):
        _, lo, hi, at = segment
        return [(o // BANK, max(o, lo), min(o + BANK, hi), at + max(o, lo) - lo)
                for o in range(lo // BANK * BANK, hi, BANK)]

    assert (2 * U) % S == 0 and (2 * U) % W == 0
    with ExitStack() as s:
        q_sb = [c.sb(s, "q_sb", [R3, N], BF16) for _ in range(2)]
        k_sb = [c.sb(s, "k_sb", [R3, N], BF16) for _ in range(2)]
        v_sb = [c.sb(s, "v_sb", [P, T, 32], BF16) for _ in range(2)]
        slots = [c.ps(s, "score", [P, N // 2]) for _ in range(S)]
        sums = [c.ps(s, "sums", [P, BANK]) for _ in range(2)]
        rounded = [c.sb(s, "rounded", [P, N // 2], U8) for _ in range(W)]
        weights = [c.sb(s, "weights", [P, N // 2], BF16) for _ in range(W)]
        stage = [c.sb(s, "stage", [P, BANK]) for _ in range(2)]
        loaded = [c.sem("loaded0"), c.sem("loaded1")]
        scored, exped, clipped, used = c.sem("scored"), c.sem("exped"), c.sem("clipped"), c.sem("used")
        staged, stored = c.sem("staged"), [c.sem("stored0"), c.sem("stored1")]
        q_op, k_op = operands
        HEAD_PAIRS = H // 2
        with nc.Block() as block:
            @block.sync
            def _(sp):
                def loads(head, par, products, sums_):
                    wait(sp, used, sums_)
                    sp.dma_start(q_sb[par][0:R3, None, :], q_op[0:R3, bass.ds(head, 1), :]).then_inc(loaded[par], 16)
                    sp.dma_start(k_sb[par][0:R3, None, :], k_op[0:R3, bass.ds(head, 1), :]).then_inc(loaded[par], 16)
                    sp.dma_start(v_sb[par][:, None, :, :], values32[:, bass.ds(head, 1), :, :]).then_inc(loaded[par], 16)

                def store(head, par, n):
                    sp.wait_ge(staged, n)
                    sp.dma_start(out_rows[bass.ds(head, 1), :, :].rearrange("o p q -> (o p) q"), stage[par][:]).then_inc(stored[par], 16)

                loads(0, 0, 0, 0)
                loads(1, 1, 0, 0)
                with sp.Fori(0, HEAD_PAIRS - 1) as g:
                    for par in range(2):
                        loads(g * 2 + (2 + par), par, 0, g * (2 * U) + U * (par + 1))
                        store(g * 2 + par, par, g * 2 + (par + 1))
                for par in range(2):
                    store(H - 2 + par, par, H - 1 + par)
                for par in range(2):
                    sp.wait_ge(stored[par], 16 * HEAD_PAIRS)

            @block.tensor
            def _(pe):
                def score(g, i):
                    par, unit, slot = i // U % 2, units[i % U], i % S
                    if i % U == 0:
                        pe.wait_ge(loaded[par], (g + (i // U // 2 + 1)) * (16 * 3))
                    if not (isinstance(g, int) and g * 2 * U + i < S):
                        pe.wait_ge(exped, g * (2 * U) + (i - S + 1))
                    for segment in places(unit)[0]:
                        k = segment[0]
                        for _, a, b, at in pieces(segment):
                            has_diag = a <= k * P < b
                            last = pe.matmul(slots[slot][:, at:at + b - a], k_sb[par][0:R3, k * P:(k + 1) * P],
                                             q_sb[par][0:R3, a:b], start=True, stop=not has_diag)
                            if has_diag:
                                diag = at + k * P - a
                                last = pe.matmul(slots[slot][:, diag:diag + P], c.identb[:],
                                                 c.mask_kq[:, 0:P], start=False, stop=True)
                    last.then_inc(scored, 1)

                def add_up(g, i):
                    par, unit, slot = i // U, units[i % U], i % W
                    pe.wait_ge(clipped, g * (2 * U) + (i + 1))
                    if i % U == 0:
                        wait(pe, staged, g * 2 + (par - 1))
                    for segment in places(unit)[0]:
                        k = segment[0]
                        for j, a, b, at in pieces(segment):
                            last = pe.matmul(sums[par][32 * j:32 * j + 32, a - j * BANK:b - j * BANK],
                                             v_sb[par][:, k, :], weights[slot][:, at:at + b - a],
                                             start=(k == 0), stop=(k == 4 * j + 3), skip_group_check=True)
                    last.then_inc(used, 1)

                def pair(g, more):
                    for i in range(0, 2 * U, 2):
                        for j in (i + LAG, i + LAG + 1):
                            if more or j < 2 * U:
                                score(g, j)
                        add_up(g, i)
                        add_up(g, i + 1)

                for i in range(LAG):
                    score(0, i)
                pair(0, True)
                with pe.Fori(1, HEAD_PAIRS - 1) as g:
                    pair(g, True)
                pair(HEAD_PAIRS - 1, False)

            @block.scalar
            def _(act):
                def exp(g, i):
                    span = columns(units[i % U])
                    act.wait_ge(scored, g * (2 * U) + (i + 1))
                    if not (isinstance(g, int) and i < W):
                        act.wait_ge(clipped, g * (2 * U) + (i - W + 1))
                    nc.scalar.activation(rounded[i % W][:, span], slots[i % S][:, span],
                                         ACT.Exp).then_inc(exped, 1)

                for i in range(2 * U):
                    exp(0, i)
                with act.Fori(1, HEAD_PAIRS) as g:
                    for i in range(2 * U):
                        exp(g, i)

            @block.vector
            def _(dve):
                def clip(g, i):
                    span = columns(units[i % U])
                    dve.wait_ge(exped, g * (2 * U) + (i + 1))
                    if not (isinstance(g, int) and g * 2 * U + i < W):
                        dve.wait_ge(used, g * (2 * U) + (i - W + 1))
                    dve.tensor_scalar(weights[i % W][:, span], rounded[i % W][:, span],
                                      HALF - 1, None, ALU.min).then_inc(clipped, 1)

                def evacuate(g, par):
                    dve.wait_ge(used, g * (2 * U) + U * (par + 1))
                    wait(dve, stored[par], g * 16)
                    dve.tensor_copy(stage[par][:], sums[par][:]).then_inc(staged, 1)

                def pair(g, first, last):
                    for i in range(2 * U):
                        clip(g, i)
                        if i == LAG + 1 and not first:
                            evacuate(g - 1, 1)
                        if i == U + LAG + 1:
                            evacuate(g, 0)
                    if last:
                        evacuate(g, 1)

                pair(0, True, False)
                pair(1, False, False)
                with dve.Fori(2, HEAD_PAIRS - 1) as g:
                    pair(g, False, False)
                pair(HEAD_PAIRS - 1, False, True)


def layer0_attention(c, w_attn, b_attn, w_proj, b_proj):
    nc = c.nc
    q_op = c.dram("q_op", [R3, H, N], BF16)
    k_op = c.dram("k_op", [R3, H, N], BF16)
    sums = c.dram("sums", [H, P, BANK])
    scales = c.dram("scales", [H, N])
    with ExitStack() as s:
        wp = c.sb(s, "wp", [P, DT, D], BF16)
        b_proj_sb = c.sb(s, "b_proj_sb", [P, D])
        values = c.sb(s, "values", [P, T, D], BF16)
        with ExitStack() as s1:
            wq = c.sb(s1, "wq", [P, DT, 3 * D], BF16)
            hT = c.sb(s1, "hT", [P, DT, N], BF16)
            b_attn_sb = c.sb(s1, "b_attn_sb", [P, 3 * D])
            with ExitStack() as s2:
                h = c.sb(s2, "h", [P, T, D])
                hq = c.sb(s2, "hq", [P, T, D], BF16)
                wa = c.sb(s2, "wa", [P, DT, 3 * D])
                wo = c.sb(s2, "wo", [P, DT, D])
                loads = start_loads(c, [(wa[:], w_attn.rearrange("(k p) n -> p k n", p=P)),
                         (wo[:], w_proj.rearrange("(k p) n -> p k n", p=P)),
                         (b_attn_sb[:], row_of(b_attn, 3 * D)), (b_proj_sb[:], row_of(b_proj, D)),
                         ] + [(op[a:a + PARTS].rearrange("r (g h) n -> (r g) (h n)", g=8), c.ones_wide[0:8 * PARTS, :])
                              for op, a in ((q_op, R2), (k_op, R1))])
                layernorm(c, c.x, h)
                quantize(c, h, hq, T, D, D)
                finish_loads(c, loads)
                quantize(c, wa, wq, DT, 3 * D, 3 * D)
                quantize(c, wo, wp, DT, D, D)
                transpose_tiles(c, hq, hT, dt=BF16)
            qkv = [c.sb(s1, n, [P, T, D]) for n in ("q", "k", "v")]
            for i, dst in enumerate(qkv):
                project_tokens(c, hT, wq[:, :, i * D:(i + 1) * D], b_attn_sb[:, i * D:(i + 1) * D], D, T, N, dst)
            qd = c.sb(s1, "qd", [P, T, D], BF16)
            kd = c.sb(s1, "kd", [P, T, D], BF16)
            quantize(c, qkv[0], qd, T, D, HD, fold=HD ** -0.5, by_element=True)
            quantize(c, qkv[1], kd, T, D, HD, rows_first=True, by_element=True)
            quantize(c, qkv[2], values, T, D, HD)
            transposed_to_dram(c, [(qd, q_op), (kd, k_op)])
        c.recycle()
        HT = H * T
        values32 = c.sb(s, "values32", [P, H, T, 32], BF16)
        shift, total, logs = c.sb(s, "shift", [P, HT]), c.sb(s, "total", [P, HT]), c.sb(s, "logs", [P, HT])
        scale, low, step = c.sb(s, "scale", [P, HT]), c.sb(s, "low", [P, HT]), c.sb(s, "step", [P, HT])
        top = c.sb(s, "top", [P, HT])

        def small(*steps):
            chain = c.sem("chain")
            order = list(enumerate(steps))
            with nc.Block() as block:
                def run(eng, mine):
                    for i, (who, f) in order:
                        if who == mine:
                            wait(eng, chain, i)
                            f(eng).then_inc(chain, 1)

                @block.vector
                def _(dve):
                    run(dve, "dve")

                @block.scalar
                def _(act):
                    run(act, "act")

                @block.gpsimd
                def _(pool):
                    run(pool, "pool")

        act = lambda out, in_, f, **k: ("act", lambda e: nc.scalar.activation(out, in_, f, **k))
        two = lambda out, a, b, op: ("dve", lambda e: e.tensor_tensor(out, a, b, op))
        one = lambda out, a, v, op: ("dve", lambda e: e.tensor_scalar(out, a, v, None, op))

        def scale_of(m):
            return [act(scale[:], m, ACT.Exp), one(scale[:], scale[:], TINY_SCALE, ALU.max),
                    ("dve", lambda e: e.tensor_scalar(low[:].bitcast(I32), scale[:].bitcast(I32), 0x7F800000, None,
                                                      ALU.bitwise_and)),
                    two(step[:], scale[:], low[:], ALU.is_gt),
                    ("dve", lambda e: e.scalar_tensor_tensor(scale[:], step[:], 1.0, low[:], ALU.add, ALU.mult))]

        with ExitStack() as s1:
            lows, sums1 = c.sb(s1, "lows", [P, HT * NWIDE]), c.sb(s1, "sums", [P, HT * NWIDE])
            by_chunk = lambda a: a[:].rearrange("p (i c) -> p i c", c=NWIDE)
            small(("dve", lambda e: e.memset(lows[:], -BIG)), ("dve", lambda e: e.memset(sums1[:], 0.0)))
            causal_stats(c, (q_op, k_op), lows, sums1)
            small(("dve", lambda e: e.tensor_reduce(shift[:], by_chunk(lows), X, ALU.min)),
                  two(by_chunk(lows), shift[:, :, None].to_broadcast([P, HT, NWIDE]), by_chunk(lows), ALU.subtract),
                  act(lows[:], lows[:], ACT.Exp), two(sums1[:], sums1[:], lows[:], ALU.mult),
                  ("dve", lambda e: e.tensor_reduce(total[:], by_chunk(sums1), X, ALU.add)),
                  act(logs[:], total[:], ACT.Ln), two(shift[:], shift[:], logs[:], ALU.subtract))
        split_rows(c, shift[:], [q_op[R1 + i] for i in range(PARTS)])
        causal_maxima(c, (q_op, k_op), R2, True, top)
        by_tile = scale[:].rearrange("p (h t) -> p h t", h=H)
        small(*scale_of(top[:]), act(logs[:], scale[:], ACT.Ln), one(logs[:], logs[:], -1.0, ALU.mult),
              ("dve", lambda e: e.memset(values32[:], 0.0)),
              ("dve", lambda e: e.tensor_tensor(values32[:, :, :, 0:HD],
                                                values[:, :, :].rearrange("p t (h e) -> p h t e", e=HD),
                                                by_tile[:, :, :, None].to_broadcast([P, H, T, HD]), ALU.mult)))
        split_rows(c, logs[:], [k_op[R2 + i] for i in range(PARTS)])
        causal_maxima(c, (q_op, k_op), R3, False, top)
        small(*scale_of(top[:]), one(scale[:], scale[:], 1.0 / HALF, ALU.mult), act(logs[:], scale[:], ACT.Ln),
              two(shift[:], shift[:], logs[:], ALU.subtract))
        split_rows(c, shift[:], [q_op[R1 + i] for i in range(PARTS)])
        rows_to_dram(c, scale[:], scales)
        causal_weights(c, (q_op, k_op), values32, sums)
        quantized_output(c, sums, scales, wp, b_proj_sb)


def rows_to_dram(c, values, out):
    nc = c.nc
    W = H * T
    with ExitStack() as s:
        ps = c.ps(s, "turned", [P, W // P, P])
        sb = c.sb(s, "turned", [P, W // P, P])
        turned, copied, stored = c.sem("turned"), c.sem("copied"), c.sem("stored")
        with nc.Block() as block:
            @block.tensor
            def _(pe):
                for b in range(W // P):
                    last = pe.transpose(ps[:, b, :], values[:, b * P:(b + 1) * P], c.identf[:])
                last.then_inc(turned, 1)

            @block.vector
            def _(dve):
                dve.wait_ge(turned, 1)
                dve.tensor_copy(sb[:], ps[:]).then_inc(copied, 1)

            @block.sync
            def _(sp):
                sp.wait_ge(copied, 1)
                sp.dma_start(out.rearrange("h (t q) -> (h t) q", q=P).rearrange("(b r) q -> r b q", r=P),
                             sb[:]).then_inc(stored, 16)
                sp.wait_ge(stored, 16)


def quantized_output(c, sums, scales, wp, bias):
    nc = c.nc
    with ExitStack() as s:
        oT = c.sb(s, "oT", [P, DT, N])
        by_query = c.sb(s, "by_query", [P, DT, N])
        o = c.sb(s, "o", [P, T, D])
        oq = c.sb(s, "oq", [P, T, D], BF16)
        oqT = c.sb(s, "oqT", [P, DT, N], BF16)
        col, cl, cs, ci = (c.sb(s, n, [P, DT]) for n in ("col", "cl", "cs", "ci"))
        row, rl, rs = (c.sb(s, n, [P, T]) for n in ("row", "rl", "rs"))
        load(c, [job for jobs in zip(sums_by_head(sums, oT), rows_by_head(scales, by_query)) for job in jobs])
        chain = c.sem("chain")
        with nc.Block() as block:
            @block.vector
            def _(dve):
                line = Line(dve, chain)
                line(dve.tensor_tensor(oT[:], oT[:], by_query[:], ALU.mult))
                line(dve.tensor_reduce(col[:], oT[:], X, ALU.max, apply_absolute_value=True))
                ceil_pow2(line, dve, col[:], cl[:], cs[:])
                line(dve.reciprocal(ci[:], col[:]))
        transpose_tiles_back(c, oT, o, ci)
        rows_scaled = c.sem("rows_scaled")
        with nc.Block() as block:
            @block.vector
            def _(dve):
                line = Line(dve, rows_scaled)
                line(dve.tensor_reduce(row[:], o[:], X, ALU.max, apply_absolute_value=True))
                ceil_pow2(line, dve, row[:], rl[:], rs[:])
                line(dve.reciprocal(rl[:], row[:]))
                line(dve.tensor_scalar(rl[:], rl[:], HALF, None, ALU.mult))
                line(dve.tensor_tensor(o[:], o[:], rl[:, :, None].to_broadcast([P, T, D]), ALU.mult))
                line(dve.tensor_scalar(o[:], o[:], MAGIC, MAGIC + HALF - 1, ALU.add, ALU.min))
                line(dve.tensor_scalar(oq[:], o[:], MAGIC, None, ALU.subtract))
                line(dve.tensor_scalar(row[:], row[:], 1.0 / HALF, None, ALU.mult))
        transpose_tiles(c, oq, oqT, dt=BF16, scale=col)
        project_tokens(c, oqT, wp, bias, D, T, N, c.x, scale=row, residual=c.x)


def sums_by_head(sums, oT):
    return [(oT[h % HALF_HEADS * HD:(h % HALF_HEADS + 1) * HD, h // HALF_HEADS, :]
             .rearrange("p (j q) -> p j q", q=BANK),
             sums[h].rearrange("(j r) q -> r j q", r=32)[0:HD]) for h in range(H)]


def rows_by_head(rows, out):
    return [(out[h % HALF_HEADS * HD:(h % HALF_HEADS + 1) * HD, h // HALF_HEADS, :],
             rows[h:h + 1, :].to_broadcast([HD, N])) for h in range(H)]


def transpose_tiles_back(c, src, dst, scale):
    nc = c.nc
    with ExitStack() as s:
        slots = [c.ps(s, "tp", [P, 2 * D]) for _ in range(4)]
        scaled, turned, copied = c.sem("scaled"), c.sem("turned"), c.sem("copied")
        with nc.Block() as block:
            @block.scalar
            def _(act):
                for h in range(DT):
                    nc.scalar.activation(src[:, h, :], src[:, h, :], ACT.Copy, scale=scale[:, h:h + 1]).then_inc(scaled, 1)

            @block.tensor
            def _(pe):
                pe.wait_ge(scaled, DT)
                for i in range(T // 2):
                    if i >= 4:
                        pe.wait_ge(copied, i - 3)
                    for t in range(2):
                        for h in range(DT):
                            last = pe.transpose(slots[i % 4][:, t * D + h * P:t * D + (h + 1) * P],
                                                src[:, h, (2 * i + t) * P:(2 * i + t + 1) * P], c.identf[:])
                    last.then_inc(turned, 1)

            @block.vector
            def _(dve):
                for i in range(T // 2):
                    dve.wait_ge(turned, i + 1)
                    dve.tensor_copy(dst[:, 2 * i:2 * i + 2, :],
                                    slots[i % 4][:].rearrange("p (t d) -> p t d", t=2)).then_inc(copied, 1)


def project_features(c, lhs, rhs, bias, cols, dst, scale=1.0):
    nc = c.nc
    jobs = [(h, o, min(BANK, cols - o)) for h in range(DT) for o in range(0, cols, BANK)]
    with ExitStack() as s:
        slots = [c.ps(s, "prod", [P, BANK]) for _ in range(4)]
        scaled = c.sb(s, "scaled", [P, DT])
        multiplied, bias_ready = c.sem("multiplied"), c.sem("bias_ready")
        added = [c.sem("added_dve"), c.sem("added_act")]
        with nc.Block() as block:
            @block.tensor
            def _(pe):
                for i, (h, o, w) in enumerate(jobs):
                    if i >= 4:
                        pe.wait_ge(added[i % 2], (i - 4) // 2 + 1)
                    for k in range(DT):
                        last = pe.matmul(slots[i % 4][:, 0:w], lhs[:, k, h * P:(h + 1) * P],
                                         rhs[:, k, o:o + w], start=(k == 0), stop=(k == DT - 1))
                    last.then_inc(multiplied, 1)

            @block.vector
            def _(dve):
                dve.tensor_scalar(scaled[:], bias[:], scale, None, ALU.mult).then_inc(bias_ready, 1)
                dve.wait_ge(bias_ready, 1)
                for i in range(0, len(jobs), 2):
                    h, o, w = jobs[i]
                    dve.wait_ge(multiplied, i + 1)
                    dve.tensor_scalar(dst[:, h, o:o + w], slots[i % 4][:, 0:w], scale, scaled[:, h:h + 1],
                                      ALU.mult, ALU.add).then_inc(added[0], 1)

            @block.scalar
            def _(act):
                act.wait_ge(bias_ready, 1)
                for i in range(1, len(jobs), 2):
                    h, o, w = jobs[i]
                    act.wait_ge(multiplied, i + 1)
                    nc.scalar.activation(dst[:, h, o:o + w], slots[i % 4][:, 0:w], ACT.Identity,
                                         bias=scaled[:, h:h + 1], scale=scale).then_inc(added[1], 1)


def split_to_dram(c, src, cols, parts, order):
    nc = c.nc
    step = 2 * BANK
    jobs = [(h, o, min(step, cols - o)) for h in range(DT) for o in range(0, cols, step)]
    J = len(jobs)
    rows = parts.rearrange("(a f e) h n -> f a (e h) n", a=PARTS, f=DT)
    with ExitStack() as s:
        part = c.sb(s, "part", [P, J, PARTS, step], BF16)
        rest = c.sb(s, "rest", [P, 2, step])
        high, middle, rested, low, stored = (c.sem("high"), c.sem("middle"), c.sem("rested"), c.sem("low"),
                                             c.sem("stored"))
        with nc.Block() as block:
            @block.scalar
            def _(act):
                for i, (h, o, w) in enumerate(jobs):
                    nc.scalar.activation(part[:, i, order[0], 0:w], src[:, h, o:o + w], ACT.Copy).then_inc(high, 1)

            @block.vector
            def _(dve):
                for i, (h, o, w) in enumerate(jobs):
                    dve.wait_ge(high, i + 1)
                    if i >= 2:
                        dve.wait_ge(low, i - 1)
                    dve.tensor_tensor(rest[:, i % 2, 0:w], src[:, h, o:o + w], part[:, i, order[0], 0:w],
                                      ALU.subtract).then_inc(rested, 1)
                    dve.wait_ge(rested, i + 1)
                    dve.tensor_copy(part[:, i, order[1], 0:w], rest[:, i % 2, 0:w]).then_inc(middle, 1)

            @block.gpsimd
            def _(pool):
                for i, (h, o, w) in enumerate(jobs):
                    pool.wait_ge(middle, i + 1)
                    pool.tensor_tensor(part[:, i, order[2], 0:w], rest[:, i % 2, 0:w], part[:, i, order[1], 0:w],
                                       ALU.subtract).then_inc(low, 1)

            @block.sync
            def _(sp):
                for i, (h, o, w) in enumerate(jobs):
                    sp.wait_ge(low, i + 1)
                    sp.dma_start(rows[h, :, :, o:o + w].rearrange("a p n -> p a n"),
                                 part[:, i, :, 0:w]).then_inc(stored, 16)
                sp.wait_ge(stored, 16 * J)


Q_ORDER, K_ORDER = (0, 1, 2), (2, 1, 0)
RUNS = [(0, 0, 0, 3), (3, 0, 1, 2), (5, 0, 2, 1)]
PAIR_LOADS = 2 * len(RUNS)


def load_pairs(eng, q_dst, k_dst, q_parts, k_parts, head, sem):
    for at, q_first, k_first, n in RUNS:
        for dst, parts, first in ((q_dst, q_parts, q_first), (k_dst, k_parts, k_first)):
            eng.dma_start(dst[at * HD:(at + n) * HD, None, :],
                          parts[first * HD:(first + n) * HD, bass.ds(head, 1), :]).then_inc(sem, 16)


def scratch_by_element(c, v):
    out = c.dram(c.unique("by_element"), [D])
    elements = out.rearrange("(e h o) -> e h o", e=HD, o=1)
    if v.shape[0] == D:
        return out, (elements, v.rearrange("(h e o) -> e h o", e=HD, o=1))
    return out, (elements, v.rearrange("(e h o) -> e h o", h=1, o=1).to_broadcast([HD, H, 1]))


def order_by_element(c, pairs):
    nc = c.nc
    ordered = c.sem("ordered")
    with nc.Block() as block:
        @block.vector
        def _(dve):
            for dst, src in pairs:
                dve.tensor_copy(dst[:, :, :].rearrange("p t (e h) -> p t h e", e=HD),
                                src[:, :, :].rearrange("p t (h e) -> p t h e", e=HD)).then_inc(ordered, 1)
            dve.wait_ge(ordered, len(pairs))


class Step:

    def __init__(self, g, o):
        self.head, self.slot, self.prior = g * 3 + o, o % 3, g + o // 3


def cross_attention(c, q_parts, k_parts, values, out_rows):
    nc = c.nc
    CHUNKS = 4
    edges = [M * i // CHUNKS for i in range(CHUNKS + 1)]
    NA = T * CHUNKS
    NB = MT * CH
    SA, SB, SP = 4, 3, 3
    LEAD = 4 * CHUNKS
    BEHIND = 1
    mrows = c.dram(c.unique("mrows"), [3, PARTS, N], BF16)
    with ExitStack() as s:
        q_sb = [c.sb(s, "q_sb", [SRM, N], BF16) for _ in range(3)]
        k_sb = [c.sb(s, "k_sb", [SRM, M], BF16) for _ in range(3)]
        v_sb = [c.sb(s, "v_sb", [P, MT, 32]) for _ in range(3)]
        a_slots = [c.ps(s, "a_score", [P, BANK]) for _ in range(SA)]
        b_slots = [c.ps(s, "b_score", [P, BANK]) for _ in range(SB)]
        sums = c.ps(s, "sums", [P, BANK])
        probs = [[c.sb(s, "probs", [P, BANK]) for _ in range(CH)] for _ in range(SP)]
        maxima = c.sb(s, "maxima", [P, T, CHUNKS])
        shift, rest = c.sb(s, "shift", [P, T]), c.sb(s, "rest", [P, T])
        part = c.sb(s, "part", [P, PARTS, 32], BF16)
        turned = [c.sb(s, "turned", [P, PARTS, 32], BF16) for _ in range(3)]
        stage = [c.sb(s, "stage", [P, BANK]) for _ in range(3)]
        loaded, shift_stored, shift_loaded, stored = ([c.sem(f"{n}{i}") for i in range(3)] for n in
                                                      ("loaded", "shift_stored", "shift_loaded", "stored"))
        a_scored, a_maxed, scored, exped, used = (c.sem(n) for n in ("a_scored", "a_maxed", "scored", "exped", "used"))
        chain, shift_ready, staged, ones_set, pad_set = (c.sem(n) for n in ("chain", "shift_ready", "staged", "ones_set", "pad_set"))
        LOADS = PAIR_LOADS + 1
        LINKS = 5
        quarter = P // 32

        def over_steps(eng, step, first, last):
            first()
            for o in range(1, 4):
                step(Step(0, o), Step(0, o - 1), Step(0, o + 1))
            with eng.Fori(1, (H - 1) // 3 - 1) as g:
                for o in range(1, 4):
                    step(Step(g, o), Step(g, o - 1), Step(g, o + 1))
            g = (H - 1) // 3 - 1
            for o in range(1, 4):
                step(Step(g, o), Step(g, o - 1), Step(g, o + 1) if o < 3 else None)
            last()

        def maxima_chunks(a, ahead):
            return [(a, n) for n in range(LEAD, NA)] + ([(ahead, n) for n in range(LEAD)] if ahead else [])

        with nc.Block() as block:
            @block.sync
            def _(sp):
                def loads(a):
                    wait(sp, used, (a.head - 2) * MT)
                    load_pairs(sp, q_sb[a.slot], k_sb[a.slot], q_parts, k_parts, a.head, loaded[a.slot])
                    sp.dma_start(v_sb[a.slot][:, None, :, :],
                                 values[:, bass.ds(a.head, 1), :, :]).then_inc(loaded[a.slot], 16)

                def shifts(a):
                    wait(sp, shift_loaded[a.slot], a.prior * 16)
                    sp.wait_ge(shift_ready, a.head + 1)
                    rows = mrows[a.slot].rearrange("a (t b q) -> t b a q", b=quarter, q=32)
                    for b in range(quarter):
                        sp.dma_start(rows[:, b, :, :], turned[a.slot][32 * b:32 * b + T, :, :])\
                            .then_inc(shift_stored[a.slot], 16)
                    sp.wait_ge(shift_stored[a.slot], (a.prior + 1) * (16 * quarter))
                    sp.dma_start(q_sb[a.slot][SR:SRM, :], mrows[a.slot]).then_inc(shift_loaded[a.slot], 16)

                loads(Step(0, 0))
                loads(Step(0, 1))
                shifts(Step(0, 0))
                for o in range(1, 4):
                    loads(Step(0, o + 1))
                    shifts(Step(0, o))
                with sp.Fori(1, (H - 1) // 3 - 1) as g:
                    for o in range(1, 4):
                        loads(Step(g, o + 1))
                        shifts(Step(g, o))
                g = (H - 1) // 3 - 1
                for o in range(1, 4):
                    if o < 3:
                        loads(Step(g, o + 1))
                    shifts(Step(g, o))

            @block.gpsimd
            def _(pool):
                for k in range(3):
                    pool.memset(k_sb[k][SR:SRM, :], 1.0).then_inc(ones_set, 1)
                pool.wait_ge(ones_set, 3)
                pool.memset(part[:], 0.0).then_inc(pad_set, 1)

                def store(b):
                    pool.wait_ge(staged, b.head + 1)
                    pool.dma_start(out_rows[bass.ds(b.head, 1), :, :].rearrange("o p q -> (o p) q"),
                                   stage[b.slot][:]).then_inc(stored[b.slot], 16)

                over_steps(pool, lambda a, b, ahead: store(b), lambda: None, lambda: store(Step(0, H - 1)))
                for k in range(3):
                    pool.wait_ge(stored[k], 16 * len(range(k, H, 3)))

            @block.tensor
            def _(pe):
                def maxima_scores(a, n):
                    t, ch = n // CHUNKS, n % CHUNKS
                    if n == 0:
                        pe.wait_ge(loaded[a.slot], (a.prior + 1) * (16 * LOADS))
                    wait(pe, a_maxed, a.head * NA + (n - SA + 1))
                    lo, hi = edges[ch], edges[ch + 1]
                    pe.matmul(a_slots[(a.slot * NA + n) % SA][:, 0:hi - lo], q_sb[a.slot][0:SR, t * P:(t + 1) * P],
                              k_sb[a.slot][0:SR, lo:hi], start=True, stop=True).then_inc(a_scored, 1)

                def scores(b, k, j):
                    u = k * CH + j
                    n = min(P, M - k * P)
                    if u == 0:
                        pe.wait_ge(shift_loaded[b.slot], (b.prior + 1) * 16)
                    wait(pe, exped, b.head * NB + (u - SB + 1))
                    pe.matmul(b_slots[(b.slot * NB + u) % SB][0:n, :], k_sb[b.slot][0:SRM, k * P:k * P + n],
                              q_sb[b.slot][0:SRM, j * BANK:(j + 1) * BANK], start=True, stop=True).then_inc(scored, 1)

                def add_up(b, k):
                    n = min(P, M - k * P)
                    if k == 0:
                        wait(pe, staged, b.head)
                    for j in range(CH):
                        pe.wait_ge(exped, b.head * NB + (k * CH + j + 1))
                        last = pe.matmul(sums[32 * j:32 * j + 32, :], v_sb[b.slot][0:n, k, :],
                                         probs[(b.slot * MT + k) % SP][j][0:n, :], start=(k == 0), stop=(k == MT - 1),
                                         skip_group_check=True)
                    last.then_inc(used, 1)

                events = []
                for k in range(MT):
                    for j in range(CH):
                        events.append(("s", k, j))
                    if k >= BEHIND:
                        events.append(("p", k - BEHIND, 0))
                events += [("p", k, 0) for k in range(MT - BEHIND, MT)]

                def step(a, b, ahead):
                    chunks = maxima_chunks(a, ahead) if a else []
                    done = 0
                    for e, (what, k, j) in enumerate(events):
                        due = len(chunks) * (e + 1) // len(events)
                        for head, n in chunks[done:due]:
                            maxima_scores(head, n)
                        done = due
                        if what == "s":
                            scores(b, k, j)
                        else:
                            add_up(b, k)

                def first():
                    pe.wait_ge(ones_set, 3)
                    for n in range(LEAD):
                        maxima_scores(Step(0, 0), n)
                    for head, n in maxima_chunks(Step(0, 0), Step(0, 1)):
                        maxima_scores(head, n)

                over_steps(pe, step, first, lambda: step(None, Step(0, H - 1), None))

            @block.scalar
            def _(act):
                def exps(b):
                    for u in range(NB):
                        k, j = u // CH, u % CH
                        n = min(P, M - k * P)
                        act.wait_ge(scored, b.head * NB + (u + 1))
                        wait(act, used, b.head * MT + (k - SP + 1))
                        nc.scalar.activation(probs[(b.slot * MT + k) % SP][j][0:n, :], b_slots[(b.slot * NB + u) % SB][0:n, :],
                                             ACT.Exp).then_inc(exped, 1)

                over_steps(act, lambda a, b, ahead: exps(b), lambda: None, lambda: exps(Step(0, H - 1)))

            @block.vector
            def _(dve):
                def maximum(a, n):
                    t, ch = n // CHUNKS, n % CHUNKS
                    dve.wait_ge(a_scored, a.head * NA + (n + 1))
                    w = edges[ch + 1] - edges[ch]
                    dve.tensor_reduce(maxima[:, t, ch:ch + 1], a_slots[(a.slot * NA + n) % SA][:, 0:w], X, ALU.max).then_inc(a_maxed, 1)

                def negate_and_split(a):
                    at = [0]

                    def link(ins):
                        at[0] += 1
                        ins.then_inc(chain, 1)
                        dve.wait_ge(chain, a.head * LINKS + at[0])

                    dve.wait_ge(a_maxed, a.head * NA + NA)
                    link(dve.tensor_reduce(shift[:], maxima[:], X, ALU.max, negate=True))
                    link(dve.tensor_copy(part[:, 0, 0:T], shift[:]))
                    link(dve.tensor_tensor(rest[:], shift[:], part[:, 0, 0:T], ALU.subtract))
                    link(dve.tensor_copy(part[:, 1, 0:T], rest[:]))
                    link(dve.tensor_tensor(part[:, 2, 0:T], rest[:], part[:, 1, 0:T], ALU.subtract))
                    wait(dve, shift_stored[a.slot], a.prior * (16 * quarter))
                    dve.transpose(turned[a.slot][:].rearrange("p a q -> p (a q)"),
                                  part[:].rearrange("p a q -> p (a q)")).then_inc(shift_ready, 1)

                def evacuate(b):
                    dve.wait_ge(used, b.head * MT + MT)
                    wait(dve, stored[b.slot], b.prior * 16)
                    dve.tensor_copy(stage[b.slot][:], sums[:]).then_inc(staged, 1)

                def step(a, b, ahead):
                    for head, n in maxima_chunks(a, ahead):
                        maximum(head, n)
                        if head is a and n == NA - 1:
                            negate_and_split(a)
                    if b:
                        evacuate(b)

                def first():
                    dve.wait_ge(pad_set, 1)
                    for n in range(LEAD):
                        maximum(Step(0, 0), n)
                    step(Step(0, 0), None, Step(0, 1))

                over_steps(dve, step, first, lambda: evacuate(Step(0, H - 1)))


def attention_output(c, sums, w, bias):
    nc = c.nc
    inverse_rows = c.dram(c.unique("inverse_rows"), [H, N])
    with ExitStack() as s:
        oT = c.sb(s, "oT", [P, DT, N])
        inverses = c.sb(s, "inverses", [P, DT, N])
        totals, inverse = (c.sb(s, n, [H * CH, BANK]) for n in ("totals", "inverse"))
        totals_loaded, inverted, stored, weighted = (c.sem(n) for n in ("totals_loaded", "inverted", "stored", "weighted"))
        sums_loaded, inverses_loaded = ([c.sem(f"{n}{h}") for h in range(DT)] for n in ("sums_loaded", "inverses_loaded"))
        with nc.Block() as block:
            @block.sync
            def _(sp):
                sp.dma_start(totals[:], sums.rearrange("h (j r) q -> (h j) r q", r=32)[:, HD, :])\
                    .then_inc(totals_loaded, 16)
                sp.wait_ge(inverted, 1)
                sp.dma_start(inverse_rows.rearrange("h (j q) -> (h j) q", q=BANK), inverse[:]).then_inc(stored, 16)
                sp.wait_ge(stored, 16)
                for h, (dst, src) in enumerate(rows_by_head(inverse_rows, inverses)):
                    sp.dma_start(dst, src).then_inc(inverses_loaded[h // HALF_HEADS], 16)

            @block.scalar
            def _(act):
                for h, (dst, src) in enumerate(sums_by_head(sums, oT)):
                    act.dma_start(dst, src).then_inc(sums_loaded[h // HALF_HEADS], 16)

            @block.vector
            def _(dve):
                dve.wait_ge(totals_loaded, 16)
                dve.reciprocal(inverse[:], totals[:]).then_inc(inverted, 1)
                for half in range(DT):
                    dve.wait_ge(sums_loaded[half], 16 * HALF_HEADS)
                    dve.wait_ge(inverses_loaded[half], 16 * HALF_HEADS)
                    dve.tensor_tensor(oT[:, half, :], oT[:, half, :], inverses[:, half, :], ALU.mult).then_inc(weighted, 1)
                dve.wait_ge(weighted, DT)
        project_tokens(c, oT, w, bias, D, T, N, c.x, residual=c.x)


def values_with_ones(c, v, out, tiles):
    nc = c.nc
    filled, placed = c.sem("filled"), c.sem("placed")
    with nc.Block() as block:
        @block.vector
        def _(dve):
            dve.memset(out[:, :, :, HD:2 * HD], 1.0).then_inc(filled, 1)
            dve.tensor_copy(out[:, :, :, 0:HD], v[:].rearrange("p t (h e) -> p h t e", e=HD)).then_inc(placed, 1)
            dve.wait_ge(filled, 1)
            dve.wait_ge(placed, 1)


def zero(c, buf):
    nc = c.nc
    zeroed = c.sem("zeroed")
    with nc.Block() as block:
        @block.gpsimd
        def _(pool):
            pool.memset(buf, 0.0).then_inc(zeroed, 1)
            pool.wait_ge(zeroed, 1)


def by_feature(dst, v):
    return [(dst[:, h:h + 1], v.rearrange("(h p o) -> h p o", p=P, o=1)[h]) for h in range(DT)]


def cross_layer(c, name, ctx_in, ws, bs, transposed):
    nc = c.nc
    q_parts = c.dram(f"{name}_q_parts", [PARTS * HD, H, N], BF16)
    k_parts = c.dram(f"{name}_k_parts", [PARTS * HD, H, M], BF16)
    sums = c.dram(f"{name}_sums", [H, P, BANK])
    with ExitStack() as s:
        w_sb = [c.sb(s, n, [P, DT, D]) for n in ("wq", "wk", "wv", "wo")]
        bq, bk = c.sb(s, "bq", [P, DT]), c.sb(s, "bk", [P, DT])
        bv, bo = c.sb(s, "bv", [P, D]), c.sb(s, "bo", [P, D])
        scratch, fills = zip(*(scratch_by_element(c, v) for v in bs[0:2]))
        jobs = list(fills) + [(bv[:], row_of(bs[2], D)), (bo[:], row_of(bs[3], D))]
        ordered = [c.sb(s, n, [P, DT, D]) for n in ("wq_ordered", "wk_ordered")]
        weights = [c.sb(s, "raw", [P, DT, D]) for _ in range(4)] if transposed else w_sb
        values = c.sb(s, "values", [P, H, MT, 32])
        ctx = c.sb(s, "ctx", [P, MT, D])
        full = (MT - 1) * P
        with nc.allow_non_contiguous_dma(reason="the biases' two times 256 elements"):
            loads = start_loads(c, [(r[:], w.rearrange("(k p) n -> p k n", p=P)) for r, w in zip(weights, ws)] + jobs +
                                [(ctx[:, 0:MT - 1, :], ctx_in[0, 0:full, :].rearrange("(t p) d -> p t d", p=P)),
                                 (ctx[0:M - full, MT - 1, :], ctx_in[0, full:M, :])])
        with ExitStack() as s1:
            hT = c.sb(s1, "hT", [P, DT, N])
            with ExitStack() as s2:
                h = c.sb(s2, "h", [P, T, D])
                norm_and_turn(c, c.x, hT, h)
            finish_loads(c, loads)
            bias_loads = start_loads(c, by_feature(bq, scratch[0]) + by_feature(bk, scratch[1]))
            if transposed:
                for r, w in zip(weights, w_sb):
                    transpose_tiles(c, r, w, tiles=DT, rows=D)
            order_by_element(c, list(zip(ordered, w_sb[0:2])))
            finish_loads(c, bias_loads)
            qT = c.sb(s1, "qT", [P, DT, N])
            project_features(c, ordered[0], hT, bq, N, qT, scale=HD ** -0.5)
            split_to_dram(c, qT, N, q_parts, Q_ORDER)
        with ExitStack() as s1:
            ctxT = c.sb(s1, "ctxT", [P, DT, M])
            transpose_tiles(c, ctx, ctxT, tiles=MT, rows=M)
            with ExitStack() as s2:
                v = c.sb(s2, "v", [P, MT, D])
                zero(c, v[:, MT - 1, :])
                project_tokens(c, ctxT, w_sb[2], bv, D, MT, M, v)
                values_with_ones(c, v, values, MT)
            with ExitStack() as s2:
                kT = c.sb(s2, "kT", [P, DT, M])
                project_features(c, ordered[1], ctxT, bk, M, kT)
                split_to_dram(c, kT, M, k_parts, K_ORDER)
        cross_attention(c, q_parts, k_parts, values, sums)
        attention_output(c, sums, w_sb[3], bo)


E = 8
HID = 1024
MH = HID // P
CAP = int(N / E * 1.25)
ST = (CAP + P - 1) // P


def route(c, gates, scatter_at, gather_at, weight):
    nc = c.nc
    with ExitStack() as s:
        best = c.sb(s, "best", [P, T, 8])
        index = c.sb(s, "index", [P, T, 8], U32)
        number_i, number = c.sb(s, "number_i", [P, E], I32), c.sb(s, "number", [P, E])
        token_i, token = c.sb(s, "token_i", [P, T], I32), c.sb(s, "token", [P, T])
        which = [c.sb(s, "which", [P, T]) for _ in range(2)]
        chosen = [c.sb(s, "chosen", [P, T, E]) for _ in range(2)]
        label = c.sb(s, "label", [P, T, E], BF16)
        before = c.sb(s, "before", [P, T, E])
        place = c.sb(s, "place", [P, T, E])
        masked = c.sb(s, "masked", [P, T, E])
        seat, fits, row, back = (c.sb(s, n, [P, T]) for n in ("seat", "fits", "row", "back"))
        gap, ratio, one = (c.sb(s, n, [P, T]) for n in ("gap", "ratio", "one"))
        counts = c.ps(s, "counts", [P, T, E])
        totals = c.ps(s, "totals", [P, T, E])
        chain, numbered, labelled, counted = (c.sem(n) for n in ("chain", "numbered", "labelled", "counted"))
        gap_ready, ratio_ready, topped = c.sem("gap_ready"), c.sem("ratio_ready"), c.sem("topped")
        spread = lambda a: a[:, :, None].to_broadcast([P, T, E])
        with nc.Block() as block:
            @block.gpsimd
            def _(pool):
                pool.iota(number_i[:], pattern=[[1, E]], base=0, channel_multiplier=0).then_inc(numbered, 1)
                pool.iota(token_i[:], pattern=[[P, T]], base=0, channel_multiplier=1).then_inc(numbered, 1)

            @block.tensor
            def _(pe):
                pe.wait_ge(labelled, 1)
                pe.matmul(counts[:], c.triu[:], label[:], start=True, stop=True)
                pe.matmul(totals[:], c.onesb[:], label[:], start=True, stop=True).then_inc(counted, 1)

            @block.scalar
            def _(act):
                act.wait_ge(gap_ready, 1)
                nc.scalar.activation(ratio[:], gap[:], ACT.Exp).then_inc(ratio_ready, 1)

            @block.vector
            def _(dve):
                line = Line(dve, chain)
                for t in range(T):
                    dve.max(best[:, t, :], gates[:, t, :]).then_inc(topped, 1)
                for t in range(T):
                    dve.wait_ge(topped, t + 1)
                    last = dve.max_index(index[:, t, :], best[:, t, :], gates[:, t, :])
                line(last)
                dve.tensor_tensor(gap[:], best[:, :, 1], best[:, :, 0], ALU.subtract).then_inc(gap_ready, 1)
                dve.wait_ge(numbered, 2)
                line(dve.tensor_copy(number[:], number_i[:]))
                line(dve.tensor_copy(token[:], token_i[:]))
                for k in range(2):
                    line(dve.tensor_copy(which[k][:], index[:, :, k]))
                    line(dve.tensor_tensor(chosen[k][:], number[:, None, :].to_broadcast([P, T, E]), spread(which[k]),
                                           ALU.is_equal))
                dve.tensor_tensor(label[:], chosen[0][:], chosen[1][:], ALU.add).then_inc(labelled, 1)
                line(dve.memset(before[:, 0, :], 0.0))
                dve.wait_ge(counted, 1)
                for t in range(1, T):
                    line(dve.tensor_tensor(before[:, t, :], before[:, t - 1, :], totals[:, t - 1, :], ALU.add))
                line(dve.tensor_tensor(place[:], counts[:], before[:], ALU.add))
                for k in range(2):
                    line(dve.tensor_tensor(masked[:], place[:], chosen[k][:], ALU.mult))
                    line(dve.tensor_reduce(seat[:], masked[:], X, ALU.add))
                    line(dve.tensor_scalar(fits[:], seat[:], float(CAP), None, ALU.is_le))
                    line(dve.scalar_tensor_tensor(row[:], which[k][:], float(CAP), seat[:], ALU.mult, ALU.add))
                    line(dve.tensor_scalar(back[:], token[:], float(E * CAP + k * N), None, ALU.add))
                    line(dve.scalar_tensor_tensor(row[:], row[:], -1.0, back[:], ALU.add, ALU.subtract))
                    line(dve.tensor_tensor(row[:], row[:], fits[:], ALU.mult))
                    line(dve.tensor_tensor(scatter_at[k][:], row[:], back[:], ALU.add))
                    line(dve.tensor_tensor(row[:], row[:], back[:], ALU.add))
                    line(dve.tensor_scalar(row[:], row[:], float(E * CAP), None, ALU.min))
                    line(dve.tensor_copy(gather_at[k][:], row[:]))
                dve.wait_ge(ratio_ready, 1)
                line(dve.tensor_scalar(one[:], ratio[:], 1.0, None, ALU.add))
                line(dve.reciprocal(weight[0][:], one[:]))
                line(dve.tensor_tensor(weight[1][:], ratio[:], weight[0][:], ALU.mult))


def indirect(c, jobs):
    nc = c.nc
    moved = c.sem("moved")
    with nc.Block() as block:
        @block.gpsimd
        def _(pool):
            for scatter, a, rows, b in jobs:
                at = bass.IndirectOffsetOnAxis(ap=rows, axis=0)
                pool.indirect_dma_start(out=a, out_offset=at if scatter else None, in_=b,
                                        in_offset=None if scatter else at).then_inc(moved, 16)
            pool.wait_ge(moved, 16 * len(jobs))


def expert_weights(eng, buffers, weights, e, par, loaded):
    for dst, w in zip(buffers, weights):
        eng.dma_start(dst[par][:, :, :], w[bass.ds(e, 1), :, :].rearrange("o (k p) n -> p (o k) n", p=P))\
            .then_inc(loaded[par], 16)


def experts(c, slots_in, buffers, weights, loaded, slots_out):
    nc = c.nc
    full = CAP // P
    part = CAP - full * P
    sizes = [min(P, CAP - i * P) for i in range(ST)]
    with ExitStack() as s:
        w1_sb, w2_sb, w3_sb = buffers
        rows = [c.sb(s, "rows", [P, ST, D]) for _ in range(2)]
        rowsT = [c.sb(s, "rowsT", [P, DT, CAP]) for _ in range(2)]
        tanh = [c.sb(s, "tanh", [P, CAP]) for _ in range(2)]
        gate = [c.sb(s, "gate", [P, CAP]) for _ in range(2)]
        hidden = [c.sb(s, "hidden", [P, MH, CAP]) for _ in range(2)]
        out_sb = [c.sb(s, "out", [P, ST, D]) for _ in range(2)]
        turn_ps = [c.ps(s, "turn", [P, BANK]) for _ in range(2)]
        a_ps = [c.ps(s, "a", [P, BANK]) for _ in range(2)]
        b_ps = [c.ps(s, "b", [P, BANK]) for _ in range(2)]
        out_ps = [c.ps(s, "outp", [P, BANK]) for _ in range(2)]
        stored = [c.sem("stored0"), c.sem("stored1")]
        turned, placed, multiplied, tanhed, gated, joined, summed, copied = (
            c.sem(n) for n in ("turned", "placed", "multiplied", "tanhed", "gated", "joined", "summed", "copied"))
        LOADS = 3 + 1 + (part > 0)

        def pairs(eng, step):
            for par in range(2):
                step(0, par)
            with eng.Fori(1, E // 2 - 1) as g:
                for par in range(2):
                    step(g, par)
            for par in range(2):
                step(E // 2 - 1, par)

        with nc.Block() as block:
            @block.sync
            def _(sp):
                def loads(g, par):
                    e = g * 2 + par
                    wait(sp, summed, (e - 1) * ST)
                    sp.dma_start(rows[par][:, 0:full, :],
                                 slots_in[bass.ds(e * CAP, full * P), :].rearrange("(t p) d -> p t d", p=P))\
                        .then_inc(loaded[par], 16)
                    if part:
                        sp.dma_start(rows[par][0:part, full, :],
                                     slots_in[bass.ds(e * CAP + full * P, part), :]).then_inc(loaded[par], 16)
                    if not isinstance(g, int) or g > 0:
                        expert_weights(sp, buffers, weights, e, par, loaded)

                pairs(sp, loads)

            @block.gpsimd
            def _(pool):
                def store(g, par):
                    e = g * 2 + par
                    pool.wait_ge(copied, (e + 1) * ST)
                    pool.dma_start(slots_out[bass.ds(e * CAP, full * P), :].rearrange("(t p) d -> p t d", p=P),
                                   out_sb[par][:, 0:full, :]).then_inc(stored[par], 16)
                    if part:
                        pool.dma_start(slots_out[bass.ds(e * CAP + full * P, part), :],
                                       out_sb[par][0:part, full, :]).then_inc(stored[par], 16)

                pairs(pool, store)
                for par in range(2):
                    pool.wait_ge(stored[par], 16 * (E // 2) * (1 + (part > 0)))

            @block.tensor
            def _(pe):
                def turn(g, par):
                    e = g * 2 + par
                    pe.wait_ge(loaded[par], (g + 1) * (16 * LOADS))
                    for h in range(DT):
                        wait(pe, placed, e * DT + (h - 1))
                        for i, n in enumerate(sizes):
                            last = pe.transpose(turn_ps[h % 2][:, i * P:i * P + n], rows[par][0:n, i, h * P:(h + 1) * P],
                                                c.identf[0:n, 0:n])
                        last.then_inc(turned, 1)

                def widen(g, par):
                    e = g * 2 + par
                    pe.wait_ge(placed, (e + 1) * DT)
                    for m in range(MH):
                        wait(pe, joined, e * MH + (m - 1))
                        for ps, w in ((a_ps, w1_sb), (b_ps, w2_sb)):
                            for k in range(DT):
                                last = pe.matmul(ps[m % 2][:, 0:CAP], w[par][:, k, m * P:(m + 1) * P],
                                                 rowsT[par][:, k, :], start=(k == 0), stop=(k == DT - 1))
                        last.then_inc(multiplied, 1)

                def narrow(g, par):
                    e = g * 2 + par
                    pe.wait_ge(joined, (e + 1) * MH)
                    for i, n in enumerate(sizes):
                        wait(pe, copied, e * ST + (i - 1))
                        for m in range(MH):
                            last = pe.matmul(out_ps[(par * ST + i) % 2][0:n, 0:D], hidden[par][:, m, i * P:i * P + n],
                                             w3_sb[par][:, m, :], start=(m == 0), stop=(m == MH - 1))
                        last.then_inc(summed, 1)

                def step(g, par):
                    widen(g, par)
                    if not (isinstance(g, int) and g * 2 + par == E - 1):
                        turn(g + par, 1 - par)
                    narrow(g, par)

                turn(0, 0)
                pairs(pe, step)

            @block.scalar
            def _(act):
                def step(g, par):
                    e = g * 2 + par
                    for m in range(MH):
                        act.wait_ge(multiplied, e * MH + (m + 1))
                        wait(act, gated, e * MH + (m - 1))
                        nc.scalar.activation(tanh[m % 2][:], a_ps[m % 2][:, 0:CAP], ACT.Tanh, scale=0.5)\
                            .then_inc(tanhed, 1)
                    for i, n in enumerate(sizes):
                        act.wait_ge(summed, e * ST + (i + 1))
                        if i == 0:
                            wait(act, stored[par], g * (16 * (1 + (part > 0))))
                        nc.scalar.activation(out_sb[par][0:n, i, :], out_ps[(par * ST + i) % 2][0:n, 0:D], ACT.Copy)\
                            .then_inc(copied, 1)

                pairs(act, step)

            @block.vector
            def _(dve):
                def place(g, par):
                    e = g * 2 + par
                    for h in range(DT):
                        dve.wait_ge(turned, e * DT + (h + 1))
                        dve.tensor_copy(rowsT[par][:, h, :], turn_ps[h % 2][:, 0:CAP]).then_inc(placed, 1)

                def step(g, par):
                    e = g * 2 + par
                    for m in range(MH):
                        dve.wait_ge(tanhed, e * MH + (m + 1))
                        wait(dve, joined, e * MH + (m - 1))
                        dve.scalar_tensor_tensor(gate[m % 2][:], tanh[m % 2][:], 1.0, a_ps[m % 2][:, 0:CAP],
                                                 ALU.add, ALU.mult).then_inc(gated, 1)
                        dve.wait_ge(gated, e * MH + (m + 1))
                        if m == 0:
                            wait(dve, summed, (e - 1) * ST)
                        dve.scalar_tensor_tensor(hidden[par][:, m, :], gate[m % 2][:], 0.5, b_ps[m % 2][:, 0:CAP],
                                                 ALU.mult, ALU.mult).then_inc(joined, 1)
                    if not (isinstance(g, int) and e == E - 1):
                        place(g + par, 1 - par)

                place(0, 0)
                pairs(dve, step)


def expert_layer(c, wg, bg, w1, w2, w3):
    nc = c.nc
    slots_in = c.dram("slots_in", [E * CAP + 2 * N, D])
    slots_out = c.dram("slots_out", [E * CAP + 1, D])
    with ExitStack() as s:
        scatter_at = [c.sb(s, "scatter_at", [P, T], U32) for _ in range(2)]
        gather_at = [c.sb(s, "gather_at", [P, T], U32) for _ in range(2)]
        weight = [c.sb(s, "weight", [P, T]) for _ in range(2)]
        buffers = [[c.sb(s, n, shape) for _ in range(2)]
                   for n, shape in (("w1", [P, DT, HID]), ("w2", [P, DT, HID]), ("w3", [P, MH, D]))]
        expert_loaded = [c.sem("expert_loaded0"), c.sem("expert_loaded1")]
        with ExitStack() as s1:
            h = c.sb(s1, "h", [P, T, D])
            hT = c.sb(s1, "hT", [P, DT, N])
            wg_sb, bg_sb = c.sb(s1, "wg", [P, DT, E]), c.sb(s1, "bg", [P, E])
            gates = c.sb(s1, "gates", [P, T, E])
            zeros = c.sb(s1, "zeros", [P, E * CAP // P, D])
            zero(c, zeros[:])
            loads = start_loads(c, [(wg_sb[:], wg.rearrange("(k p) n -> p k n", p=P)), (bg_sb[:], row_of(bg, E)),
                                    (slots_in[0:E * CAP, :].rearrange("(t p) d -> p t d", p=P), zeros[:]),
                                    (slots_out[E * CAP:E * CAP + 1, :], zeros[0:1, 0, :])])
            with nc.Block() as block:
                @block.sync
                def _(sp):
                    for e in range(2):
                        expert_weights(sp, buffers, (w1, w2, w3), e, e, expert_loaded)

            norm_and_turn(c, c.x, hT, h)
            finish_loads(c, loads)
            project_tokens(c, hT, wg_sb, bg_sb, E, T, N, gates)
            route(c, gates, scatter_at, gather_at, weight)
            indirect(c, [(True, slots_in, scatter_at[k][:, t:t + 1], h[:, t, :]) for t in range(T) for k in range(2)])
        experts(c, slots_in, buffers, (w1, w2, w3), expert_loaded, slots_out)
        with ExitStack() as s1:
            y = [c.sb(s1, "y", [P, T, D]) for _ in range(2)]
            gathered, added = [c.sem("gathered0"), c.sem("gathered1")], c.sem("added")
            with nc.Block() as block:
                @block.gpsimd
                def _(pool):
                    for k in range(2):
                        for t in range(T):
                            at = bass.IndirectOffsetOnAxis(ap=gather_at[k][:, t:t + 1], axis=0)
                            pool.indirect_dma_start(out=y[k][:, t, :], out_offset=None, in_=slots_out,
                                                    in_offset=at).then_inc(gathered[k], 16)

                @block.vector
                def _(dve):
                    for k in range(2):
                        dve.wait_ge(gathered[k], 16 * T)
                        for t in range(T):
                            if k:
                                dve.wait_ge(added, t + 1)
                            dve.scalar_tensor_tensor(c.x[:, t, :], y[k][:, t, :], weight[k][:, t:t + 1], c.x[:, t, :],
                                                     ALU.mult, ALU.add).then_inc(added, 1)


WIN = 2 * P
TURN = 4


def window_maxima(c, q_parts, k_parts, shift):
    nc = c.nc
    GT = N // WIN
    G = T // GT
    with ExitStack() as s:
        q_sb = [c.sb(s, "q_sb", [SR, N], BF16) for _ in range(TURN)]
        k_sb = [c.sb(s, "k_sb", [SR, N], BF16) for _ in range(TURN)]
        slots = [c.ps(s, "score", [P, GT, WIN]) for _ in range(2)]
        loaded = [c.sem(f"loaded{k}") for k in range(TURN)]
        scored, maxed = c.sem("scored"), c.sem("maxed")
        with nc.Block() as block:
            @block.sync
            def _(sp):
                def loads(head, par, products):
                    wait(sp, scored, products)
                    load_pairs(sp, q_sb[par], k_sb[par], q_parts, k_parts, head, loaded[par])

                for par in range(TURN):
                    loads(par, par, 0)
                with sp.Fori(0, H // TURN - 1) as g:
                    for par in range(TURN):
                        loads(g * TURN + (TURN + par), par, g * (TURN * G) + G * (par + 1))

            @block.tensor
            def _(pe):
                with pe.Fori(0, H // TURN) as g:
                    for par in range(TURN):
                        pe.wait_ge(loaded[par], (g + 1) * (16 * PAIR_LOADS))
                        for i in range(G):
                            n = par * G + i
                            pe.wait_ge(maxed, g * (TURN * G) + (n + 1))
                            for t in range(GT * i, GT * (i + 1)):
                                o = slots[n % 2][:, t - GT * i, :]
                                still = q_sb[par][:, t * P:(t + 1) * P]
                                if t:
                                    pe.matmul(o, still, k_sb[par][:, (t - 1) * P:(t + 1) * P], start=True, stop=False)
                                    last = pe.matmul(o, c.identb[:], c.mask_qk[:], start=False, stop=True)
                                else:
                                    pe.matmul(o, c.identb[:], c.mask_first[:], start=True, stop=False)
                                    last = pe.matmul(o[:, P:2 * P], still, k_sb[par][:, 0:P], start=False, stop=True)
                            last.then_inc(scored, 1)

            @block.vector
            def _(dve):
                dve.sem_inc(maxed, 2)
                with dve.Fori(0, H // TURN) as g:
                    for par in range(TURN):
                        for i in range(G):
                            n = par * G + i
                            dve.wait_ge(scored, g * (TURN * G) + (n + 1))
                            dve.tensor_reduce(shift[:, bass.ds(g * (TURN * T) + n * GT, GT)], slots[n % 2][:], X, ALU.max,
                                              negate=True).then_inc(maxed, 1)


def window_weights(c, q_parts, k_parts, shift_rows, values, out_rows):
    nc = c.nc
    KT = CH
    U, LAG, S = T // KT, 2, 2
    assert U == T // CH
    LOADS = PAIR_LOADS + 2
    with ExitStack() as s:
        q_sb = [c.sb(s, "q_sb", [SRM, N], BF16) for _ in range(TURN)]
        k_sb = [c.sb(s, "k_sb", [SRM, N], BF16) for _ in range(TURN)]
        v_sb = [c.sb(s, "v_sb", [P, T, 32]) for _ in range(TURN)]
        slots = [c.ps(s, "score", [P, KT, WIN]) for _ in range(S)]
        sums = [c.ps(s, "sums", [P, BANK]) for _ in range(2)]
        probs = [c.sb(s, "probs", [P, KT, WIN]) for _ in range(S)]
        stage = [c.sb(s, "stage", [P, BANK]) for _ in range(2)]
        loaded = [c.sem(f"loaded{k}") for k in range(TURN)]
        stored = [c.sem("stored0"), c.sem("stored1")]
        scored, exped, used, staged, ones_set = (c.sem(n) for n in ("scored", "exped", "used", "staged", "ones_set"))

        def turns(eng, turn):
            turn(0, False)
            with eng.Fori(1, H // TURN - 1) as g:
                turn(g, False)
            turn(H // TURN - 1, True)

        with nc.Block() as block:
            @block.sync
            def _(sp):
                def loads(head, par, products):
                    wait(sp, used, products)
                    load_pairs(sp, q_sb[par], k_sb[par], q_parts, k_parts, head, loaded[par])
                    sp.dma_start(q_sb[par][SR:SRM, None, :], shift_rows[:, bass.ds(head, 1), :]).then_inc(loaded[par], 16)
                    sp.dma_start(v_sb[par][:, None, :, :], values[:, bass.ds(head, 1), :, :]).then_inc(loaded[par], 16)

                for par in range(TURN):
                    loads(par, par, 0)
                with sp.Fori(0, H // TURN - 1) as g:
                    for par in range(TURN):
                        loads(g * TURN + (TURN + par), par, g * (TURN * U) + U * (par + 1))

            @block.gpsimd
            def _(pool):
                for par in range(TURN):
                    pool.memset(k_sb[par][SR:SRM, :], 1.0).then_inc(ones_set, 1)

                def turn(g, last):
                    for par in range(TURN):
                        pool.wait_ge(staged, g * TURN + (par + 1))
                        pool.dma_start(out_rows[bass.ds(g * TURN + par, 1), :, :].rearrange("o p q -> (o p) q"),
                                       stage[par % 2][:]).then_inc(stored[par % 2], 16)

                turns(pool, turn)
                for par in range(2):
                    pool.wait_ge(stored[par], 16 * (H // 2))

            @block.tensor
            def _(pe):
                def score(g, i):
                    par, u, slot = i // U % TURN, i % U, i % S
                    if u == 0:
                        pe.wait_ge(loaded[par], (g + (i // U // TURN + 1)) * (16 * LOADS))
                    wait(pe, exped, g * (TURN * U) + (i - S + 1))
                    for i_k, k in enumerate(range(u, T, U)):
                        w = min(WIN, N - k * P)
                        o = slots[slot][:, i_k, 0:w]
                        pe.matmul(o, k_sb[par][:, k * P:(k + 1) * P], q_sb[par][:, k * P:k * P + w],
                                  start=True, stop=False)
                        last = pe.matmul(o, c.identb[:], c.mask_kq[:, 0:w], start=False, stop=True)
                    last.then_inc(scored, 1)

                def add_up(g, i):
                    par, u, slot = i // U, i % U, i % S
                    pe.wait_ge(exped, g * (TURN * U) + (i + 1))
                    if u == 0:
                        wait(pe, staged, g * TURN + (par - 1))
                    for later in range(2):
                        for i_k, k in enumerate(range(u, T, U)):
                            t = k + later
                            if t == T:
                                continue
                            j, o = t // CH, t % CH * P
                            last = pe.matmul(sums[par % 2][32 * j:32 * j + 32, o:o + P], v_sb[par][:, k, :],
                                             probs[slot][:, i_k, later * P:(later + 1) * P],
                                             start=(u == 0 and later == 0), stop=(t == k), skip_group_check=True)
                    last.then_inc(used, 1)

                def turn(g, last):
                    for i in range(TURN * U):
                        if not last or i + LAG < TURN * U:
                            score(g, i + LAG)
                        add_up(g, i)

                pe.wait_ge(ones_set, TURN)
                for i in range(LAG):
                    score(0, i)
                turns(pe, turn)

            @block.scalar
            def _(act):
                def turn(g, last):
                    for i in range(TURN * U):
                        u, slot = i % U, i % S
                        act.wait_ge(scored, g * (TURN * U) + (i + 1))
                        wait(act, used, g * (TURN * U) + (i - S + 1))
                        end = KT * WIN - (P if u == U - 1 else 0)
                        flat = lambda a: a[:].rearrange("p k w -> p (k w)")[:, 0:end]
                        nc.scalar.activation(flat(probs[slot]), flat(slots[slot]), ACT.Exp).then_inc(exped, 1)

                turns(act, turn)

            @block.vector
            def _(dve):
                def turn(g, last):
                    for par in range(TURN):
                        dve.wait_ge(used, g * (TURN * U) + U * (par + 1))
                        wait(dve, stored[par % 2], g * (16 * TURN // 2) + 16 * (par // 2))
                        dve.tensor_copy(stage[par % 2][:], sums[par % 2][:]).then_inc(staged, 1)

                turns(dve, turn)


def head_norm(c, a, out, gamma, beta, fold):
    nc = c.nc
    HT = H * T
    with ExitStack() as s:
        mean, var, root = (c.sb(s, n, [P, HT]) for n in ("mean", "var", "root"))
        square = c.sb(s, "square", [P, T, D])
        chain, centred, squared, var_ready, root_ready = (c.sem(n) for n in ("chain", "centred", "squared", "var_ready", "root_ready"))
        by_head = lambda x: x[:, :, :].rearrange("p t (h e) -> p (t h) e", e=HD)
        over = lambda x: x[:, :, None].to_broadcast([P, HT, HD])
        with nc.Block() as block:
            @block.vector
            def _(dve):
                line = Line(dve, chain)
                line(dve.tensor_reduce(mean[:], by_head(a), X, ALU.add))
                line(dve.tensor_scalar(mean[:], mean[:], -1.0 / HD, None, ALU.mult))
                dve.tensor_tensor(by_head(a), by_head(a), over(mean), ALU.add).then_inc(centred, 1)
                line(dve.tensor_scalar(gamma[:], gamma[:], fold, None, ALU.mult))
                line(dve.tensor_scalar(beta[:], beta[:], fold, None, ALU.mult))
                dve.wait_ge(squared, 1)
                line(dve.tensor_reduce(var[:], by_head(square), X, ALU.add))
                dve.tensor_scalar(var[:], var[:], 1.0 / HD, None, ALU.mult).then_inc(var_ready, 1)
                dve.wait_ge(root_ready, 1)
                line(dve.reciprocal(root[:], root[:]))
                line(dve.tensor_tensor(out[:, :, :].rearrange("p t (e h) -> p t h e", e=HD),
                                       a[:, :, :].rearrange("p t (h e) -> p t h e", e=HD),
                                       root[:].rearrange("p (t h) -> p t h", h=H)[:, :, :, None]
                                       .to_broadcast([P, T, H, HD]), ALU.mult))

            @block.scalar
            def _(act):
                act.wait_ge(centred, 1)
                nc.scalar.activation(square[:], a[:, :, :], ACT.Square).then_inc(squared, 1)
                act.wait_ge(var_ready, 1)
                nc.scalar.activation(root[:], var[:], ACT.Sqrt, bias=c.eps[:, 0:1]).then_inc(root_ready, 1)


def window_layer(c, w_qkv, b_qkv, q_gamma, q_beta, k_gamma, k_beta, w_out, b_out):
    nc = c.nc
    q_parts = c.dram("w_q_parts", [PARTS * HD, H, N], BF16)
    k_parts = c.dram("w_k_parts", [PARTS * HD, H, N], BF16)
    shift_rows = c.dram("w_shift_rows", [PARTS, H, N], BF16)
    sums = c.dram("w_sums", [H, P, BANK])
    with ExitStack() as s:
        wo, bo = c.sb(s, "wo", [P, DT, D]), c.sb(s, "bo", [P, D])
        values = c.sb(s, "values", [P, H, T, 32])
        with ExitStack() as s1:
            w, b = c.sb(s1, "w", [P, DT, 3 * D]), c.sb(s1, "b", [P, 3 * D])
            affine = [c.sb(s1, "affine", [P, DT]) for _ in range(4)]
            scratch, fills = zip(*(scratch_by_element(c, v) for v in (q_gamma, q_beta, k_gamma, k_beta)))
            loads = start_loads(c, list(fills) +
                                [(w[:], w_qkv.rearrange("(k p) n -> p k n", p=P)), (b[:], row_of(b_qkv, 3 * D)),
                                 (wo[:], w_out.rearrange("(k p) n -> p k n", p=P)), (bo[:], row_of(b_out, D))])
            qk = [c.sb(s1, n, [P, T, D]) for n in ("q", "k")]
            with ExitStack() as s2:
                hT = c.sb(s2, "hT", [P, DT, N])
                v = c.sb(s2, "v", [P, T, D])
                norm_and_turn(c, c.x, hT, v)
                finish_loads(c, loads)
                loads = start_loads(c, [job for a, v_ in zip(affine, scratch) for job in by_feature(a, v_)])
                for i, dst in enumerate((*qk, v)):
                    project_tokens(c, hT, w[:, :, i * D:(i + 1) * D], b[:, i * D:(i + 1) * D], D, T, N, dst)
                values_with_ones(c, v, values, T)
            finish_loads(c, loads)
            for i, parts in enumerate((q_parts, k_parts)):
                with ExitStack() as s2:
                    gamma, beta = affine[2 * i:2 * i + 2]
                    normed = c.sb(s2, "normed", [P, T, D])
                    head_norm(c, qk[i], normed, gamma, beta, (HD ** -0.5, 1.0)[i])
                    turned = c.sb(s2, "turned", [P, DT, N])
                    transpose_tiles(c, normed, turned, scale=gamma, bias=beta)
                    split_to_dram(c, turned, N, parts, (Q_ORDER, K_ORDER)[i])
        shift = c.sb(s, "shift", [P, H * T])
        window_maxima(c, q_parts, k_parts, shift)
        split_rows(c, shift[:], [shift_rows[i] for i in range(PARTS)])
        window_weights(c, q_parts, k_parts, shift_rows, values, sums)
        attention_output(c, sums, wo, bo)


NE = 64
NP = 32
SL = NE * NP
SLT = SL // P
SPT = P // NP
LOW_CLIP, HIGH_CLIP = -33000.0, 65000.0


def bias_rows(c, v, rows):
    nc = c.nc
    parts = c.dram("bias_parts", [PARTS, SL], BF16)
    with ExitStack() as s:
        a = c.sb(s, "a", [SLT, P])
        part = c.sb(s, "part", [SLT, PARTS, P], BF16)
        rest = c.sb(s, "rest", [SLT, 2, P])
        loaded, chain, stored = c.sem("loaded"), c.sem("chain"), c.sem("stored")
        with nc.Block() as block:
            @block.sync
            def _(sp):
                sp.dma_start(a[:], v.rearrange("(t q) -> t q", q=P)).then_inc(loaded, 16)
                sp.wait_ge(chain, 5)
                sp.dma_start(parts.rearrange("a (t q) -> t a q", q=P), part[:]).then_inc(stored, 16)
                sp.wait_ge(stored, 16)
                sp.dma_start(rows[:], parts).then_inc(loaded, 16)
                sp.wait_ge(loaded, 32)

            @block.vector
            def _(dve):
                line = Line(dve, chain)
                dve.wait_ge(loaded, 16)
                line(dve.tensor_copy(part[:, 0, :], a[:]))
                line(dve.tensor_tensor(rest[:, 0, :], a[:], part[:, 0, :], ALU.subtract))
                line(dve.tensor_copy(part[:, 1, :], rest[:, 0, :]))
                line(dve.tensor_tensor(rest[:, 1, :], rest[:, 0, :], part[:, 1, :], ALU.subtract))
                line(dve.tensor_copy(part[:, 2, :], rest[:, 1, :]))


def logits(c, pe, out, hT, phiT, bias, t, first_col, cols):
    for o in range(0, cols, BANK):
        pe.matmul(out[:, o:o + BANK], c.onesb[0:PARTS, :], bias[:, first_col + o:first_col + o + BANK],
                  start=True, stop=False)
        for k in range(DT):
            last = pe.matmul(out[:, o:o + BANK], hT[:, k, t * P:(t + 1) * P],
                             phiT[:, k, first_col + o:first_col + o + BANK], start=False, stop=(k == DT - 1))
    return last


def dispatch(c, h, hT, phiT, bias, mixed, logit_rows):
    nc = c.nc
    W = SL // 2
    G = W // NP
    jobs = [(half, t) for half in range(2) for t in range(T)]
    ht = SLT // 2
    S, LAG = 4, 2
    K = 2
    with ExitStack() as s:
        lg = [c.ps(s, "logit", [P, W]) for _ in range(2)]
        acc = c.ps(s, "acc", [P, ht, D])
        e = [c.sb(s, "e", [P, W]) for _ in range(S)]
        top, total, inverse = ([c.sb(s, n, [P, G]) for _ in range(S)] for n in ("top", "total", "inverse"))
        kept = [c.sb(s, "kept", [P, W]) for _ in range(K)]
        copied, stored = c.sem("copied"), [c.sem(f"stored{k}") for k in range(K)]
        scored, topped, shifted, exped, summed, inverted, weighed, used, out = (
            c.sem(n) for n in ("scored", "topped", "shifted", "exped", "summed", "inverted", "weighed", "used", "out"))
        by = lambda a: a[:].rearrange("p (g e) -> p g e", e=NP)
        over = lambda a: a[:, :, None].to_broadcast([P, G, NP])
        with nc.Block() as block:
            @block.tensor
            def _(pe):
                def mix(i):
                    half, t = jobs[i]
                    pe.wait_ge(weighed, i + 1)
                    if t == 0 and half:
                        pe.wait_ge(out, 1)
                    for b in range(ht):
                        last = pe.matmul(acc[:, b, :], e[i % S][:, b * P:(b + 1) * P], h[:, t, :],
                                         start=(t == 0 and b % 2 == 0), stop=(t == T - 1), skip_group_check=True)
                    last.then_inc(used, 1)

                for i, (half, t) in enumerate(jobs):
                    wait(pe, copied, i - 1)
                    logits(c, pe, lg[i % 2], hT, phiT, bias, t, half * W, W).then_inc(scored, 1)
                    if i >= LAG:
                        mix(i - LAG)
                for i in range(len(jobs) - LAG, len(jobs)):
                    mix(i)

            @block.vector
            def _(dve):
                def shift(i):
                    b = i % S
                    dve.wait_ge(copied, i + 1)
                    dve.tensor_reduce(top[b][:], by(kept[i % K]), X, ALU.max).then_inc(topped, 1)
                    dve.wait_ge(topped, i + 1)
                    wait(dve, used, i - S + 1)
                    dve.tensor_tensor(by(e[b]), by(kept[i % K]), over(top[b]), ALU.subtract).then_inc(shifted, 1)

                def total_of(i):
                    b = i % S
                    dve.wait_ge(exped, i + 1)
                    dve.tensor_reduce(total[b][:], by(e[b]), X, ALU.add).then_inc(summed, 1)
                    dve.wait_ge(summed, i + 1)
                    dve.reciprocal(inverse[b][:], total[b][:]).then_inc(inverted, 1)

                def clip(half):
                    dve.wait_ge(used, (half + 1) * T)
                    dve.tensor_scalar(mixed[:, half * ht:(half + 1) * ht, :], acc[:], LOW_CLIP, HIGH_CLIP,
                                      ALU.max, ALU.min).then_inc(out, 1)

                for i in range(len(jobs)):
                    if i == T + LAG:
                        clip(0)
                    shift(i)
                    if i:
                        total_of(i - 1)
                total_of(len(jobs) - 1)
                clip(1)

            @block.scalar
            def _(act):
                for i in range(len(jobs)):
                    act.wait_ge(scored, i + 1)
                    wait(act, shifted, i - K + 1)
                    wait(act, stored[i % K], i // K * 16)
                    nc.scalar.activation(kept[i % K][:], lg[i % 2][:], ACT.Copy).then_inc(copied, 1)
                    act.wait_ge(shifted, i + 1)
                    nc.scalar.activation(e[i % S][:], e[i % S][:], ACT.Exp).then_inc(exped, 1)

            @block.sync
            def _(sp):
                for i, (half, t) in enumerate(jobs):
                    sp.wait_ge(copied, i + 1)
                    sp.dma_start(logit_rows[t * P:(t + 1) * P, half * W:(half + 1) * W], kept[i % K][:])\
                        .then_inc(stored[i % K], 16)
                for k in range(K):
                    sp.wait_ge(stored[k], 16 * len(jobs[k::K]))

            @block.gpsimd
            def _(pool):
                for i in range(len(jobs)):
                    pool.wait_ge(inverted, i + 1)
                    pool.tensor_tensor(by(e[i % S]), by(e[i % S]), over(inverse[i % S]), ALU.mult).then_inc(weighed, 1)


def soft_expert_weights(sp, w_sb, w, i, loaded):
    b = i % len(w_sb)
    sp.dma_start(w_sb[b][:], w[i * SPT:(i + 1) * SPT].rearrange("e (k p) n -> p (e k) n", p=P)).then_inc(loaded[b], 16)


def soft_experts(c, slotsT, w, bias, results, w_sb, loaded):
    nc = c.nc
    B = len(w_sb)
    with ExitStack() as s:
        pick = c.sb(s, "pick", [SPT, P])
        slots = [c.ps(s, "out", [P, D]) for _ in range(4)]
        ones_set, picked, multiplied, copied = (c.sem(n) for n in ("ones_set", "picked", "multiplied", "copied"))
        with nc.Block() as block:
            @block.sync
            def _(sp):
                for i in range(B, SLT):
                    sp.wait_ge(multiplied, i - B + 1)
                    soft_expert_weights(sp, w_sb, w, i, loaded)

            @block.gpsimd
            def _(pool):
                pool.memset(pick[:], 1.0).then_inc(ones_set, 1)
                pool.wait_ge(ones_set, 1)
                pool.affine_select(out=pick[:], in_=pick[:], compare_op=ALU.is_ge, fill=0.0, base=0,
                                   pattern=[[1, P]], channel_multiplier=-NP).then_inc(picked, 1)
                pool.wait_ge(picked, 1)
                pool.affine_select(out=pick[:], in_=pick[:], compare_op=ALU.is_gt, fill=0.0, base=NP,
                                   pattern=[[-1, P]], channel_multiplier=NP).then_inc(picked, 1)

            @block.tensor
            def _(pe):
                pe.wait_ge(picked, 2)
                for i in range(SLT):
                    wait(pe, copied, i - 3)
                    pe.wait_ge(loaded[i % B], (i // B + 1) * 16)
                    pe.matmul(slots[i % 4][:], pick[:], bias[:, i, :], start=True, stop=False, skip_group_check=True)
                    for k in range(DT):
                        for j in range(SPT):
                            a = i * P + j * NP
                            last = pe.matmul(slots[i % 4][j * NP:(j + 1) * NP, :], slotsT[:, k, a:a + NP],
                                             w_sb[i % B][:, j * DT + k, :], start=False, stop=(k == DT - 1),
                                             skip_group_check=True)
                    last.then_inc(multiplied, 1)

            @block.vector
            def _(dve):
                for i in range(SLT):
                    dve.wait_ge(multiplied, i + 1)
                    dve.tensor_copy(results[:, i, :], slots[i % 4][:]).then_inc(copied, 1)


def combine(c, logit_rows, results):
    B, S, TS = 3, 3, 4
    nc = c.nc
    with ExitStack() as s:
        lg = [c.sb(s, "logit", [P, SL]) for _ in range(B)]
        turn = [c.ps(s, "turn", [P, BANK]) for _ in range(TS)]
        y = [c.ps(s, "y", [P, BANK]) for _ in range(2)]
        e = [c.sb(s, "e", [P, SL]) for _ in range(S)]
        eT = [c.sb(s, "eT", [P, SLT, P]) for _ in range(2)]
        top, total, inverse = ([c.sb(s, n, [P, NP]) for _ in range(S)] for n in ("top", "total", "inverse"))
        loaded = [c.sem(f"loaded{k}") for k in range(B)]
        topped, shifted, exped, summed, inverted, weighed, turned, copied, used, added = (
            c.sem(n) for n in ("topped", "shifted", "exped", "summed", "inverted", "weighed", "turned", "copied", "used",
                               "added"))
        by_number = lambda a: a[:].rearrange("p (n q) -> p q n", q=NP)
        by = lambda a: a[:].rearrange("p (n q) -> p n q", q=NP)
        over = lambda a: a[:, None, :].to_broadcast([P, NE, NP])
        TG = SLT // 4
        with nc.Block() as block:
            @block.sync
            def _(sp):
                for t in range(T):
                    wait(sp, shifted, t - B + 1)
                    sp.dma_start(lg[t % B][:], logit_rows[t * P:(t + 1) * P, :]).then_inc(loaded[t % B], 16)

            @block.tensor
            def _(pe):
                def turn_over(t):
                    pe.wait_ge(weighed, t + 1)
                    for g in range(TG):
                        n = t * TG + g
                        wait(pe, copied, n - TS + 1)
                        for b in range(4):
                            st = 4 * g + b
                            last = pe.transpose(turn[n % TS][:, b * P:(b + 1) * P], e[t % S][:, st * P:(st + 1) * P],
                                                c.identf[:])
                        last.then_inc(turned, 1)

                def sum_up(t):
                    pe.wait_ge(copied, (t + 1) * TG)
                    wait(pe, added, t - 1)
                    for st in range(SLT):
                        last = pe.matmul(y[t % 2][:, 0:D], eT[t % 2][:, st, :], results[:, st, :],
                                         start=(st == 0), stop=(st == SLT - 1))
                    last.then_inc(used, 1)

                for t in range(T):
                    turn_over(t)
                    if t:
                        sum_up(t - 1)
                sum_up(T - 1)

            @block.vector
            def _(dve):
                def shift(t):
                    dve.wait_ge(loaded[t % B], (t // B + 1) * 16)
                    dve.tensor_reduce(top[t % S][:], by_number(lg[t % B]), X, ALU.max).then_inc(topped, 1)
                    dve.wait_ge(topped, t + 1)
                    wait(dve, turned, (t - S + 1) * TG)
                    dve.tensor_tensor(by(e[t % S]), by(lg[t % B]), over(top[t % S]), ALU.subtract).then_inc(shifted, 1)

                def total_of(t):
                    dve.wait_ge(exped, t + 1)
                    dve.tensor_reduce(total[t % S][:], by_number(e[t % S]), X, ALU.add).then_inc(summed, 1)
                    dve.wait_ge(summed, t + 1)
                    dve.reciprocal(inverse[t % S][:], total[t % S][:]).then_inc(inverted, 1)

                def add(t):
                    dve.wait_ge(used, t + 1)
                    dve.tensor_tensor(c.x[:, t, :], y[t % 2][:, 0:D], c.x[:, t, :], ALU.add).then_inc(added, 1)

                for t in range(T):
                    shift(t)
                    if t > 2:
                        add(t - 3)
                    total_of(t)
                add(T - 3)
                add(T - 2)
                add(T - 1)

            @block.scalar
            def _(act):
                def copy(t):
                    wait(act, used, t - 1)
                    for g in range(TG):
                        act.wait_ge(turned, t * TG + g + 1)
                        out = eT[t % 2][:, 4 * g:4 * g + 4, :].rearrange("p a b -> p (a b)")
                        nc.scalar.activation(out, turn[(t * TG + g) % TS][:], ACT.Copy).then_inc(copied, 1)

                for t in range(T):
                    if t > 1:
                        copy(t - 2)
                    act.wait_ge(shifted, t + 1)
                    nc.scalar.activation(e[t % S][:], e[t % S][:], ACT.Exp).then_inc(exped, 1)
                copy(T - 2)
                copy(T - 1)

            @block.gpsimd
            def _(pool):
                for t in range(T):
                    pool.wait_ge(inverted, t + 1)
                    pool.tensor_tensor(by(e[t % S]), by(e[t % S]), over(inverse[t % S]), ALU.mult).then_inc(weighed, 1)


def soft_layer(c, phi_w, phi_b, expert_w, expert_b):
    nc = c.nc
    with ExitStack() as s:
        logit_rows = c.dram("logit_rows", [N, SL])
        expert_bias = c.sb(s, "expert_bias", [SPT, SLT, D])
        results = c.sb(s, "results", [P, SLT, D])
        with ExitStack() as s1:
            mixed = c.sb(s1, "mixed", [P, SLT, D])
            with ExitStack() as s2:
                hT = c.sb(s2, "hT", [P, DT, N])
                phiT = c.sb(s2, "phiT", [P, DT, SL])
                bias = c.sb(s2, "bias", [PARTS, SL], BF16)
                h, phi = c.sb(s2, "h", [P, T, D]), c.sb(s2, "phi", [P, SLT, D])
                loads = start_loads(c, [(phi[:], phi_w.rearrange("(t p) d -> p t d", p=P)),
                                        (expert_bias[:], expert_b.rearrange("(t j) d -> j t d", j=SPT))])
                norm_and_turn(c, c.x, hT, h)
                bias_rows(c, phi_b, bias)
                finish_loads(c, loads)
                transpose_tiles(c, phi, phiT)
                dispatch(c, h, hT, phiT, bias, mixed, logit_rows)
            slotsT = c.sb(s1, "slotsT", [P, DT, SL])
            w_sb = [c.sb(s1, "w", [P, SPT * DT, D]) for _ in range(6)]
            w_loaded = [c.sem("w_loaded") for _ in w_sb]
            with nc.Block() as block:
                @block.sync
                def _(sp):
                    for i in range(len(w_sb)):
                        soft_expert_weights(sp, w_sb, expert_w, i, w_loaded)

            norm_and_turn(c, mixed, slotsT, mixed, ACT.Tanh)
            soft_experts(c, slotsT, expert_w, expert_bias, results, w_sb, w_loaded)
        combine(c, logit_rows, results)


def store_x(c, out):
    nc = c.nc
    stored = c.sem("stored")
    with nc.Block() as block:
        @block.sync
        def _(sp):
            sp.dma_start(out.rearrange("b (t p) d -> p (b t) d", p=P), c.x[:]).then_inc(stored, 16)
            sp.wait_ge(stored, 16)


def decoder(nc, a, out):
    with ExitStack() as ctx:
        c = Core(nc, ctx)
        setup(c, a["x"])
        layer0_attention(c, *(a[f"L0_attn_{n}"] for n in ("w_attn", "b_attn", "w_proj", "b_proj")))
        c.recycle()
        cross_layer(c, "c0", a["ctx_1024"], [a[f"L0_xattn_W_{n}"] for n in "qkvo"],
                    [a[f"L0_xattn_b_{n}"] for n in "qkvo"], False)
        c.recycle()
        expert_layer(c, *(a[f"L0_ffn_{n}"] for n in ("Wg", "bg", "W1", "W2", "W3")))
        c.recycle()
        window_layer(c, *(a[f"L1_attn_{n}"] for n in ("W_qkv", "b_qkv", "q_gamma", "q_beta", "k_gamma", "k_beta",
                                                      "W_out", "b_out")))
        c.recycle()
        cross_layer(c, "c1", a["ctx_1024"], [a[f"L1_xattn_W{n}"] for n in "qkvo"],
                    [a[f"L1_xattn_b{n}"] for n in "qkvo"], True)
        c.recycle()
        soft_layer(c, *(a[f"L1_ffn_{n}"] for n in ("phi_w", "phi_b", "expert_w", "expert_b")))
        store_x(c, out)


def kernel(**inputs):
    import numpy as np
    import concourse.bacc as bacc
    from concourse.bass_utils import run_bass_kernel_spmd

    nc = bacc.Bacc("TRN2", target_bir_lowering=False, num_devices=1)
    arrays, args = {}, {}
    for name, value in inputs.items():
        value = np.ascontiguousarray(value)
        arrays[f"in_{name}"] = value
        args[name] = nc.dram_tensor(f"in_{name}", value.shape, mybir.dt.from_np(value.dtype), kind="ExternalInput").ap()
    out = nc.dram_tensor("out_x", (1, N, D), F32, kind="ExternalOutput").ap()
    decoder(nc, args, out)
    return run_bass_kernel_spmd(nc, [arrays], core_ids=[0]).results[0]["out_x"]
```
